# Optimizing a Trainium2 kernel written in Bass

```python
import numpy as np
import jax
import jax.numpy as jnp

def _softmax(x, axis=-1):
    return jax.nn.softmax(x, axis=axis)

def _gelu(x):
    return jax.nn.gelu(x, approximate=True)

def _silu(x):
    return jax.nn.silu(x)

def _sigmoid(x):
    return jax.nn.sigmoid(x)

def _layernorm(x, axis=-1, eps=1e-05):
    m = jnp.mean(x, axis=axis, keepdims=True)
    v = jnp.var(x, axis=axis, keepdims=True)
    return (x - m) / jnp.sqrt(v + eps)

def _scatter_add(tgt, idx, src, axis=0):
    return tgt.at[idx].add(src)

def _segment_sum(src, seg, n):
    return jax.ops.segment_sum(src, seg, n)
kernel_name = 'mk_rec_standalone_d1_rec_r8_24cf80'

def setup_inputs(seed: int=0):
    np.random.seed(seed)
    _w = jnp.asarray

    def _rec_inputs():
        import jax
        import jax.numpy as jnp
        _rk = jax.random.key(seed)
        r_target_item = jnp.stack([jax.random.randint(jax.random.fold_in(jax.random.fold_in(_rk, 1), 0), (256,), 78, 99953, jnp.int32), jax.random.randint(jax.random.fold_in(jax.random.fold_in(_rk, 1), 1), (256,), 72, 99964, jnp.int32)], axis=1)
        r_hist_item = jax.random.randint(jax.random.fold_in(_rk, 2), (256, 200, 2), 0, 12500, jnp.int32)
        r_neg_hist_item = jax.random.randint(jax.random.fold_in(_rk, 3), (256, 200, 2), 0, 12500, jnp.int32)
        r_hist_valid_lens = jax.random.randint(jax.random.fold_in(_rk, 4), (256,), 1, 201, jnp.int32)
        r_sparse_feature = jnp.stack([jax.random.randint(jax.random.fold_in(jax.random.fold_in(_rk, 5), 0), (256,), 142, 99955, jnp.int32), jax.random.randint(jax.random.fold_in(jax.random.fold_in(_rk, 5), 1), (256,), 22, 99986, jnp.int32), jax.random.randint(jax.random.fold_in(jax.random.fold_in(_rk, 5), 2), (256,), 6, 99994, jnp.int32), jax.random.randint(jax.random.fold_in(jax.random.fold_in(_rk, 5), 3), (256,), 4, 99971, jnp.int32), jax.random.randint(jax.random.fold_in(jax.random.fold_in(_rk, 5), 4), (256,), 61, 99907, jnp.int32), jax.random.randint(jax.random.fold_in(jax.random.fold_in(_rk, 5), 5), (256,), 74, 99911, jnp.int32), jax.random.randint(jax.random.fold_in(jax.random.fold_in(_rk, 5), 6), (256,), 28, 99927, jnp.int32), jax.random.randint(jax.random.fold_in(jax.random.fold_in(_rk, 5), 7), (256,), 17, 99994, jnp.int32)], axis=1)
        return (r_target_item, r_hist_item, r_neg_hist_item, r_hist_valid_lens, r_sparse_feature)
    r_target_item, r_hist_item, r_neg_hist_item, r_hist_valid_lens, r_sparse_feature = _rec_inputs()

    def _L0_rec_setup():
        import jax, jax.numpy as jnp
        import numpy as np
        B, T, E, NF, SL, DL, VOCAB = (256, 200, 32, 2, 8, 16, 12500)
        D = E * NF
        ATT_IN = 4 * D
        BN_EPS = 1e-05

        def _gru_outputs(keys, lengths, wih, whh, bih, bhh):
            x = jnp.swapaxes(keys, 0, 1)
            gi = jnp.einsum('tbd,gd->tbg', x, wih) + bih
            valid = (jnp.arange(T)[:, None] < lengths[None, :])[:, :, None]
            h0 = jnp.zeros((keys.shape[0], D), keys.dtype)

            def step(h, inp):
                g, v = inp
                gh = h @ whh.T + bhh
                i_r, i_z, i_n = jnp.split(g, 3, axis=-1)
                h_r, h_z, h_n = jnp.split(gh, 3, axis=-1)
                r = jax.nn.sigmoid(i_r + h_r)
                z = jax.nn.sigmoid(i_z + h_z)
                n = jnp.tanh(i_n + r * h_n)
                h_new = (1.0 - z) * n + z * h
                h = jnp.where(v, h_new, h)
                return (h, jnp.where(v, h, 0.0))
            _, outs = jax.lax.scan(step, h0, (gi, valid))
            return jnp.swapaxes(outs, 0, 1)

        def _augru_last(keys, att, lengths, wih, whh, bih, bhh):
            x = jnp.swapaxes(keys, 0, 1)
            gi = jnp.einsum('tbd,gd->tbg', x, wih) + bih
            a = jnp.swapaxes(att, 0, 1)[:, :, None]
            valid = (jnp.arange(T)[:, None] < lengths[None, :])[:, :, None]
            h0 = jnp.zeros((keys.shape[0], D), keys.dtype)

            def step(h, inp):
                g, av, v = inp
                gh = h @ whh.T + bhh
                i_r, i_z, i_n = jnp.split(g, 3, axis=-1)
                h_r, h_z, h_n = jnp.split(gh, 3, axis=-1)
                r = jax.nn.sigmoid(i_r + h_r)
                z = av * jax.nn.sigmoid(i_z + h_z)
                n = jnp.tanh(i_n + r * h_n)
                h_new = (1.0 - z) * h + z * n
                return (jnp.where(v, h_new, h), None)
            h_last, _ = jax.lax.scan(step, h0, (gi, a, valid))
            return h_last

        def _attention_scores(query, keys, lengths, w1, b1, w2, b2, w3, b3):
            q = jnp.broadcast_to(query[:, None, :], keys.shape)
            ai = jnp.concatenate([q, keys, q - keys, q * keys], axis=-1)
            h = jax.nn.relu(ai @ w1 + b1)
            h = jax.nn.relu(h @ w2 + b2)
            s = (h @ w3 + b3)[..., 0]
            m = jnp.arange(T)[None, :] < lengths[:, None]
            s = jnp.where(m, s, -1000000000.0)
            return jax.nn.softmax(s, axis=-1)

        def _dien_forward(target_item, hist_item, neg_hist_item, hist_valid_lens, dense_feature, sparse_feature, emb, gru_wih, gru_whh, gru_bih, gru_bhh, augru_wih, augru_whh, augru_bih, augru_bhh, att_w1, att_b1, att_w2, att_b2, att_w3, att_b3, bn_gamma, bn_beta, dnn_w1, dnn_b1, dnn_w2, dnn_b2, out_w, out_b):
            target_emb = emb[target_item].reshape(B, NF * E)
            hist_emb = emb[hist_item].reshape(B, T, NF * E)
            sparse_emb = emb[sparse_feature].reshape(B, SL * E)
            interests = _gru_outputs(hist_emb, hist_valid_lens, gru_wih, gru_whh, gru_bih, gru_bhh)
            att = _attention_scores(target_emb, interests, hist_valid_lens, att_w1, att_b1, att_w2, att_b2, att_w3, att_b3)
            hist = _augru_last(interests, att, hist_valid_lens, augru_wih, augru_whh, augru_bih, augru_bhh)
            dnn_in = jnp.concatenate([sparse_emb, dense_feature, hist], axis=-1)
            mu = jnp.mean(dnn_in, axis=0)
            var = jnp.var(dnn_in, axis=0)
            x = (dnn_in - mu) * jax.lax.rsqrt(var + BN_EPS) * bn_gamma + bn_beta
            x = jax.nn.relu(x @ dnn_w1 + dnn_b1)
            x = jax.nn.relu(x @ dnn_w2 + dnn_b2)
            return x @ out_w + out_b
        key = jax.random.key(seed)
        ks = jax.random.split(key, 32)
        f32 = jnp.float32

        def rn(k, shape, std):
            return (jax.random.normal(k, shape) * std).astype(f32)
        return {'target_item': jax.random.randint(ks[0], (B, NF), 0, VOCAB), 'hist_item': jax.random.randint(ks[1], (B, T, NF), 0, VOCAB), 'neg_hist_item': jax.random.randint(ks[2], (B, T, NF), 0, VOCAB), 'hist_valid_lens': jnp.maximum(jax.random.randint(ks[3], (B,), 0, T + 1), 1), 'dense_feature': jax.random.normal(ks[4], (B, DL), f32), 'sparse_feature': jax.random.randint(ks[5], (B, SL), 0, VOCAB), 'emb': rn(ks[6], (VOCAB, E), 0.01), 'gru_wih': rn(ks[7], (3 * D, D), 0.001), 'gru_whh': rn(ks[8], (3 * D, D), 0.001), 'gru_bih': jnp.zeros((3 * D,), f32), 'gru_bhh': jnp.zeros((3 * D,), f32), 'augru_wih': rn(ks[9], (3 * D, D), 0.001), 'augru_whh': rn(ks[10], (3 * D, D), 0.001), 'augru_bih': jnp.zeros((3 * D,), f32), 'augru_bhh': jnp.zeros((3 * D,), f32), 'att_w1': rn(ks[11], (ATT_IN, 64), 0.05), 'att_b1': jnp.zeros((64,), f32), 'att_w2': rn(ks[12], (64, 16), 0.05), 'att_b2': jnp.zeros((16,), f32), 'att_w3': rn(ks[13], (16, 1), 0.05), 'att_b3': jnp.zeros((1,), f32), 'bn_gamma': jnp.ones((E * SL + DL + D,), f32), 'bn_beta': jnp.zeros((E * SL + DL + D,), f32), 'dnn_w1': rn(ks[14], (E * SL + DL + D, 256), 0.05), 'dnn_b1': jnp.zeros((256,), f32), 'dnn_w2': rn(ks[15], (256, 128), 0.05), 'dnn_b2': jnp.zeros((128,), f32), 'out_w': rn(ks[16], (128, 1), 0.05), 'out_b': jnp.zeros((1,), f32)}
    _L0_rec_all = _L0_rec_setup()
    _L0_rec_in = {k: v for k, v in _L0_rec_all.items() if k in ('dense_feature', 'emb', 'gru_wih', 'gru_whh', 'gru_bih', 'gru_bhh', 'augru_wih', 'augru_whh', 'augru_bih', 'augru_bhh', 'att_w1', 'att_b1', 'att_w2', 'att_b2', 'att_w3', 'att_b3', 'bn_gamma', 'bn_beta', 'dnn_w1', 'dnn_b1', 'dnn_w2', 'dnn_b2', 'out_w', 'out_b')}
    del _L0_rec_all
    return {'r_target_item': r_target_item, 'r_hist_item': r_hist_item, 'r_neg_hist_item': r_neg_hist_item, 'r_hist_valid_lens': r_hist_valid_lens, 'r_sparse_feature': r_sparse_feature, 'L0_rec_dense_feature': _L0_rec_in['dense_feature'], 'L0_rec_emb': _L0_rec_in['emb'], 'L0_rec_gru_wih': _L0_rec_in['gru_wih'], 'L0_rec_gru_whh': _L0_rec_in['gru_whh'], 'L0_rec_gru_bih': _L0_rec_in['gru_bih'], 'L0_rec_gru_bhh': _L0_rec_in['gru_bhh'], 'L0_rec_augru_wih': _L0_rec_in['augru_wih'], 'L0_rec_augru_whh': _L0_rec_in['augru_whh'], 'L0_rec_augru_bih': _L0_rec_in['augru_bih'], 'L0_rec_augru_bhh': _L0_rec_in['augru_bhh'], 'L0_rec_att_w1': _L0_rec_in['att_w1'], 'L0_rec_att_b1': _L0_rec_in['att_b1'], 'L0_rec_att_w2': _L0_rec_in['att_w2'], 'L0_rec_att_b2': _L0_rec_in['att_b2'], 'L0_rec_att_w3': _L0_rec_in['att_w3'], 'L0_rec_att_b3': _L0_rec_in['att_b3'], 'L0_rec_bn_gamma': _L0_rec_in['bn_gamma'], 'L0_rec_bn_beta': _L0_rec_in['bn_beta'], 'L0_rec_dnn_w1': _L0_rec_in['dnn_w1'], 'L0_rec_dnn_b1': _L0_rec_in['dnn_b1'], 'L0_rec_dnn_w2': _L0_rec_in['dnn_w2'], 'L0_rec_dnn_b2': _L0_rec_in['dnn_b2'], 'L0_rec_out_w': _L0_rec_in['out_w'], 'L0_rec_out_b': _L0_rec_in['out_b']}

def reference(r_target_item, r_hist_item, r_neg_hist_item, r_hist_valid_lens, r_sparse_feature, L0_rec_dense_feature, L0_rec_emb, L0_rec_gru_wih, L0_rec_gru_whh, L0_rec_gru_bih, L0_rec_gru_bhh, L0_rec_augru_wih, L0_rec_augru_whh, L0_rec_augru_bih, L0_rec_augru_bhh, L0_rec_att_w1, L0_rec_att_b1, L0_rec_att_w2, L0_rec_att_b2, L0_rec_att_w3, L0_rec_att_b3, L0_rec_bn_gamma, L0_rec_bn_beta, L0_rec_dnn_w1, L0_rec_dnn_b1, L0_rec_dnn_w2, L0_rec_dnn_b2, L0_rec_out_w, L0_rec_out_b):
    import jax
    import jax.numpy as jnp

    def _L0_rec_ref(target_item, hist_item, neg_hist_item, hist_valid_lens, dense_feature, sparse_feature, emb, gru_wih, gru_whh, gru_bih, gru_bhh, augru_wih, augru_whh, augru_bih, augru_bhh, att_w1, att_b1, att_w2, att_b2, att_w3, att_b3, bn_gamma, bn_beta, dnn_w1, dnn_b1, dnn_w2, dnn_b2, out_w, out_b):
        import jax, jax.numpy as jnp
        import numpy as np
        B, T, E, NF, SL, DL, VOCAB = (256, 200, 32, 2, 8, 16, 12500)
        D = E * NF
        ATT_IN = 4 * D
        BN_EPS = 1e-05

        def _gru_outputs(keys, lengths, wih, whh, bih, bhh):
            x = jnp.swapaxes(keys, 0, 1)
            gi = jnp.einsum('tbd,gd->tbg', x, wih) + bih
            valid = (jnp.arange(T)[:, None] < lengths[None, :])[:, :, None]
            h0 = jnp.zeros((keys.shape[0], D), keys.dtype)

            def step(h, inp):
                g, v = inp
                gh = h @ whh.T + bhh
                i_r, i_z, i_n = jnp.split(g, 3, axis=-1)
                h_r, h_z, h_n = jnp.split(gh, 3, axis=-1)
                r = jax.nn.sigmoid(i_r + h_r)
                z = jax.nn.sigmoid(i_z + h_z)
                n = jnp.tanh(i_n + r * h_n)
                h_new = (1.0 - z) * n + z * h
                h = jnp.where(v, h_new, h)
                return (h, jnp.where(v, h, 0.0))
            _, outs = jax.lax.scan(step, h0, (gi, valid))
            return jnp.swapaxes(outs, 0, 1)

        def _augru_last(keys, att, lengths, wih, whh, bih, bhh):
            x = jnp.swapaxes(keys, 0, 1)
            gi = jnp.einsum('tbd,gd->tbg', x, wih) + bih
            a = jnp.swapaxes(att, 0, 1)[:, :, None]
            valid = (jnp.arange(T)[:, None] < lengths[None, :])[:, :, None]
            h0 = jnp.zeros((keys.shape[0], D), keys.dtype)

            def step(h, inp):
                g, av, v = inp
                gh = h @ whh.T + bhh
                i_r, i_z, i_n = jnp.split(g, 3, axis=-1)
                h_r, h_z, h_n = jnp.split(gh, 3, axis=-1)
                r = jax.nn.sigmoid(i_r + h_r)
                z = av * jax.nn.sigmoid(i_z + h_z)
                n = jnp.tanh(i_n + r * h_n)
                h_new = (1.0 - z) * h + z * n
                return (jnp.where(v, h_new, h), None)
            h_last, _ = jax.lax.scan(step, h0, (gi, a, valid))
            return h_last

        def _attention_scores(query, keys, lengths, w1, b1, w2, b2, w3, b3):
            q = jnp.broadcast_to(query[:, None, :], keys.shape)
            ai = jnp.concatenate([q, keys, q - keys, q * keys], axis=-1)
            h = jax.nn.relu(ai @ w1 + b1)
            h = jax.nn.relu(h @ w2 + b2)
            s = (h @ w3 + b3)[..., 0]
            m = jnp.arange(T)[None, :] < lengths[:, None]
            s = jnp.where(m, s, -1000000000.0)
            return jax.nn.softmax(s, axis=-1)

        def _dien_forward(target_item, hist_item, neg_hist_item, hist_valid_lens, dense_feature, sparse_feature, emb, gru_wih, gru_whh, gru_bih, gru_bhh, augru_wih, augru_whh, augru_bih, augru_bhh, att_w1, att_b1, att_w2, att_b2, att_w3, att_b3, bn_gamma, bn_beta, dnn_w1, dnn_b1, dnn_w2, dnn_b2, out_w, out_b):
            target_emb = emb[target_item].reshape(B, NF * E)
            hist_emb = emb[hist_item].reshape(B, T, NF * E)
            sparse_emb = emb[sparse_feature].reshape(B, SL * E)
            interests = _gru_outputs(hist_emb, hist_valid_lens, gru_wih, gru_whh, gru_bih, gru_bhh)
            att = _attention_scores(target_emb, interests, hist_valid_lens, att_w1, att_b1, att_w2, att_b2, att_w3, att_b3)
            hist = _augru_last(interests, att, hist_valid_lens, augru_wih, augru_whh, augru_bih, augru_bhh)
            dnn_in = jnp.concatenate([sparse_emb, dense_feature, hist], axis=-1)
            mu = jnp.mean(dnn_in, axis=0)
            var = jnp.var(dnn_in, axis=0)
            x = (dnn_in - mu) * jax.lax.rsqrt(var + BN_EPS) * bn_gamma + bn_beta
            x = jax.nn.relu(x @ dnn_w1 + dnn_b1)
            x = jax.nn.relu(x @ dnn_w2 + dnn_b2)
            return x @ out_w + out_b
        return _dien_forward(target_item, hist_item, neg_hist_item, hist_valid_lens, dense_feature, sparse_feature, emb, gru_wih, gru_whh, gru_bih, gru_bhh, augru_wih, augru_whh, augru_bih, augru_bhh, att_w1, att_b1, att_w2, att_b2, att_w3, att_b3, bn_gamma, bn_beta, dnn_w1, dnn_b1, dnn_w2, dnn_b2, out_w, out_b)
    y = _L0_rec_ref(r_target_item, r_hist_item, r_neg_hist_item, r_hist_valid_lens, L0_rec_dense_feature, r_sparse_feature, L0_rec_emb, L0_rec_gru_wih, L0_rec_gru_whh, L0_rec_gru_bih, L0_rec_gru_bhh, L0_rec_augru_wih, L0_rec_augru_whh, L0_rec_augru_bih, L0_rec_augru_bhh, L0_rec_att_w1, L0_rec_att_b1, L0_rec_att_w2, L0_rec_att_b2, L0_rec_att_w3, L0_rec_att_b3, L0_rec_bn_gamma, L0_rec_bn_beta, L0_rec_dnn_w1, L0_rec_dnn_b1, L0_rec_dnn_w2, L0_rec_dnn_b2, L0_rec_out_w, L0_rec_out_b)
    return y

_drawn_inputs = setup_inputs


def setup_inputs(seed=0):
    import zlib

    import numpy as np

    out = dict(_drawn_inputs(seed))
    spreads = {'L0_rec_gru_bih': (0.0, 0.8),
     'L0_rec_gru_bhh': (0.0, 0.8),
     'L0_rec_augru_bih': (0.0, 0.1),
     'L0_rec_augru_bhh': (0.0, 0.1),
     'L0_rec_att_b1': (0.0, 2.0),
     'L0_rec_att_b2': (0.0, 2.0),
     'L0_rec_bn_gamma': (1.0, 0.2),
     'L0_rec_bn_beta': (0.0, 0.1),
     'L0_rec_dnn_b1': (0.0, 0.1),
     'L0_rec_dnn_b2': (0.0, 0.1)}
    factors = {'L0_rec_gru_wih': 200.0,
     'L0_rec_gru_whh': 64.0,
     'L0_rec_augru_wih': 8.0,
     'L0_rec_augru_whh': 56.605,
     'L0_rec_att_w1': 8.0,
     'L0_rec_att_w2': 8.0,
     'L0_rec_att_w3': 31.872}
    for name, (base, spread) in spreads.items():
        noise = np.random.default_rng([zlib.crc32(name.encode()), seed]).standard_normal(out[name].shape)
        drawn = base * np.exp(spread * noise) if base else spread * noise
        out[name] = jnp.asarray(drawn.astype(out[name].dtype))
    for name, factor in factors.items():
        out[name] = (out[name] * factor).astype(out[name].dtype)
    return out
```

```python
from contextlib import ExitStack

import concourse.bass as bass
from concourse import mybir

F32 = mybir.dt.float32
BF16 = mybir.dt.bfloat16
I32 = mybir.dt.int32
U32 = mybir.dt.uint32
ALU = mybir.AluOpType
ACT = mybir.ActivationFunctionType
AX = mybir.AxisListType

B, T, E, V = 256, 200, 32, 12500
D = 2 * E
HALF = D
P = 128
NSP = 8
ND = 16
HID1, HID2 = 256, 128
ATT1, ATT2 = 64, 16
BN_EPS = 1e-5
MASKED = 1e9
UN = 8
BODIES = T // UN
SLOTS = 2 * T + UN
MISC = 2 + NSP + 1
IDX = 2 * T
R_, Z_, N_ = 0, 1, 2
GRU, AUG = 0, 1


def build_dien(nc, lens_row, lens_col, ints, dense, emb, gate_w, gate_b, att_w1, att_b1, att_w2, att_b2,
               att_w3, att_b3, bn_par, w1, b1, w2, b2, out_w, out_b, out):
    ctx = ExitStack()
    with ctx:
        def sb(name, shape, dt=F32):
            return ctx.enter_context(nc.sbuf_tensor(name, shape, dt))

        def bank(name):
            return ctx.enter_context(nc.psum_tensor(name, [P, 512], F32))

        def sem(name):
            return ctx.enter_context(nc.semaphore(name))

        slot_x = sb("slot_x", [P, SLOTS, D])
        hist_a = sb("hist_a", [P, UN + 1 + T + 2, D])
        fetched = sb("fetched", [P, UN, D])
        slot_idx = sb("slot_idx", [P, 2 * T, 2], U32)
        stage_idx = sb("stage_idx", [P, UN, 2], U32)
        misc_idx = sb("misc_idx", [P, 2, 2 + NSP], U32)
        spare = [(UN + 1 + 3) * D]

        def early(shape, dt=F32, rows_=P):
            n = 1
            for k in shape:
                n *= k
            words = n if dt != BF16 else n // 2
            flat = hist_a[:, :, :].rearrange("p k d -> p (k d)")[0:rows_, spare[0]:spare[0] + words]
            spare[0] += words
            assert spare[0] <= (UN + 1 + T) * D
            flat = flat if dt == F32 else flat.bitcast(dt)
            return flat if len(shape) == 1 else flat.rearrange("p (a b) -> p a b", a=shape[0])

        raw = early([2, IDX + MISC + IDX], I32)
        rows = early([2, IDX + MISC + IDX])
        wrapped = early([2, IDX + MISC + IDX])
        srt = early([2, IDX + MISC])
        from_b = early([2 * T, 2])
        keep_a = early([T])
        perm = early([2, B])
        slot_no = sb("slot_no", [P, T])
        lrow_i = early([B], I32)
        lcol_i = sb("lcol_i", [P, 2], I32)
        key_row = early([B])
        key_col = sb("key_col", [P, 2])
        iota_b = early([B])
        iota_p = sb("iota_p", [P, 1])
        pos_rank = early([B])
        above = early([B])
        rank = sb("rank", [P, 2])
        perm_t = sb("perm_t", [P, 2, B])
        ends = sb("ends", [P, 2])
        ends_i = sb("ends_i", [1, 2], I32)
        ends_f = sb("ends_f", [1, 2])
        gate_open = sb("gate_open", [P, 1])
        ident = sb("ident", [P, P])
        ones_b = sb("ones_b", [P, P], BF16)
        gw = sb("gw", [P, 12, P])
        gb = early([12, P], rows_=3)
        gbs = early([8, P], rows_=3)
        gbr = early([8, P], rows_=3)
        gb1 = early([8, P], BF16, rows_=3)
        bias_w = sb("bias_w", [P, 8, P], BF16)
        aw1 = sb("aw1", [P, 4, P])
        wk = sb("wk", [P, P])
        wq = sb("wq", [P, P])
        ab1 = sb("ab1", [P, 1])
        aw2 = sb("aw2", [P, 4, P])
        ab2 = sb("ab2", [P, 1])
        aw3 = sb("aw3", [P, 8])
        ab3 = sb("ab3", [D, 1])
        target = sb("target", [P, 2, D])
        query = [sb(f"query{c}", [P, D]) for c in range(2)]
        hq = [sb(f"hq{c}", [P, D]) for c in range(2)]
        qh = sb("qh", [P, 2, 2, D])
        att1 = sb("att1", [P, P])
        att2 = sb("att2", [P, P])
        score = [sb(f"score{c}", [D, 2, 2 * UN + T]) for c in range(2)]
        len_f = sb("len_f", [D, 2, 2])
        mask = sb("mask", [D, 2, T])
        smx = sb("smx", [D, 2])
        ssum = sb("ssum", [D, 2])
        prob = sb("prob", [D, 2, T])
        prob_t = sb("prob_t", [P, 4, D])
        att_bc = [sb(f"att_bc{c}", [P, 2, UN * D]) for c in range(2)]
        r_t = [sb(f"r_t{c}", [P, D]) for c in range(2)]
        z_t = [sb(f"z_t{c}", [P, D]) for c in range(2)]
        az_t = [sb(f"az_t{c}", [P, D]) for c in range(2)]
        m_t = [sb(f"m_t{c}", [P, D]) for c in range(2)]
        n_t = [sb(f"n_t{c}", [P, D]) for c in range(2)]
        v_t = [sb(f"v_t{c}", [P, D]) for c in range(2)]
        keep_t = [sb(f"keep_t{c}", [P, D]) for c in range(2)]
        state = [sb(f"state{c}", [P, 2, D]) for c in range(2)]
        sparse = slot_idx[:, :, :].rearrange("p k f -> p (k f)")[:, 0:2 * NSP * E].bitcast(F32)
        sparse = sparse.rearrange("p (c n) -> p c n", c=2)
        dense_sb = sb("dense_sb", [P, 2, ND])
        late = hist_a[:, 0:8 * B // D, :].rearrange("p k d -> p (k d)").rearrange("p (k n) -> p k n", n=B)
        feat = [late[:, 0, :], late[:, 1, :], sb("feat2", [P, B])[:, :]]
        fnorm = [late[:, 2 + k, :] for k in range(3)]
        par = sb("par", [P, 3, 2])
        stats = sb("stats", [P, 3, 6])
        mv = sb("mv", [P, 3, 2])
        std = sb("std", [P, 3])
        sc = sb("sc", [P, 3])
        w1_sb = sb("w1_sb", [P, 3, HID1])
        b1_sb = sb("b1_sb", [P, 2])
        w2_sb = sb("w2_sb", [P, 2, HID2])
        b2_sb = sb("b2_sb", [P, 1])
        ow_sb = sb("ow_sb", [P, 1])
        ob_sb = sb("ob_sb", [1, 1])
        h1 = late[:, 5:7, :]
        h2 = late[:, 7, :]
        ycol = sb("ycol", [P, 2])
        yrow = late[0:1, 0, :]

        bank_r = [bank(f"bank_r{c}") for c in range(2)]
        bank_z = [bank(f"bank_z{c}") for c in range(2)]
        bank_n = [bank(f"bank_n{c}") for c in range(2)]
        bank_1 = bank("bank_1")
        turn_bank = [bank_r[1], bank_z[1]]
        bank_2 = bank("bank_2")

        att_dram = nc.dram_tensor("att_dram", [2, 2, 2 * T + UN, D], F32, kind="Internal").ap()

        s_ints = sem("s_ints")
        s_weights = sem("s_weights")
        s_dnn = sem("s_dnn")
        s_consts = sem("s_consts")
        s_dve = sem("s_dve")
        s_act = sem("s_act")
        s_perm = sem("s_perm")
        s_sorted = sem("s_sorted")
        s_ends = sem("s_ends")
        s_bounds = sem("s_bounds")
        s_table = sem("s_table")
        s_stage = sem("s_stage")
        s_pair = [sem(f"s_pair{p}") for p in range(4)]
        s_target = sem("s_target")
        s_sparse = sem("s_sparse")
        s_turned = sem("s_turned")
        s_filed = sem("s_filed")
        s_permt = sem("s_permt")
        s_permc = sem("s_permc")
        s_query = sem("s_query")
        s_qcopy = sem("s_qcopy")
        s_hq = sem("s_hq")
        s_hqs = sem("s_hqs")
        s_setup = sem("s_setup")
        s_zero_b = sem("s_zero_b")
        s_ztail = sem("s_ztail")
        s_qh = [sem(f"s_qh{c}") for c in range(2)]
        s_l1 = [sem(f"s_l1_{c}") for c in range(2)]
        s_a1 = [sem(f"s_a1_{c}") for c in range(2)]
        s_l2 = [sem(f"s_l2_{c}") for c in range(2)]
        s_a2 = [sem(f"s_a2_{c}") for c in range(2)]
        s_l3 = [sem(f"s_l3_{c}") for c in range(2)]
        s_sc = [sem(f"s_sc{c}") for c in range(2)]
        s_max = [sem(f"s_max{c}") for c in range(2)]
        s_exp = [sem(f"s_exp{c}") for c in range(2)]
        s_prob = [sem(f"s_prob{c}") for c in range(2)]
        s_pt = [sem(f"s_pt{c}") for c in range(2)]
        s_ptc = [sem(f"s_ptc{c}") for c in range(2)]
        s_pd = [sem(f"s_pd{c}") for c in range(2)]
        s_bc = [sem(f"s_bc{c}") for c in range(2)]
        s_spt = sem("s_spt")
        s_feat = sem("s_feat")
        s_dt = sem("s_dt")
        s_norm = sem("s_norm")
        s_var = sem("s_var")
        s_std = sem("s_std")
        s_h1 = sem("s_h1")
        s_h1c = sem("s_h1c")
        s_h2 = sem("s_h2")
        s_h2c = sem("s_h2c")
        s_y = sem("s_y")
        s_yc = sem("s_yc")
        s_yo = sem("s_yo")
        s_yr = sem("s_yr")
        s_out = sem("s_out")

        class Role:

            def __init__(self, name, kind, c):
                self.kind, self.c = kind, c
                self.state_ok = sem(f"{name}_state_ok")
                self.r_mm = sem(f"{name}_r_mm")
                self.z_mm = sem(f"{name}_z_mm")
                self.n_mm = sem(f"{name}_n_mm")
                self.r_ok = sem(f"{name}_r_ok")
                self.z_ok = sem(f"{name}_z_ok")
                self.pre_ok = sem(f"{name}_pre_ok")
                self.n_free = sem(f"{name}_n_free")
                self.mul_ok = sem(f"{name}_mul_ok")
                self.az_ok = sem(f"{name}_az_ok")
                self.keep_ok = sem(f"{name}_keep_ok")
                self.v_ok = sem(f"{name}_v_ok")

            def order(self, u):
                return u % 2 if self.c == 0 else 1 - u % 2

        gru = [Role("gru_a", GRU, 0), Role("gru_b", GRU, 1)]
        aug = [Role("aug_a", AUG, 0), Role("aug_b", AUG, 1)]

        def blocks(tile, first, n):
            flat = tile[:, :, :].rearrange("p k d -> p (k d)")
            return flat[:, bass.ds(limited(first * D, 0, (tile.shape[1] - n) * D), n * D)]

        def b_slot(top, u):
            return top - 1 - u

        def pair_of_states(c, base, u):
            return blocks(hist_a, base + (UN + 1 + u), 2) if c == 0 else blocks(slot_x, b_slot(base, u + 1), 2)

        def pair_of_inputs(c, base, u):
            return blocks(slot_x, base + u, 2) if c == 0 else blocks(slot_x, b_slot(base, u + 1), 2)

        def state_before(role, base, u):
            if role.kind == AUG:
                return state[role.c][:, u % 2, :]
            return blocks(hist_a, base + (UN + u), 1) if role.c == 0 else blocks(slot_x, b_slot(base, u - 1), 1)

        def state_after(role, base, u):
            if role.kind == AUG:
                return state[role.c][:, (u + 1) % 2, :]
            return blocks(hist_a, base + (UN + 1 + u), 1) if role.c == 0 else blocks(slot_x, b_slot(base, u), 1)

        def bounds(eng):
            eng.wait_ge(s_bounds, 1)
            slots = eng.value_load(ends_i[0:1, 0:1], min_val=T + UN, max_val=2 * T)
            steps = eng.value_load(ends_i[0:1, 1:2], min_val=1, max_val=T)
            n_slots = eng.snap((slots + (UN - 1)) >> 3)
            n_b = eng.snap((steps + (UN - 1)) >> 3)
            return n_slots, n_b

        def limited(value, low, high):
            return value if isinstance(value, int) else value.with_bounds(min_val=low, max_val=high)

        block = ctx.enter_context(nc.Block())

        @block.sync
        def _(sp):
            sp.dma_start(lrow_i, lens_row).then_inc(s_ints, 16)
            sp.dma_start(lcol_i[:, :], lens_col).then_inc(s_ints, 16)
            sp.dma_start(raw[:, :, :], ints).then_inc(s_ints, 16)
            sp.dma_start(gw[:, :, :], gate_w).then_inc(s_weights, 16)
            sp.dma_start(gb[:, :, :], gate_b).then_inc(s_weights, 16)
            sp.dma_start(aw1[:, :, :], att_w1).then_inc(s_weights, 16)
            sp.dma_start(ab1[:, :], att_b1).then_inc(s_weights, 16)
            sp.dma_start(aw2[:, :, :], att_w2).then_inc(s_weights, 16)
            sp.dma_start(ab2[:, :], att_b2).then_inc(s_weights, 16)
            sp.dma_start(aw3[:, :], att_w3).then_inc(s_weights, 16)
            sp.dma_start(ab3[:, :], att_b3).then_inc(s_weights, 16)
            sp.dma_start(dense_sb[:, :, :], dense).then_inc(s_dnn, 16)
            sp.dma_start(par[:, :, :], bn_par).then_inc(s_dnn, 16)
            sp.dma_start(w1_sb[:, :, :], w1).then_inc(s_dnn, 16)
            sp.dma_start(b1_sb[:, :], b1).then_inc(s_dnn, 16)
            sp.dma_start(w2_sb[:, :, :], w2).then_inc(s_dnn, 16)
            sp.dma_start(b2_sb[:, :], b2).then_inc(s_dnn, 16)
            sp.dma_start(ow_sb[:, :], out_w).then_inc(s_dnn, 16)
            sp.dma_start(ob_sb[:, :], out_b).then_inc(s_dnn, 16)
            sp.wait_ge(s_setup, 1)
            tail = T + UN
            for c in range(2):
                for s in range(2):
                    sp.dma_start(att_dram[c, s, T:, :].rearrange("(a b) d -> a (b d)", a=tail // UN),
                                 hist_a[0:tail // UN, 0:UN, :].rearrange("p k d -> p (k d)")).then_inc(s_ztail, 16)
            sp.wait_ge(s_ztail, 64)

            def save_att(c):
                flat = att_dram[c, :, 0:T, :]
                sp.wait_ge(s_ptc[c], 1)
                n = 0
                for k in range(4):
                    row, left = k * P, min(P, 2 * T - k * P)
                    while left:
                        s, t0 = row // T, row % T
                        m = min(left, T - t0)
                        at = row - k * P
                        sp.dma_start(flat[s, t0:t0 + m, :], prob_t[at:at + m, k, :]).then_inc(s_pd[c], 16)
                        row, left, n = row + m, left - m, n + 1
                sp.wait_ge(s_pd[c], 16 * n)

            def load_att(c, first, at):
                for s in range(2):
                    src = att_dram[c, s, bass.ds(first, UN), :].rearrange("t d -> (t d)")
                    src = src.rearrange("(a n) -> a n", a=1).to_broadcast([D, UN * D])
                    dst = att_bc[c][:, :, :].rearrange("p b n -> p (b n)")[
                        s * D:(s + 1) * D, bass.ds(at, UN * D)]
                    sp.dma_start(dst, src).then_inc(s_bc[c], 16)

            n_slots, n_b = bounds(sp)
            n_rest = sp.snap(sp_max(sp, BODIES - n_b, n_b))
            save_att(0)
            load_att(0, 0, 0)
            with sp.Fori(0, n_b) as i:
                first = held(sp, "first", (i + 1) * UN, UN, T + UN)
                at = held(sp, "at", ((i + 1) & 1) * (UN * D), 0, UN * D)
                sp.wait_ge(aug[0].az_ok, i * UN + 1)
                sp.wait_ge(s_bc[0], i * 32 + 32)
                load_att(0, first, at)
            save_att(1)
            load_att(1, 0, 0)
            with sp.Fori(0, n_rest) as i:
                j = sp.snap(limited(n_b + i, 1, 2 * BODIES - 1))
                for c, k in ((0, j), (1, i)):
                    first = held(sp, f"first{c}", (k + 1) * UN, UN, 2 * T)
                    at = held(sp, f"at{c}", ((k + 1) & 1) * (UN * D), 0, UN * D)
                    sp.wait_ge(aug[c].az_ok, k * UN + 1)
                    sp.wait_ge(s_bc[c], k * 32 + 32)
                    load_att(c, first, at)
            j = sp.snap(limited(n_b + n_rest, 1, 2 * BODIES))
            sp.wait_ge(s_bc[0], j * 32 + 32)
            sp.wait_ge(s_bc[1], n_rest * 32 + 32)
            sp.wait_ge(s_yr, 1)
            sp.dma_start(out, yrow).then_inc(s_out, 16)
            sp.wait_ge(s_out, 16)

        @block.gpsimd
        def _(pool):
            nc.gpsimd.memset(ident[:, :], 0.0).then_inc(s_consts, 1)
            pool.wait_ge(s_consts, 1)
            nc.gpsimd.affine_select(out=ident[:, :], in_=ident[:, :], compare_op=ALU.not_equal, fill=1.0, base=0,
                                    pattern=[[-1, P]], channel_multiplier=1).then_inc(s_consts, 1)
            nc.gpsimd.iota(iota_b, pattern=[[1, B]], base=0, channel_multiplier=0,
                           allow_small_or_imprecise_dtypes=True).then_inc(s_consts, 1)
            nc.gpsimd.iota(iota_p[:, :], pattern=[[1, 1]], base=0, channel_multiplier=1,
                           allow_small_or_imprecise_dtypes=True).then_inc(s_consts, 1)
            nc.gpsimd.iota(pos_rank[:, 0:P], pattern=[[1, P]], base=0, channel_multiplier=0,
                           allow_small_or_imprecise_dtypes=True).then_inc(s_consts, 1)
            nc.gpsimd.iota(pos_rank[:, P:B], pattern=[[-1, P]], base=B - 1, channel_multiplier=0,
                           allow_small_or_imprecise_dtypes=True).then_inc(s_consts, 1)
            nc.gpsimd.iota(slot_no[:, :], pattern=[[1, T]], base=0, channel_multiplier=0,
                           allow_small_or_imprecise_dtypes=True).then_inc(s_consts, 1)

            def gather(dst, idx):
                return nc.gpsimd.indirect_dma_start(
                    out=dst, out_offset=None, in_=emb[:, :],
                    in_offset=bass.IndirectOffsetOnAxis(ap=idx, axis=0))

            flat_idx = slot_idx[:, :, :].rearrange("p k f -> p (k f)")

            def fetch_half(i, k, first):
                if not first:
                    pool.wait_ge(s_pair[2 * k], i * 64)
                    pool.wait_ge(s_pair[2 * k + 1], i * 64)
                nc.gpsimd.tensor_copy(stage_idx[:, :, :].rearrange("p k f -> p (k f)")[:, k * UN:(k + 1) * UN],
                                      flat_idx[:, bass.ds(i * (2 * UN) + k * UN, UN)]).then_inc(s_stage, 1)
                pool.wait_ge(s_stage, i * 2 + (k + 1))
                if not first:
                    pool.wait_ge(s_turned, i * 2 + (k - 1))
                nc.gpsimd.tensor_tensor(gate_open[:, :], iota_p[:, :], iota_p[:, :], ALU.add)
                for q in range(4):
                    for f in range(2):
                        slot = 4 * k + q
                        gather(fetched[:, slot, f * E:(f + 1) * E],
                               stage_idx[:, slot, f:f + 1]).then_inc(s_pair[slot // 2], 16)

            pool.wait_ge(s_table, 1)
            fetch_half(0, 0, True)
            fetch_half(0, 1, True)
            for c in range(2):
                for f in range(2):
                    gather(target[:, c, f * E:(f + 1) * E], misc_idx[:, c, f:f + 1]).then_inc(s_target, 16)
            n_slots, n_b = bounds(pool)
            with pool.Fori(1, n_slots) as i:
                i = pool.snap(limited(i, 1, 2 * BODIES - 1))
                fetch_half(i, 0, False)
                fetch_half(i, 1, False)
            for c in range(2):
                for f in range(NSP):
                    gather(sparse[:, c, f * E:(f + 1) * E], misc_idx[:, c, 2 + f:3 + f]).then_inc(s_sparse, 16)

        @block.tensor
        def _(pe):
            mm = nc.tensor.matmul

            pe.wait_ge(s_perm, 1)
            for c in range(2):
                for k in range(2):
                    last = mm(bank_r[c][:, 0:IDX + MISC], perm[:, k, c * P:(c + 1) * P],
                              wrapped[:, k, c * IDX:c * IDX + IDX + MISC], start=k == 0, stop=k == 1)
                last.then_inc(s_sorted, 1)
            pe.wait_ge(s_ends, 1)
            for k in range(2):
                last = mm(bank_z[0][0:1, k * P:(k + 1) * P], ends[:, k:k + 1], ident[:, :], start=True, stop=True)
            last.then_inc(s_sorted, 1)
            for c in range(2):
                for k in range(2):
                    last = nc.tensor.transpose(bank_n[c][:, k * P:(k + 1) * P], perm[:, k, c * P:(c + 1) * P],
                                               ident[:, :])
            last.then_inc(s_permt, 1)
            pe.wait_ge(s_dnn, 128)
            for k in range(2):
                last = mm(bank_2[0:ND, 256:512], dense_sb[:, k, :], perm[:, k, :], start=k == 0, stop=k == 1)
            last.then_inc(s_dt, 1)

            def turn(m, k):
                for q in range(2):
                    pe.wait_ge(s_pair[2 * k + q], m * 64 + 64)
                pe.wait_ge(s_filed, m * 8 + (4 * k - 3))
                for q in range(2):
                    pair = fetched[:, 4 * k + 2 * q:4 * k + 2 * q + 2, :].rearrange("p k d -> p (k d)")
                    last = nc.tensor.transpose(turn_bank[k][:, P * q:P * (q + 1)], pair, ident[:, :])
                last.then_inc(s_turned, 1)

            def seed_rz(role, base, u):
                k, c = role.kind, role.c
                x = pair_of_inputs(c, base, u) if k == GRU else pair_of_states(c, base, u)
                for g, to in ((R_, bank_r[c]), (Z_, bank_z[c])):
                    mm(to[:, 0:P], bias_w[:, 4 * k + g, :], ones_b[:, :], start=True, stop=False,
                       skip_group_check=True)
                    mm(to[:, 0:P], gw[:, 6 * k + g, :], x, start=False, stop=True, skip_group_check=True)

            def seed_n(role, base, u):
                k, c = role.kind, role.c
                x = pair_of_inputs(c, base, u) if k == GRU else pair_of_states(c, base, u)
                to = bank_n[c]
                mm(to[:, 0:P], bias_w[:, 4 * k + 2, :], ones_b[:, :], start=True, stop=False, skip_group_check=True)
                mm(to[:, 0:P], gw[:, 6 * k + 2, :], x, start=False, stop=True, skip_group_check=True)
                mm(to[:, P:2 * P], bias_w[:, 4 * k + 3, :], ones_b[:, :], start=True, stop=True,
                   skip_group_check=True)

            def gates(role, base, u, t1):
                k, c = role.kind, role.c
                at = role.order(u) * D
                if u % 2 == 0:
                    pe.wait_ge(role.n_free, t1)
                    seed_n(role, base, u)
                pe.wait_ge(role.state_ok, t1)
                h = state_before(role, base, u)
                mm(bank_r[c][:, at:at + D], gw[:, 6 * k + 3 + R_, :], h, start=False, stop=True,
                   skip_group_check=True).then_inc(role.r_mm, 1)
                mm(bank_n[c][:, P + at:P + at + D], gw[:, 6 * k + 3 + N_, :], h, start=False, stop=True,
                   skip_group_check=True).then_inc(role.n_mm, 1)
                mm(bank_z[c][:, at:at + D], gw[:, 6 * k + 3 + Z_, :], h, start=False, stop=True,
                   skip_group_check=True).then_inc(role.z_mm, 1)

            def seed_next(role, base_next, u_next, t1):
                pe.wait_ge(role.r_ok, t1)
                pe.wait_ge(role.z_ok, t1)
                seed_rz(role, base_next, u_next)

            def att_layer1(c, base, p, n1):
                pe.wait_ge(s_qh[c], n1)
                pe.wait_ge(s_a1[c], n1)
                to = bank_1[:, 0:P]
                both = hq[c][:, :].rearrange("p (o d) -> p o d", o=1).to_broadcast([P, 2, D])
                mm(to, wk[:, :], pair_of_states(c, base, 2 * p), start=True, stop=False)
                mm(to, aw1[:, 3, :], qh[:, p % 2, :, :], start=False, stop=False)
                mm(to.rearrange("p (o d) -> p o d", o=2), ident[:, :], both, start=False,
                   stop=True).then_inc(s_l1[c], 1)

            def att_layer2(c, p, n1, body1):
                pe.wait_ge(s_a1[c], n1 + 1)
                if p == 0:
                    pe.wait_ge(s_sc[c], body1)
                mm(bank_2[:, 0:P], aw2[:, p, :], att1[:, :], start=p == 0, stop=p == 3,
                   skip_group_check=True).then_inc(s_l2[c], 1)

            def att_layer3(c, body1):
                pe.wait_ge(s_a2[c], body1)
                mm(bank_2[:, P:P + 8], att2[:, :], aw3[:, :], start=True, stop=True,
                   skip_group_check=True).then_inc(s_l3[c], 1)

            def att_extras(c, base, i, u):
                if u % 2 == 0:
                    att_layer1(c, base, u // 2, i * 4 + (u // 2 + 1))
                else:
                    att_layer2(c, u // 2, i * 4 + (u // 2 + 1), i + 1)
                if u == UN - 1:
                    att_layer3(c, i + 1)

            pe.wait_ge(s_setup, 1)
            pe.wait_ge(s_permc, 1)
            for k in range(2):
                for q in range(2):
                    pe.wait_ge(s_pair[2 * k + q], 64)
                for q in range(2):
                    pair = fetched[:, 4 * k + 2 * q:4 * k + 2 * q + 2, :].rearrange("p k d -> p (k d)")
                    last = nc.tensor.transpose(turn_bank[k][:, P * q:P * (q + 1)], pair, ident[:, :])
                last.then_inc(s_turned, 1)
            pe.wait_ge(s_filed, 9)
            seed_rz(gru[0], 0, 0)
            pe.wait_ge(s_target, 64)
            nc.tensor.transpose(bank_1[:, 0:P], target[:, :, :].rearrange("p c d -> p (c d)"),
                                ident[:, :]).then_inc(s_query, 1)
            pe.wait_ge(s_qcopy, 4)
            pe.wait_ge(s_feat, 1)
            for c in range(2):
                last = mm(bank_2[:, c * D:(c + 1) * D], wq[:, :], query[c][:, :], start=True, stop=True)
            last.then_inc(s_hq, 1)
            pe.wait_ge(s_hqs, 2)
            mm(bank_2[:, P:P + 8], att2[:, :], aw3[:, :], start=True, stop=True,
               skip_group_check=True).then_inc(s_l3[0], 1)
            n_slots, n_b = bounds(pe)

            def phase1(i, turning):
                base = pe.snap(i * UN) if not isinstance(i, int) else i * UN
                back = base - UN
                for u in range(UN):
                    gates(gru[0], base, u, base + (u + 1))
                    att_extras(0, back, i, u)
                    if turning and u == 2:
                        turn(i + 1, 0)
                    if turning and u == 6:
                        turn(i + 1, 1)
                    if u % 2 and (u < UN - 1 or turning):
                        if u == UN - 1:
                            pe.wait_ge(s_filed, i * 8 + 17)
                        seed_next(gru[0], base, u + 1, base + (u + 1))

            with pe.Fori(0, BODIES - 1) as i:
                phase1(i, True)
            phase1(BODIES - 1, False)
            with pe.Fori(BODIES, n_slots) as m:
                m = pe.snap(limited(m, BODIES, 2 * BODIES - 1))
                turn(m, 0)
                turn(m, 1)
            for u in range(UN):
                att_extras(0, BODIES * UN - UN, BODIES, u)

            def att_turn(c):
                pe.wait_ge(s_prob[c], 1)
                flat = prob[:, :, :].rearrange("p s t -> p (s t)")
                for k in range(4):
                    n = min(P, 2 * T - k * P)
                    last = nc.tensor.transpose(bank_2[0:n, k * D:(k + 1) * D], flat[:, k * P:k * P + n],
                                               ident[0:D, 0:D])
                last.then_inc(s_pt[c], 1)

            att_turn(0)
            pe.wait_ge(s_ptc[0], 1)
            mm(bank_2[:, P:P + 8], att2[:, :], aw3[:, :], start=True, stop=True,
               skip_group_check=True).then_inc(s_l3[1], 1)

            pe.wait_ge(gru[0].state_ok, T + 1)
            pe.wait_ge(s_filed, n_slots * 8 + 1)
            pe.wait_ge(s_zero_b, 1)
            seed_rz(aug[0], 0, 0)
            seed_rz(gru[1], limited(n_slots * UN, T + UN, 2 * T), 0)
            with pe.Fori(0, n_b) as i:
                base = pe.snap(i * UN)
                top = pe.snap(limited(n_slots * UN - base, UN, 2 * T))
                for u in range(UN):
                    t1 = pe.snap(base + (u + 1))
                    gates(aug[0], base, u, t1)
                    gates(gru[1], top, u, t1)
                    att_extras(1, top + UN, i, u)
                    if u % 2:
                        seed_next(aug[0], base, u + 1, t1)
                        seed_next(gru[1], top, u + 1, t1)
            top = pe.snap(limited(n_slots * UN - n_b * UN, 0, 2 * T))
            for u in range(UN):
                att_extras(1, top + UN, n_b, u)
            att_turn(1)

            pe.wait_ge(gru[1].state_ok, n_b * UN + 1)
            seed_rz(aug[1], limited(n_slots * UN, T + UN, 2 * T), 0)
            n_rest = pe.snap(sp_max(pe, BODIES - n_b, n_b))
            with pe.Fori(0, n_rest) as i:
                j = n_b + i
                done = pe.snap(j * UN)
                base = pe.snap(limited(sp_min(pe, done, T - UN), UN, T - UN))
                own = pe.snap(i * UN)
                top = pe.snap(limited(n_slots * UN - own, UN, 2 * T))
                for u in range(UN):
                    ta = pe.snap(done + (u + 1))
                    gates(aug[0], base, u, ta)
                    tb = pe.snap(own + (u + 1))
                    gates(aug[1], top, u, tb)
                    if u % 2:
                        seed_next(aug[0], base, u + 1, ta)
                        seed_next(aug[1], top, u + 1, tb)

            pe.wait_ge(s_sparse, 16 * 2 * NSP)
            pe.wait_ge(s_ptc[1], 1)
            for c in range(2):
                for k in range(2):
                    last = nc.tensor.transpose(bank_1[:, (2 * c + k) * P:(2 * c + k + 1) * P],
                                               sparse[:, c, k * P:(k + 1) * P], ident[:, :])
            last.then_inc(s_spt, 1)
            pe.wait_ge(s_norm, 1)
            for m in range(2):
                for k, rows_ in enumerate((P, P, D + ND)):
                    last = mm(bank_r[m][:, 0:B], w1_sb[0:rows_, k, m * P:(m + 1) * P], fnorm[k][0:rows_, :],
                              start=k == 0, stop=k == 2)
            last.then_inc(s_h1, 1)
            pe.wait_ge(s_h1c, 2)
            for m in range(2):
                last = mm(bank_z[0][:, 0:B], w2_sb[:, m, :], h1[:, m, :], start=m == 0, stop=m == 1)
            last.then_inc(s_h2, 1)
            pe.wait_ge(s_h2c, 1)
            for c in range(2):
                last = mm(bank_z[1][:, c:c + 1], h2[:, c * P:(c + 1) * P], ow_sb[:, :], start=True, stop=True)
            last.then_inc(s_y, 1)
            pe.wait_ge(s_yc, 1)
            for c in range(2):
                last = mm(bank_2[0:1, 0:B], ycol[:, c:c + 1], perm_t[:, c, :], start=c == 0, stop=c == 1)
            last.then_inc(s_yo, 1)

        @block.scalar
        def _(act):
            A = nc.scalar.activation

            def file_piece(m, k, n):
                e, s = n // 2, n % 2
                if n == 0:
                    act.wait_ge(s_turned, m * 2 + (k + 1))
                src = turn_bank[k][e * D:(e + 1) * D, 0:2 * P].rearrange("p (q c) -> p q c", q=2)[:, :, s * D:(s + 1) * D]
                dst = slot_x[s * D:(s + 1) * D, bass.ds(m * UN + (4 * k + e), 2, step=2), :]
                A(dst, src, ACT.Copy).then_inc(s_filed, 1)

            def sig_r(role, u, t1):
                act.wait_ge(role.r_mm, t1)
                at = role.order(u) * D
                A(r_t[role.c][:, :], bank_r[role.c][:, at:at + D], ACT.Sigmoid).then_inc(role.r_ok, 1)

            def sig_z(role, u, t1):
                act.wait_ge(role.z_mm, t1)
                at = role.order(u) * D
                A(z_t[role.c][:, :], bank_z[role.c][:, at:at + D], ACT.Sigmoid,
                  scale=-1.0 if role.kind == GRU else 1.0).then_inc(role.z_ok, 1)

            def tanh(role, u, t1):
                act.wait_ge(role.pre_ok, t1)
                at = role.order(u) * D
                A(n_t[role.c][:, :], bank_n[role.c][:, at:at + D], ACT.Tanh).then_inc(role.n_free, 1)

            def att_extras(c, i, u):
                if u % 2 == 0:
                    n1 = i * 4 + (u // 2 + 1)
                    act.wait_ge(s_l1[c], n1)
                    act.wait_ge(s_l2[c], n1)
                    A(att1[:, :], bank_1[:, 0:P], ACT.Relu).then_inc(s_a1[c], 1)
                if u == UN - 1:
                    act.wait_ge(s_l2[c], i * 4 + 5)
                    A(att2[:, :], bank_2[:, 0:P], ACT.Relu, bias=ab2[:, :]).then_inc(s_a2[c], 1)

            act.wait_ge(s_permt, 1)
            for c in range(2):
                last = A(perm_t[:, c, :], bank_n[c][:, 0:B], ACT.Copy)
            last.then_inc(s_permc, 1)
            act.wait_ge(s_dt, 1)
            A(feat[2][D:D + ND, :], bank_2[0:ND, 256:512], ACT.Copy).then_inc(s_feat, 1)
            act.wait_ge(s_setup, 1)
            for k in range(2):
                for n in range(4):
                    file_piece(0, k, n)
            act.wait_ge(s_query, 1)
            for c in range(2):
                for s in range(2):
                    A(query[c][s * D:(s + 1) * D, :], bank_1[c * D:(c + 1) * D, s * D:(s + 1) * D],
                      ACT.Copy).then_inc(s_qcopy, 1)
            n_slots, n_b = bounds(act)

            def phase1(i, turning):
                base = act.snap(i * UN) if not isinstance(i, int) else i * UN
                for u in range(UN):
                    t1 = base + (u + 1)
                    sig_r(gru[0], u, t1)
                    sig_z(gru[0], u, t1)
                    tanh(gru[0], u, t1)
                    att_extras(0, i, u)
                    if turning and u in (2, 3):
                        for n in range(2):
                            file_piece(i + 1, 0, 2 * (u - 2) + n)
                    if turning and u in (6, 7):
                        for n in range(2):
                            file_piece(i + 1, 1, 2 * (u - 6) + n)

            with act.Fori(0, BODIES - 1) as i:
                phase1(i, True)
            phase1(BODIES - 1, False)
            with act.Fori(BODIES, n_slots) as m:
                m = act.snap(limited(m, BODIES, 2 * BODIES - 1))
                for k in range(2):
                    for n in range(4):
                        file_piece(m, k, n)
            for u in range(UN):
                att_extras(0, BODIES, u)

            def exps(c):
                act.wait_ge(s_max[c], 1)
                for s in range(2):
                    last = A(prob[:, s, :], score[c][:, s, 2 * UN:], ACT.Exp, bias=smx[:, s:s + 1],
                             accum_out=ssum[:, s:s + 1])
                last.then_inc(s_exp[c], 1)

            exps(0)
            with act.Fori(0, n_b) as i:
                base = act.snap(i * UN)
                for u in range(UN):
                    t1 = act.snap(base + (u + 1))
                    sig_r(aug[0], u, t1)
                    sig_z(aug[0], u, t1)
                    sig_r(gru[1], u, t1)
                    tanh(aug[0], u, t1)
                    sig_z(gru[1], u, t1)
                    tanh(gru[1], u, t1)
                    att_extras(1, i, u)
            for u in range(UN):
                att_extras(1, n_b, u)
            exps(1)
            n_rest = act.snap(sp_max(act, BODIES - n_b, n_b))
            with act.Fori(0, n_rest) as i:
                done = act.snap((n_b + i) * UN)
                own = act.snap(i * UN)
                for u in range(UN):
                    ta = act.snap(done + (u + 1))
                    tb = act.snap(own + (u + 1))
                    sig_r(aug[0], u, ta)
                    sig_z(aug[0], u, ta)
                    sig_r(aug[1], u, tb)
                    tanh(aug[0], u, ta)
                    sig_z(aug[1], u, tb)
                    tanh(aug[1], u, tb)
            act.wait_ge(s_var, 1)
            A(std[:, :], mv[:, :, 1], ACT.Sqrt).then_inc(s_std, 1)
            act.wait_ge(s_h1, 1)
            for m in range(2):
                A(h1[:, m, :], bank_r[m][:, 0:B], ACT.Relu, bias=b1_sb[:, m:m + 1]).then_inc(s_h1c, 1)
            act.wait_ge(s_h2, 1)
            A(h2[:, :], bank_z[0][:, 0:B], ACT.Relu, bias=b2_sb[:, :]).then_inc(s_h2c, 1)

        @block.vector
        def _(dve):
            v = nc.vector
            count = [0]

            def link(ins):
                count[0] += 1
                ins.then_inc(s_dve, 1)
                dve.wait_ge(s_dve, count[0])

            dve.wait_ge(s_ints, 48)
            dve.wait_ge(s_consts, 7)
            link(v.tensor_scalar(lrow_i, lrow_i, 0.0, float(T), ALU.max, ALU.min))
            link(v.tensor_scalar(lcol_i[:, :], lcol_i[:, :], 0.0, float(T), ALU.max, ALU.min))
            link(v.scalar_tensor_tensor(key_row, lrow_i, float(B), iota_b, ALU.mult, ALU.add))
            link(v.tensor_scalar(key_col[:, 0:1], iota_p[:, :], 0.0, None, ALU.add))
            link(v.tensor_scalar(key_col[:, 1:2], iota_p[:, :], float(P), None, ALU.add))
            link(v.scalar_tensor_tensor(key_col[:, :], lcol_i[:, :], float(B), key_col[:, :], ALU.mult, ALU.add))
            for k in range(2):
                link(v.tensor_scalar(above, key_row, key_col[:, k:k + 1], None, ALU.is_gt))
                link(v.reduce_sum(rank[:, k:k + 1], above, AX.X))
                link(v.tensor_scalar(perm[:, k, :], pos_rank, rank[:, k:k + 1], None, ALU.is_equal))
            link(v.tensor_scalar(wrapped[:, :, :], raw[:, :, :], 0.0, float(V), ALU.is_lt, ALU.mult))
            link(v.tensor_tensor(rows[:, :, :], wrapped[:, :, :], raw[:, :, :], ALU.add))
            link(v.tensor_scalar(wrapped[:, :, :], rows[:, :, :], 0.0, float(V - 1), ALU.max, ALU.min))
            at = IDX + MISC - 1
            link(v.tensor_copy(wrapped[:, 0, at:at + 1], lcol_i[:, 0:1]))
            link(v.tensor_copy(wrapped[:, 1, at:at + 1], lcol_i[:, 1:2]))
            v.memset(from_b[:, :, :], 0.0)
            v.memset(score[0][:, :, :], 0.0)
            v.memset(score[1][:, :, :], 0.0).then_inc(s_perm, 1)
            for c in range(2):
                dve.wait_ge(s_sorted, c + 1)
                link(v.tensor_copy(srt[:, c, :], bank_r[c][:, 0:IDX + MISC]))
            len_a = srt[:, 0, IDX + MISC - 1:IDX + MISC]
            len_b = srt[:, 1, MISC - 1:MISC]
            link(v.tensor_tensor(ends[:, 0:1], len_a, len_b, ALU.add))
            v.tensor_copy(ends[:, 1:2], len_b).then_inc(s_ends, 1)
            v.tensor_copy(misc_idx[:, 0, :], srt[:, 0, IDX:IDX + 2 + NSP])
            v.tensor_copy(misc_idx[:, 1, :], srt[:, 1, 0:2 + NSP])
            for s in range(2):
                v.tensor_copy(len_f[:, 0, s:s + 1], len_a[s * D:(s + 1) * D, :])
                v.tensor_copy(len_f[:, 1, s:s + 1], len_b[s * D:(s + 1) * D, :])
            dve.wait_ge(s_sorted, 3)
            link(v.reduce_max(ends_f[:, :], bank_z[0][0:1, 0:B].rearrange("p (k n) -> p k n", k=2), AX.X))
            link(v.tensor_scalar(ends_f[:, 0:1], ends_f[:, 0:1], float(T + UN), None, ALU.max))
            link(v.tensor_scalar(ends_f[:, 1:2], ends_f[:, 1:2], 1.0, None, ALU.max))
            v.tensor_copy(ends_i[:, :], ends_f[:, :]).then_inc(s_bounds, 1)
            n_slots, n_b = bounds(dve)
            off = dve.snap(limited(n_slots * UN - T, UN, T))
            link(v.tensor_copy(from_b[:, bass.ds(off, T), :].rearrange("p k f -> p (k f)"), srt[:, 1, MISC:]))
            link(v.tensor_scalar(keep_a, slot_no[:, :], len_a, None, ALU.is_lt))
            for f in range(2):
                link(v.tensor_tensor(rows[:, f, 0:T], srt[:, 0, 0:IDX].rearrange("p (k f) -> p f k", f=2)[:, f, :],
                                     from_b[:, 0:T, f], ALU.subtract))
                link(v.tensor_tensor(rows[:, f, 0:T], rows[:, f, 0:T], keep_a, ALU.mult))
                link(v.tensor_tensor(slot_idx[:, 0:T, f], rows[:, f, 0:T], from_b[:, 0:T, f], ALU.add))
            v.tensor_copy(slot_idx[:, T:, :].rearrange("p k f -> p (k f)"),
                          from_b[:, T:, :].rearrange("p k f -> p (k f)")).then_inc(s_table, 1)

            dve.wait_ge(s_weights, 128)
            v.memset(bias_w[:, :, :].rearrange("p g c -> p (g c)").bitcast(F32), 0.0)
            v.memset(ones_b[:, :], 1.0)
            for k in range(2):
                link(v.tensor_tensor(gbs[:, 4 * k:4 * k + 2, :], gb[:, 6 * k:6 * k + 2, :],
                                     gb[:, 6 * k + 3:6 * k + 5, :], ALU.add))
                link(v.tensor_copy(gbs[:, 4 * k + 2:4 * k + 3, :], gb[:, 6 * k + 2:6 * k + 3, :]))
                link(v.tensor_copy(gbs[:, 4 * k + 3:4 * k + 4, :], gb[:, 6 * k + 5:6 * k + 6, :]))
            link(v.tensor_copy(gb1[:, :, :], gbs[:, :, :]))
            link(v.tensor_scalar(bias_w[0:3, :, :], gb1[:, :, :], ident[0:3, 0:1], None, ALU.mult))
            link(v.tensor_tensor(gbr[:, :, :], gbs[:, :, :], gb1[:, :, :], ALU.subtract))
            link(v.tensor_copy(gb1[:, :, :], gbr[:, :, :]))
            flat_b = bias_w[0:3, :, :].rearrange("p g c -> p (g c)")
            flat_1 = gb1[:, :, :].rearrange("p g c -> p (g c)")
            link(v.scalar_tensor_tensor(flat_b, flat_1, ident[0:3, 1:2], flat_b, ALU.mult, ALU.add))
            link(v.tensor_tensor(gbs[:, :, :], gbr[:, :, :], gb1[:, :, :], ALU.subtract))
            link(v.tensor_copy(gb1[:, :, :], gbs[:, :, :]))
            link(v.scalar_tensor_tensor(flat_b, flat_1, ident[0:3, 2:3], flat_b, ALU.mult, ALU.add))
            v.tensor_tensor(wk[:, :], aw1[:, 1, :], aw1[:, 2, :], ALU.subtract)
            v.tensor_tensor(wq[:, :], aw1[:, 0, :], aw1[:, 2, :], ALU.add)
            v.memset(hist_a[:, 0:UN + 1, :], 0.0)
            v.memset(hist_a[:, UN + 1 + T:, :], 0.0)
            v.memset(qh[:, :, :, :], 0.0)
            v.memset(att1[:, :], 0.0)
            v.memset(att2[:, :], 0.0)
            v.memset(feat[2][0:D, :], 0.0)
            v.memset(mv[:, :, :], 0.0)
            for c in range(2):
                v.memset(state[c][:, 0, :], 0.0)
            first_counts = [s_filed]
            for c in range(2):
                first_counts += [s_qh[c], s_a1[c], s_l2[c]]
            for role in gru + aug:
                first_counts += [role.state_ok, role.n_free]
            for k, free in enumerate(first_counts):
                v.memset(v_t[0][:, k:k + 1], 0.0).then_inc(free, 1)
            v.memset(v_t[1][:, :], 0.0).then_inc(s_setup, 1)
            dve.wait_ge(s_hq, 1)
            for c in range(2):
                v.tensor_scalar(hq[c][:, :], bank_2[:, c * D:(c + 1) * D], ab1[:, :], None,
                                ALU.add).then_inc(s_hqs, 1)

            def sums(role, u, t1):
                c, at = role.c, role.order(u) * D
                dve.wait_ge(role.r_ok, t1)
                dve.wait_ge(role.n_mm, t1)
                v.tensor_tensor(m_t[c][:, :], bank_n[c][:, P + at:P + at + D], r_t[c][:, :],
                                ALU.mult).then_inc(role.mul_ok, 1)
                dve.wait_ge(role.mul_ok, t1)
                v.tensor_tensor(bank_n[c][:, at:at + D], m_t[c][:, :], bank_n[c][:, at:at + D],
                                ALU.add).then_inc(role.pre_ok, 1)

            def kept(role, base, u, t1, flip=None):
                c = role.c
                dve.wait_ge(role.z_ok, t1)
                w = z_t[c]
                if role.kind == AUG:
                    at = flip * (UN * D) + u * D
                    a = att_bc[c][:, :, :].rearrange("p b n -> p (b n)")[:, bass.ds(at, D)]
                    v.tensor_tensor(az_t[c][:, :], z_t[c][:, :], a, ALU.mult).then_inc(role.az_ok, 1)
                    dve.wait_ge(role.az_ok, t1)
                    w = az_t[c]
                v.scalar_tensor_tensor(keep_t[c][:, :], w[:, :], -1.0, state_before(role, base, u), ALU.add,
                                       ALU.mult).then_inc(role.keep_ok, 1)

            def new_state(role, base, u, t1):
                c = role.c
                w = az_t[c] if role.kind == AUG else z_t[c]
                dve.wait_ge(role.n_free, t1 + 1)
                v.tensor_tensor(v_t[c][:, :], w[:, :], n_t[c][:, :], ALU.mult).then_inc(role.v_ok, 1)
                dve.wait_ge(role.v_ok, t1)
                dve.wait_ge(role.keep_ok, t1)
                v.tensor_tensor(state_after(role, base, u), v_t[c][:, :], keep_t[c][:, :],
                                ALU.subtract).then_inc(role.state_ok, 1)

            def att_query(c, base, p):
                both = query[c][:, :].rearrange("p (o d) -> p o d", o=1).to_broadcast([P, 2, D])
                v.tensor_tensor(qh[:, p % 2, :, :], both,
                                pair_of_states(c, base, 2 * p).rearrange("p (o d) -> p o d", o=2),
                                ALU.mult).then_inc(s_qh[c], 1)

            def file_scores(c, i):
                dve.wait_ge(s_l3[c], i + 1)
                src = bank_2[:, P:P + 8].rearrange("p (g s) -> p s g", s=2)
                for e in range(2):
                    at = e if c == 0 else 1 - e
                    to = limited(i * UN + at, 0, UN + T + at)
                    last = v.tensor_copy(score[c][:, :, bass.ds(to, 4, step=2)], src[e * D:(e + 1) * D])
                last.then_inc(s_sc[c], 1)

            def att_extras(c, base, i, u):
                back, here = base
                if u == 0:
                    file_scores(c, i)
                if u % 2 and u < UN - 1:
                    dve.wait_ge(s_l1[c], limited(i * 4 + (u // 2 + 1), 1, 1000))
                    att_query(c, back, (u + 1) // 2)
                if u == UN - 1 and here is not None:
                    att_query(c, here, 0)

            def phase1(i):
                base = dve.snap(i * UN) if not isinstance(i, int) else i * UN
                for u in range(UN):
                    t1 = base + (u + 1)
                    sums(gru[0], u, t1)
                    kept(gru[0], base, u, t1)
                    new_state(gru[0], base, u, t1)
                    if u == UN - 1:
                        dve.wait_ge(gru[0].state_ok, base + 3)
                    att_extras(0, (base - UN, base), i, u)

            dve.wait_ge(s_qcopy, 4)
            with dve.Fori(0, BODIES - 1) as i:
                phase1(i)
            phase1(BODIES - 1)
            for u in range(UN):
                att_extras(0, (T - UN, None), BODIES, u)
            file_scores(0, BODIES + 1)

            def softmax(c):
                x = score[c][:, :, 2 * UN:]
                for s in range(2):
                    link(v.tensor_scalar(mask[:, s, :], slot_no[0:D, 0:T], len_f[:, c, s:s + 1], None, ALU.is_lt))
                    link(v.scalar_tensor_tensor(x[:, s, :], x[:, s, :], ab3[:, :], mask[:, s, :], ALU.add, ALU.mult))
                link(v.tensor_scalar(prob[:, :, :], mask[:, :, :], 1.0, MASKED, ALU.subtract, ALU.mult))
                link(v.tensor_tensor(x, x, prob[:, :, :], ALU.add))
                link(v.reduce_max(smx[:, :], x, AX.X))
                v.tensor_scalar(smx[:, :], smx[:, :], -1.0, None, ALU.mult).then_inc(s_max[c], 1)
                dve.wait_ge(s_exp[c], 1)
                link(v.reciprocal(ssum[:, :], ssum[:, :]))
                for s in range(2):
                    last = v.scalar_tensor_tensor(prob[:, s, :], prob[:, s, :], ssum[:, s:s + 1], mask[:, s, :],
                                                  ALU.mult, ALU.mult)
                last.then_inc(s_prob[c], 1)
                dve.wait_ge(s_pt[c], 1)
                v.tensor_copy(prob_t[:, 0:3, :], bank_2[:, 0:3 * D].rearrange("p (k d) -> p k d", k=3))
                left = 2 * T - 3 * P
                v.tensor_copy(prob_t[0:left, 3, :], bank_2[0:left, 3 * D:4 * D]).then_inc(s_ptc[c], 1)

            softmax(0)
            end = dve.snap(limited(n_slots * UN, T + UN, 2 * T))
            v.tensor_copy(blocks(slot_x, end, UN), blocks(hist_a, 0, UN)).then_inc(s_zero_b, 1)

            with dve.Fori(0, n_b) as i:
                base = dve.snap(i * UN)
                top = dve.snap(limited(n_slots * UN - base, UN, 2 * T))
                flip = dve.snap(i & 1)
                dve.wait_ge(s_bc[0], i * 32 + 32)
                for u in range(UN):
                    t1 = dve.snap(base + (u + 1))
                    sums(aug[0], u, t1)
                    kept(aug[0], base, u, t1, flip)
                    sums(gru[1], u, t1)
                    new_state(aug[0], base, u, t1)
                    kept(gru[1], top, u, t1)
                    new_state(gru[1], top, u, t1)
                    if u == UN - 1:
                        dve.wait_ge(gru[1].state_ok, base + 3)
                    att_extras(1, (top + UN, top), i, u)
            top = dve.snap(limited(n_slots * UN - n_b * UN, 0, 2 * T))
            for u in range(UN):
                att_extras(1, (top + UN, None), n_b, u)
            file_scores(1, n_b + 1)
            softmax(1)

            n_rest = dve.snap(sp_max(dve, BODIES - n_b, n_b))
            with dve.Fori(0, n_rest) as i:
                j = dve.snap(n_b + i)
                done = dve.snap(j * UN)
                own = dve.snap(i * UN)
                flip_a = dve.snap(j & 1)
                flip_b = dve.snap(i & 1)
                dve.wait_ge(s_bc[0], j * 32 + 32)
                dve.wait_ge(s_bc[1], i * 32 + 32)
                for u in range(UN):
                    ta = dve.snap(done + (u + 1))
                    tb = dve.snap(own + (u + 1))
                    sums(aug[0], u, ta)
                    kept(aug[0], 0, u, ta, flip_a)
                    sums(aug[1], u, tb)
                    new_state(aug[0], 0, u, ta)
                    kept(aug[1], 0, u, tb, flip_b)
                    new_state(aug[1], 0, u, tb)

            dve.wait_ge(s_spt, 1)
            dve.wait_ge(aug[0].state_ok, (n_b + n_rest) * UN + 1)
            dve.wait_ge(aug[1].state_ok, n_rest * UN + 1)
            for c in range(2):
                for k in range(2):
                    v.tensor_copy(feat[k][:, c * P:(c + 1) * P], bank_1[:, (2 * c + k) * P:(2 * c + k + 1) * P])
                for s in range(2):
                    at = c * P + s * D
                    last = v.tensor_copy(feat[2][0:D, at:at + D], state[c][s * D:(s + 1) * D, 0, :])
            link(last)
            dve.wait_ge(s_feat, 1)
            for k, n in enumerate((P, P, D + ND)):
                link(v.bn_stats(stats[0:n, k, :], feat[k][0:n, :]))
                link(v.bn_aggr(mv[0:n, k, :], stats[0:n, k, :]))
            v.tensor_scalar(mv[:, :, 1], mv[:, :, 1], BN_EPS, None, ALU.add).then_inc(s_var, 1)
            dve.wait_ge(s_std, 1)
            link(v.reciprocal(std[:, :], std[:, :]))
            link(v.tensor_tensor(sc[:, :], std[:, :], par[:, :, 0], ALU.mult))
            for k, n in enumerate((P, P, D + ND)):
                link(v.tensor_scalar(feat[k][0:n, :], feat[k][0:n, :], mv[0:n, k, 0:1], None, ALU.subtract))
                last = v.tensor_scalar(fnorm[k][0:n, :], feat[k][0:n, :], sc[0:n, k:k + 1], par[0:n, k, 1:2],
                                       ALU.mult, ALU.add)
            last.then_inc(s_norm, 1)
            dve.wait_ge(s_y, 1)
            v.tensor_copy(ycol[:, :], bank_z[1][:, 0:2]).then_inc(s_yc, 1)
            dve.wait_ge(s_yo, 1)
            v.tensor_scalar(yrow, bank_2[0:1, 0:B], ob_sb[:, :], None, ALU.add).then_inc(s_yr, 1)


def held(eng, name, value, low, high):
    out = eng.alloc_register(name)
    eng.reg_mov(out, eng.to_reg(value))
    return bass.RuntimeValue.of_register_unchecked(out, min_val=low, max_val=high)


def sp_max(eng, a, b):
    out = eng.alloc_register("larger")
    eng.reg_alu(out, eng.to_reg(a), eng.to_reg(b), ALU.max)
    return bass.RuntimeValue.of_register_unchecked(out, min_val=BODIES // 2, max_val=BODIES)


def sp_min(eng, a, b):
    out = eng.alloc_register("smaller")
    eng.reg_alu(out, eng.to_reg(a), b, ALU.min)
    return bass.RuntimeValue.of_register_unchecked(out, min_val=0, max_val=b)


def _twice(w):
    import numpy as np
    n, m = w.shape
    o = np.zeros((2 * n, 2 * m), w.dtype)
    o[:n, :m] = w
    o[n:, m:] = w
    return o


def kernel(**inputs):
    import numpy as np
    import concourse.bacc as bacc
    from concourse.bass_utils import run_bass_kernel_spmd

    x = {k: np.asarray(v) for k, v in inputs.items()}
    lens = x["r_hist_valid_lens"]
    hist = x["r_hist_item"]
    two = lambda a: np.ascontiguousarray(a.reshape(2, P, -1).transpose(1, 0, 2))
    ints = np.concatenate([hist.reshape(B, -1), x["r_target_item"], x["r_sparse_feature"], lens[:, None],
                           hist[:, ::-1].reshape(B, -1)], axis=1)
    gate_w, gate_b = [], []
    for n in ("gru", "augru"):
        for m in ("ih", "hh"):
            w, b = x[f"L0_rec_{n}_w{m}"], x[f"L0_rec_{n}_b{m}"]
            for g in range(3):
                gate_w.append(_twice(w[g * D:(g + 1) * D].T))
                gate_b.append(np.concatenate([b[g * D:(g + 1) * D]] * 2))
    w1 = x["L0_rec_att_w1"]
    w2 = _twice(x["L0_rec_att_w2"])
    aw2 = np.zeros((P, 4, P), w2.dtype)
    aw3 = np.zeros((P, 8), w2.dtype)
    for g in range(4):
        aw2[:, g, g * 32:(g + 1) * 32] = w2
        for s in range(2):
            aw3[g * 32 + s * ATT2:g * 32 + (s + 1) * ATT2, 2 * g + s] = x["L0_rec_att_w3"][:, 0]
    order = np.r_[0:NSP * E, NSP * E + ND:NSP * E + ND + D, NSP * E:NSP * E + ND]
    pad = lambda a: np.concatenate([a, np.zeros((3 * P - len(a),) + a.shape[1:], a.dtype)])
    three = lambda a: np.ascontiguousarray(pad(a[order]).reshape(3, P, -1).transpose(1, 0, 2))
    arrays = {
        "lens_row": np.broadcast_to(lens[None, :], (P, B)),
        "lens_col": lens.reshape(2, P).T,
        "ints": two(ints),
        "dense": two(x["L0_rec_dense_feature"]),
        "emb": x["L0_rec_emb"],
        "gate_w": np.stack(gate_w, axis=1),
        "gate_b": np.stack([np.stack(gate_b)] * 3),
        "att_w1": np.stack([_twice(w1[k * D:(k + 1) * D]) for k in range(4)], axis=1),
        "att_b1": np.concatenate([x["L0_rec_att_b1"]] * 2)[:, None],
        "att_w2": aw2,
        "att_b2": np.concatenate([x["L0_rec_att_b2"]] * 8)[:, None],
        "att_w3": aw3,
        "att_b3": np.broadcast_to(x["L0_rec_att_b3"][None, :], (D, 1)),
        "bn_par": three(np.stack([x["L0_rec_bn_gamma"], x["L0_rec_bn_beta"]], axis=1)),
        "w1": three(x["L0_rec_dnn_w1"]),
        "b1": x["L0_rec_dnn_b1"].reshape(2, P).T,
        "w2": x["L0_rec_dnn_w2"].reshape(2, P, HID2).transpose(1, 0, 2),
        "b2": x["L0_rec_dnn_b2"][:, None],
        "out_w": x["L0_rec_out_w"],
        "out_b": x["L0_rec_out_b"][None, :],
    }
    arrays = {k: np.ascontiguousarray(a) for k, a in arrays.items()}
    nc = bacc.Bacc("TRN2", target_bir_lowering=False, num_devices=1)
    aps = [nc.dram_tensor(k, a.shape, mybir.dt.from_np(a.dtype), kind="ExternalInput").ap()
           for k, a in arrays.items()]
    out = nc.dram_tensor("out", (1, B), F32, kind="ExternalOutput").ap()
    build_dien(nc, *aps, out)
    got = run_bass_kernel_spmd(nc, [arrays], core_ids=[0])
    return got.results[0]["out"].reshape(B, 1)
```

```python
from contextlib import ExitStack

import concourse.bass as bass
from concourse import mybir

F32 = mybir.dt.float32
BF16 = mybir.dt.bfloat16
I32 = mybir.dt.int32
U32 = mybir.dt.uint32
ALU = mybir.AluOpType
ACT = mybir.ActivationFunctionType
AX = mybir.AxisListType

B, T, E, V = 256, 200, 32, 12500
D = 2 * E
HALF = D
P = 128
NSP = 8
ND = 16
HID1, HID2 = 256, 128
ATT1, ATT2 = 64, 16
BN_EPS = 1e-5
MASKED = 1e9
UN = 8
BODIES = T // UN
SLOTS = 2 * T + UN
MISC = 2 + NSP + 1
IDX = 2 * T
R_, Z_, N_ = 0, 1, 2
GRU, AUG = 0, 1


def build_dien(nc, lens_row, lens_col, ints, dense, emb, gate_w, gate_b, att_w1, att_b1, att_w2, att_b2,
               att_w3, att_b3, bn_par, w1, b1, w2, b2, out_w, out_b, out):
    ctx = ExitStack()
    with ctx:
        def sb(name, shape, dt=F32):
            return ctx.enter_context(nc.sbuf_tensor(name, shape, dt))

        def bank(name):
            return ctx.enter_context(nc.psum_tensor(name, [P, 512], F32))

        def sem(name):
            return ctx.enter_context(nc.semaphore(name))

        slot_x = sb("slot_x", [P, SLOTS, D])
        hist_a = sb("hist_a", [P, UN + 1 + T + 2, D])
        fetched = sb("fetched", [P, UN, D])
        slot_idx = sb("slot_idx", [P, 2 * T + 2, 2], U32)
        stage_idx = sb("stage_idx", [P, UN, 2], U32)
        misc_idx = sb("misc_idx", [P, 2, 2 + NSP], U32)
        spare = [(UN + 1 + 3) * D]

        def early(shape, dt=F32, rows_=P):
            n = 1
            for k in shape:
                n *= k
            words = n if dt != BF16 else n // 2
            flat = hist_a[:, :, :].rearrange("p k d -> p (k d)")[0:rows_, spare[0]:spare[0] + words]
            spare[0] += words
            assert spare[0] <= (UN + 1 + T) * D
            flat = flat if dt == F32 else flat.bitcast(dt)
            return flat if len(shape) == 1 else flat.rearrange("p (a b) -> p a b", a=shape[0])

        raw = early([2, IDX + MISC + IDX], I32)
        rows = early([2, IDX + MISC + IDX])
        wrapped = early([2, IDX + MISC + IDX])
        srt = early([2, IDX + MISC])
        from_b = early([2 * T, 2])
        keep_a = early([T])
        perm = early([2, B])
        slot_no = sb("slot_no", [P, T])
        lrow_i = early([B], I32)
        lcol_i = sb("lcol_i", [P, 2], I32)
        key_row = early([B])
        key_col = sb("key_col", [P, 2])
        iota_b = early([B])
        iota_p = sb("iota_p", [P, 1])
        pos_rank = early([B])
        above = early([B])
        rank = sb("rank", [P, 2])
        perm_t = sb("perm_t", [P, 2, B])
        ends = sb("ends", [P, 2])
        ends_i = sb("ends_i", [1, 2], I32)
        ends_f = sb("ends_f", [1, 2])
        table_call = sb("table_call", [P, 1])
        past_stage = sb("past_stage", [P, 1])
        ident = sb("ident", [P, P])
        ones_b = sb("ones_b", [P, P], BF16)
        gw = sb("gw", [P, 12, P])
        minus_r = sb("minus_r", [P, P])
        gb = early([12, P], rows_=3)
        gbs = early([8, P], rows_=3)
        gbr = early([8, P], rows_=3)
        gb1 = early([8, P], BF16, rows_=3)
        bias_w = sb("bias_w", [P, 8, P], BF16)
        aw1 = sb("aw1", [P, 4, P])
        ab1 = sb("ab1", [P, 1])
        aw2 = sb("aw2", [P, 4, P])
        ab2 = sb("ab2", [P, 1])
        aw3 = sb("aw3", [P, 8])
        ab3 = sb("ab3", [D, 1])
        target = sb("target", [P, 2, D])
        query = [sb(f"query{c}", [P, D]) for c in range(2)]
        hq = [sb(f"hq{c}", [P, D]) for c in range(2)]
        qh = sb("qh", [P, 2, 2, D])
        att1 = sb("att1", [P, P])
        att2 = sb("att2", [P, P])
        score = [sb(f"score{c}", [D, 2, 2 * UN + T]) for c in range(2)]
        len_f = sb("len_f", [D, 2, 2])
        mask = sb("mask", [D, 2, T])
        smx = sb("smx", [D, 2])
        ssum = sb("ssum", [D, 2])
        prob = sb("prob", [D, 2, T])
        prob_t = sb("prob_t", [P, 4, D])
        att_bc = sb("att_bc", [P, 2 * UN, 2 * D])
        r_t = sb("r_t", [P, 2 * D])
        z_t = sb("z_t", [P, 2 * D])
        az_t = sb("az_t", [P, 2 * D])
        m_t = sb("m_t", [P, 2 * D])
        n_t = sb("n_t", [P, 2 * D])
        v_t = sb("v_t", [P, 2 * D])
        keep_t = sb("keep_t", [P, 2 * D])
        state = sb("state", [P, 2, 2 * D])
        sparse = slot_idx[:, :, :].rearrange("p k f -> p (k f)")[:, 0:2 * NSP * E].bitcast(F32)
        sparse = sparse.rearrange("p (c n) -> p c n", c=2)
        dense_sb = sb("dense_sb", [P, 2, ND])
        late = hist_a[:, 0:8 * B // D, :].rearrange("p k d -> p (k d)").rearrange("p (k n) -> p k n", n=B)
        feat = [late[:, 0, :], late[:, 1, :], sb("feat2", [P, B])[:, :]]
        fnorm = [late[:, 2 + k, :] for k in range(3)]
        par = sb("par", [P, 3, 2])
        stats = sb("stats", [P, 3, 6])
        mv = sb("mv", [P, 3, 2])
        std = sb("std", [P, 3])
        sc = sb("sc", [P, 3])
        w1_sb = sb("w1_sb", [P, 3, HID1])
        b1_sb = sb("b1_sb", [P, 2])
        w2_sb = sb("w2_sb", [P, 2, HID2])
        b2_sb = sb("b2_sb", [P, 1])
        ow_sb = sb("ow_sb", [P, 1])
        ob_sb = sb("ob_sb", [1, 1])
        h1 = late[:, 5:7, :]
        h2 = late[:, 7, :]
        ycol = sb("ycol", [P, 2])
        yrow = late[0:1, 0, :]

        bank_r = [bank(f"bank_r{q}") for q in range(2)]
        bank_z = [bank(f"bank_z{q}") for q in range(2)]
        bank_n = [bank(f"bank_n{q}") for q in range(2)]
        turn_bank = [bank_r[1], bank_z[1]]
        bank_1 = bank("bank_1")
        bank_2 = bank("bank_2")

        att_dram = nc.dram_tensor("att_dram", [2, 2, 2 * T + UN, D], F32, kind="Internal").ap()

        s_ints = sem("s_ints")
        s_weights = sem("s_weights")
        s_dnn = sem("s_dnn")
        s_consts = sem("s_consts")
        s_dve = sem("s_dve")
        s_act = sem("s_act")
        s_perm = sem("s_perm")
        s_sorted = sem("s_sorted")
        s_ends = sem("s_ends")
        s_bounds = sem("s_bounds")
        s_table = sem("s_table")
        s_stage = sem("s_stage")
        s_pair = [sem(f"s_pair{p}") for p in range(4)]
        s_target = sem("s_target")
        s_sparse = sem("s_sparse")
        s_turned = sem("s_turned")
        s_filed = sem("s_filed")
        s_permt = sem("s_permt")
        s_permc = sem("s_permc")
        s_query = sem("s_query")
        s_qcopy = sem("s_qcopy")
        s_hq = sem("s_hq")
        s_hqs = sem("s_hqs")
        s_setup = sem("s_setup")
        s_zero_b = sem("s_zero_b")
        s_ztail = sem("s_ztail")
        s_qh = [sem(f"s_qh{c}") for c in range(2)]
        s_l1 = [sem(f"s_l1_{c}") for c in range(2)]
        s_l1q = [sem(f"s_l1q_{c}") for c in range(2)]
        s_a1 = [sem(f"s_a1_{c}") for c in range(2)]
        s_l2 = [sem(f"s_l2_{c}") for c in range(2)]
        s_a2 = [sem(f"s_a2_{c}") for c in range(2)]
        s_l3 = [sem(f"s_l3_{c}") for c in range(2)]
        s_sc = [sem(f"s_sc{c}") for c in range(2)]
        s_max = [sem(f"s_max{c}") for c in range(2)]
        s_exp = [sem(f"s_exp{c}") for c in range(2)]
        s_prob = [sem(f"s_prob{c}") for c in range(2)]
        s_pt = [sem(f"s_pt{c}") for c in range(2)]
        s_ptc = [sem(f"s_ptc{c}") for c in range(2)]
        s_pd = [sem(f"s_pd{c}") for c in range(2)]
        s_hist = sem("s_hist")
        s_stored = sem("s_stored")
        s_bc = sem("s_bc")
        s_bc_both = sem("s_bc_both")
        s_spt = sem("s_spt")
        s_feat = sem("s_feat")
        s_dt = sem("s_dt")
        s_norm = sem("s_norm")
        s_var = sem("s_var")
        s_std = sem("s_std")
        s_h1 = sem("s_h1")
        s_h1c = sem("s_h1c")
        s_h2 = sem("s_h2")
        s_h2c = sem("s_h2c")
        s_y = sem("s_y")
        s_yc = sem("s_yc")
        s_yo = sem("s_yo")
        s_yr = sem("s_yr")
        s_out = sem("s_out")

        class Steps:

            def __init__(self, name):
                self.state_ok = sem(f"{name}_state_ok")
                self.r_mm = sem(f"{name}_r_mm")
                self.z_mm = sem(f"{name}_z_mm")
                self.n_mm = sem(f"{name}_n_mm")
                self.r_ok = sem(f"{name}_r_ok")
                self.z_ok = sem(f"{name}_z_ok")
                self.pre_ok = sem(f"{name}_pre_ok")
                self.n_ok = sem(f"{name}_n_ok")
                self.mul_ok = sem(f"{name}_mul_ok")
                self.az_ok = sem(f"{name}_az_ok")
                self.keep_ok = sem(f"{name}_keep_ok")
                self.v_ok = sem(f"{name}_v_ok")

        alone = Steps("alone")
        aug_a = Steps("aug_a")
        gru_b = Steps("gru_b")
        both = Steps("both")

        def cols(tile, pair, off=0, u=0):
            if not pair:
                return tile[:, off + u % 2 * D:off + (u % 2 + 1) * D]
            four = tile[:, off:off + 4 * D].rearrange("p (k d) -> p k d", d=D)
            return four[:, 0:4:3, :] if u % 2 == 0 else four[:, 1:3, :]

        def chain_cols(c, off, u):
            at = off + (u % 2 if c == 0 else 1 - u % 2) * D
            return slice(at, at + D)

        def own(tile, pair):
            return tile[:, :].rearrange("p (c d) -> p c d", d=D) if pair else tile[:, 0:D]

        def blocks(tile, first, n):
            flat = tile[:, :, :].rearrange("p k d -> p (k d)")
            return flat[:, bass.ds(limited(first * D, 0, flat.shape[1] - n * D), n * D)]

        def b_slot(top, u):
            return top - 1 - u

        def pair_of_states(c, base, u):
            return blocks(hist_a, base + (UN + 1 + u), 2) if c == 0 else blocks(slot_x, b_slot(base, u + 1), 2)

        def pair_of_inputs(c, base, u):
            return blocks(slot_x, base + u, 2) if c == 0 else blocks(slot_x, b_slot(base, u + 1), 2)

        def bounds(eng):
            eng.wait_ge(s_bounds, 1)
            slots = eng.value_load(ends_i[0:1, 0:1], min_val=T + UN, max_val=2 * T)
            steps = eng.value_load(ends_i[0:1, 1:2], min_val=1, max_val=T)
            n_slots = eng.snap((slots + (UN - 1)) >> 3)
            n_b = eng.snap((steps + (UN - 1)) >> 3)
            return n_slots, n_b

        def limited(value, low, high):
            return value if isinstance(value, int) else value.with_bounds(min_val=low, max_val=high)

        block = ctx.enter_context(nc.Block())

        @block.sync
        def _(sp):
            sp.dma_start(lrow_i, lens_row).then_inc(s_ints, 16)
            sp.dma_start(lcol_i[:, :], lens_col).then_inc(s_ints, 16)
            sp.dma_start(raw[:, :, :], ints).then_inc(s_ints, 16)
            sp.dma_start(gw[:, :, :], gate_w).then_inc(s_weights, 16)
            sp.dma_start(gb[:, :, :], gate_b).then_inc(s_weights, 16)
            sp.dma_start(aw1[:, :, :], att_w1).then_inc(s_weights, 16)
            sp.dma_start(ab1[:, :], att_b1).then_inc(s_weights, 16)
            sp.dma_start(aw2[:, :, :], att_w2).then_inc(s_weights, 16)
            sp.dma_start(ab2[:, :], att_b2).then_inc(s_weights, 16)
            sp.dma_start(aw3[:, :], att_w3).then_inc(s_weights, 16)
            sp.dma_start(ab3[:, :], att_b3).then_inc(s_weights, 16)
            sp.dma_start(dense_sb[:, :, :], dense).then_inc(s_dnn, 16)
            sp.dma_start(par[:, :, :], bn_par).then_inc(s_dnn, 16)
            sp.dma_start(w1_sb[:, :, :], w1).then_inc(s_dnn, 16)
            sp.dma_start(b1_sb[:, :], b1).then_inc(s_dnn, 16)
            sp.dma_start(w2_sb[:, :, :], w2).then_inc(s_dnn, 16)
            sp.dma_start(b2_sb[:, :], b2).then_inc(s_dnn, 16)
            sp.dma_start(ow_sb[:, :], out_w).then_inc(s_dnn, 16)
            sp.dma_start(ob_sb[:, :], out_b).then_inc(s_dnn, 16)
            sp.wait_ge(s_setup, 1)
            tail = T + UN
            for c in range(2):
                for s in range(2):
                    sp.dma_start(att_dram[c, s, T:, :].rearrange("(a b) d -> a (b d)", a=tail // UN),
                                 hist_a[0:tail // UN, 0:UN, :].rearrange("p k d -> p (k d)")).then_inc(s_ztail, 16)
            sp.wait_ge(s_ztail, 64)

            def save_att(c):
                flat = att_dram[c, :, 0:T, :]
                sp.wait_ge(s_ptc[c], 1)
                n = 0
                for k in range(4):
                    row, left = k * P, min(P, 2 * T - k * P)
                    while left:
                        s, t0 = row // T, row % T
                        m = min(left, T - t0)
                        at = row - k * P
                        sp.dma_start(flat[s, t0:t0 + m, :], prob_t[at:at + m, k, :]).then_inc(s_pd[c], 16)
                        row, left, n = row + m, left - m, n + 1
                sp.wait_ge(s_pd[c], 16 * n)

            def load_att(c, first, at, landed):
                for s in range(2):
                    src = att_dram[c, s, bass.ds(first, UN), :].rearrange("(a t) d -> a t d", a=1)
                    sp.dma_start(att_bc[s * D:(s + 1) * D, bass.ds(at, UN), c * D:(c + 1) * D],
                                 src.to_broadcast([D, UN, D])).then_inc(landed, 16)

            n_slots, n_b = bounds(sp)
            n_rest = sp.snap(sp_max(sp, BODIES - n_b, n_b))
            save_att(0)
            load_att(0, 0, 0, s_bc)
            with sp.Fori(0, n_b) as i:
                first = held(sp, "first", (i + 1) * UN, UN, T + UN)
                at = held(sp, "at", ((i + 1) & 1) * UN, 0, UN)
                sp.wait_ge(aug_a.az_ok, i * UN + 1)
                sp.wait_ge(s_bc, i * 32 + 32)
                load_att(0, first, at, s_bc)
            save_att(1)
            first = held(sp, "first_a", n_b * UN, UN, T)
            sp.wait_ge(aug_a.az_ok, n_b * UN)
            sp.wait_ge(s_bc, n_b * 32 + 32)
            load_att(0, first, 0, s_bc_both)
            load_att(1, 0, 0, s_bc_both)
            with sp.Fori(0, n_rest) as i:
                first_a = held(sp, "next_a", (n_b + i + 1) * UN, UN, 2 * T)
                first_b = held(sp, "next_b", (i + 1) * UN, UN, T)
                at = held(sp, "next_at", ((i + 1) & 1) * UN, 0, UN)
                sp.wait_ge(both.az_ok, i * UN + 1)
                sp.wait_ge(s_bc_both, i * 64 + 64)
                load_att(0, first_a, at, s_bc_both)
                load_att(1, first_b, at, s_bc_both)
            sp.wait_ge(s_bc_both, n_rest * 64 + 64)
            sp.wait_ge(s_yr, 1)
            sp.dma_start(out, yrow).then_inc(s_out, 16)
            sp.wait_ge(s_out, 16)

        @block.gpsimd
        def _(pool):
            nc.gpsimd.memset(ident[:, :], 0.0).then_inc(s_consts, 1)
            pool.wait_ge(s_consts, 1)
            nc.gpsimd.affine_select(out=ident[:, :], in_=ident[:, :], compare_op=ALU.not_equal, fill=1.0, base=0,
                                    pattern=[[-1, P]], channel_multiplier=1).then_inc(s_consts, 1)
            nc.gpsimd.iota(iota_b, pattern=[[1, B]], base=0, channel_multiplier=0,
                           allow_small_or_imprecise_dtypes=True).then_inc(s_consts, 1)
            nc.gpsimd.iota(iota_p[:, :], pattern=[[1, 1]], base=0, channel_multiplier=1,
                           allow_small_or_imprecise_dtypes=True).then_inc(s_consts, 1)
            nc.gpsimd.iota(pos_rank[:, 0:P], pattern=[[1, P]], base=0, channel_multiplier=0,
                           allow_small_or_imprecise_dtypes=True).then_inc(s_consts, 1)
            nc.gpsimd.iota(pos_rank[:, P:B], pattern=[[-1, P]], base=B - 1, channel_multiplier=0,
                           allow_small_or_imprecise_dtypes=True).then_inc(s_consts, 1)
            nc.gpsimd.iota(slot_no[:, :], pattern=[[1, T]], base=0, channel_multiplier=0,
                           allow_small_or_imprecise_dtypes=True).then_inc(s_consts, 1)

            def gather(dst, idx):
                return nc.gpsimd.indirect_dma_start(
                    out=dst, out_offset=None, in_=emb[:, :],
                    in_offset=bass.IndirectOffsetOnAxis(ap=idx, axis=0))

            flat_idx = slot_idx[:, :, :].rearrange("p k f -> p (k f)")

            staged = stage_idx[:, :, :].rearrange("p k f -> p (k f)")

            def stage(i, p):
                nc.gpsimd.tensor_copy(staged[:, 4 * p:4 * p + 4],
                                      flat_idx[:, bass.ds(i * (2 * UN) + 4 * p, 4)]).then_inc(s_stage, 1)

            def fetch_pair(i, p, first):
                nxt, j = (p + 1) % 4, i + (p + 1) // 4
                if not first:
                    pool.wait_ge(s_turned, i * 4 + (p - 3))
                if not first or p == 3:
                    pool.wait_ge(s_pair[nxt], j * 64)
                pool.wait_ge(s_stage, i * 4 + (p + 1))
                stage(j, nxt)
                for slot in (2 * p, 2 * p + 1):
                    for f in range(2):
                        gather(fetched[:, slot, f * E:(f + 1) * E],
                               stage_idx[:, slot, f:f + 1]).then_inc(s_pair[p], 16)

            pool.wait_ge(s_table, 1)
            stage(0, 0)
            for p in range(4):
                fetch_pair(0, p, True)
            for c in range(2):
                for f in range(2):
                    gather(target[:, c, f * E:(f + 1) * E], misc_idx[:, c, f:f + 1]).then_inc(s_target, 16)
            n_slots, n_b = bounds(pool)
            with pool.Fori(1, n_slots) as i:
                i = pool.snap(limited(i, 1, 2 * BODIES - 1))
                for p in range(4):
                    fetch_pair(i, p, False)
            with pool.Fori(0, n_b) as i:
                base = pool.snap(i * UN)
                top = pool.snap(limited(n_slots * UN - base, UN, 2 * T))
                for u in range(UN):
                    pool.wait_ge(gru_b.state_ok, base + (u + 2))
                    nc.gpsimd.tensor_copy(blocks(slot_x, b_slot(top, u), 1),
                                          state[:, (u + 1) % 2, D:2 * D]).then_inc(s_stored, 1)
            pool.wait_ge(s_stage, n_slots * 4 + 1)
            nc.gpsimd.tensor_tensor(past_stage[:, :], iota_p[:, :], iota_p[:, :], ALU.add)
            for c in range(2):
                for f in range(NSP):
                    gather(sparse[:, c, f * E:(f + 1) * E], misc_idx[:, c, 2 + f:3 + f]).then_inc(s_sparse, 16)

        @block.tensor
        def _(pe):
            mm = nc.tensor.matmul

            pe.wait_ge(s_perm, 1)
            for c in range(2):
                for k in range(2):
                    last = mm(bank_r[c][:, 0:IDX + MISC], perm[:, k, c * P:(c + 1) * P],
                              wrapped[:, k, c * IDX:c * IDX + IDX + MISC], start=k == 0, stop=k == 1)
                last.then_inc(s_sorted, 1)
            pe.wait_ge(s_ends, 1)
            for k in range(2):
                last = mm(bank_z[0][0:1, k * P:(k + 1) * P], ends[:, k:k + 1], ident[:, :], start=True, stop=True)
            last.then_inc(s_sorted, 1)
            for c in range(2):
                for k in range(2):
                    last = nc.tensor.transpose(bank_n[c][:, k * P:(k + 1) * P], perm[:, k, c * P:(c + 1) * P],
                                               ident[:, :])
            last.then_inc(s_permt, 1)
            pe.wait_ge(s_dnn, 128)
            for k in range(2):
                last = mm(bank_2[0:ND, 256:512], dense_sb[:, k, :], perm[:, k, :], start=k == 0, stop=k == 1)
            last.then_inc(s_dt, 1)

            def turn(m, k, q):
                pe.wait_ge(s_pair[2 * k + q], m * 64 + 64)
                if q == 0 and not (isinstance(m, int) and m == 0):
                    pe.wait_ge(s_filed, m * 8 + (4 * k - 3))
                pair = fetched[:, 4 * k + 2 * q:4 * k + 2 * q + 2, :].rearrange("p k d -> p (k d)")
                done = nc.tensor.transpose(turn_bank[k][:, P * q:P * (q + 1)], pair, ident[:, :])
                done.then_inc(s_turned, 1)

            def seed(to, at, bias, w, x):
                mm(to[:, at:at + P], bias_w[:, bias, :], ones_b[:, :], start=at == 0, stop=w is None,
                   skip_group_check=True)
                if w is not None:
                    mm(to[:, at:at + P], gw[:, w, :], x, start=False, stop=True, skip_group_check=True)

            def seed_rz(q, kind, at, x):
                seed(bank_r[q], at, 4 * kind + R_, 6 * kind + R_, x)
                seed(bank_z[q], at, 4 * kind + Z_, 6 * kind + Z_, x)

            def seed_n(q, kind, at, x):
                seed(bank_n[q], at, 4 * kind + 2, 6 * kind + N_, x)
                seed(bank_n[q], 4 * D + at, 4 * kind + 3, None, None)

            def seed_all(q, kind, at, x):
                seed_rz(q, kind, at, x)
                seed_n(q, kind, at, x)

            def add_state(dst, w, h):
                return mm(dst, w, h, start=False, stop=True, skip_group_check=True)

            def att_layer1(c, base, p, n1):
                pe.wait_ge(s_qh[c], n1)
                pe.wait_ge(s_a1[c], n1)
                to = bank_1[:, 0:P]
                mm(to, aw1[:, 1, :], pair_of_states(c, base, 2 * p), start=True, stop=False)
                mm(to, aw1[:, 3, :], qh[:, p % 2, :, :], start=False, stop=True).then_inc(s_l1[c], 1)

            def att_layer2(c, p, n1, body1):
                pe.wait_ge(s_a1[c], n1 + 1)
                if p == 0:
                    pe.wait_ge(s_sc[c], body1)
                mm(bank_2[:, 0:P], aw2[:, p, :], att1[:, :], start=p == 0, stop=p == 3,
                   skip_group_check=True).then_inc(s_l2[c], 1)

            def att_layer3(c, i):
                pe.wait_ge(s_a2[c], i + 1)
                mm(bank_2[:, P:P + 8], att2[:, :], aw3[:, :], start=True, stop=True,
                   skip_group_check=True).then_inc(s_l3[c], 1)

            def att_extras(c, base, i, u):
                if u == 0:
                    att_layer3(c, i)
                if u % 2 == 0:
                    att_layer1(c, base, u // 2, i * 4 + (u // 2 + 1))
                else:
                    att_layer2(c, u // 2, i * 4 + (u // 2 + 1), i + 1)

            pe.wait_ge(s_setup, 1)
            pe.wait_ge(s_permc, 1)
            for k in range(2):
                for q in range(2):
                    turn(0, k, q)
            pe.wait_ge(s_filed, 5)
            seed_rz(0, GRU, 0, pair_of_inputs(0, 0, 0))
            seed_n(0, GRU, 0, pair_of_inputs(0, 0, 0))
            pe.wait_ge(s_target, 64)
            nc.tensor.transpose(bank_1[:, 0:P], target[:, :, :].rearrange("p c d -> p (c d)"),
                                ident[:, :]).then_inc(s_query, 1)
            pe.wait_ge(s_qcopy, 4)
            pe.wait_ge(s_feat, 1)
            for c in range(2):
                last = mm(bank_2[:, c * D:(c + 1) * D], aw1[:, 0, :], query[c][:, :], start=True, stop=True)
            last.then_inc(s_hq, 1)
            pe.wait_ge(s_hqs, 2)
            n_slots, n_b = bounds(pe)

            def phase1(i, turning):
                base = pe.snap(i * UN) if not isinstance(i, int) else i * UN
                for u in range(UN):
                    q, t1 = u // 2 % 2, base + (u + 1)
                    pe.wait_ge(alone.state_ok, t1)
                    h = state[:, u % 2, 0:D]
                    add_state(cols(bank_r[0], False, 0, u), gw[:, 3 + R_, :], h).then_inc(alone.r_mm, 1)
                    add_state(cols(bank_n[q], False, 4 * D, u), gw[:, 3 + N_, :], h).then_inc(alone.n_mm, 1)
                    add_state(cols(bank_z[0], False, 0, u), gw[:, 3 + Z_, :], h).then_inc(alone.z_mm, 1)
                    if turning and u % 2:
                        turn(i + 1, u // 4, u // 2 % 2)
                    if u == 0:
                        pe.wait_ge(s_hist, base + 1)
                    att_extras(0, base - UN, i, u)
                    if u >= UN - 2 and not turning:
                        continue
                    if u % 2 == 0:
                        if u == 2:
                            pe.wait_ge(s_filed, i * 8 + 9)
                        if u == UN - 2:
                            pe.wait_ge(s_filed, i * 8 + 13)
                        seed_n(1 - q, GRU, 0, pair_of_inputs(0, base, u + 2))
                    else:
                        pe.wait_ge(alone.r_ok, t1)
                        pe.wait_ge(alone.z_ok, t1)
                        seed_rz(0, GRU, 0, pair_of_inputs(0, base, u + 1))

            with pe.Fori(0, BODIES - 1) as i:
                phase1(i, True)
            phase1(BODIES - 1, False)
            with pe.Fori(BODIES, n_slots) as m:
                m = pe.snap(limited(m, BODIES, 2 * BODIES - 1))
                for k in range(2):
                    for q in range(2):
                        turn(m, k, q)
            pe.wait_ge(s_hist, T + 1)
            for u in range(UN):
                att_extras(0, BODIES * UN - UN, BODIES, u)
            att_layer3(0, BODIES + 1)

            def att_turn(c):
                pe.wait_ge(s_prob[c], 1)
                flat = prob[:, :, :].rearrange("p s t -> p (s t)")
                for k in range(4):
                    n = min(P, 2 * T - k * P)
                    last = nc.tensor.transpose(bank_2[0:n, k * D:(k + 1) * D], flat[:, k * P:k * P + n],
                                               ident[0:D, 0:D])
                last.then_inc(s_pt[c], 1)

            att_turn(0)
            pe.wait_ge(s_ptc[0], 1)

            pe.wait_ge(s_filed, n_slots * 8 + 1)

            first_top = limited(n_slots * UN, T + UN, 2 * T)
            seed_all(0, AUG, 0, pair_of_states(0, 0, 0))
            seed_all(1, GRU, 0, pair_of_inputs(1, first_top, 0))

            def chain_step(s, c, kind, u, t1, h):
                pe.wait_ge(s.state_ok, t1)
                for to, off, g, done in ((bank_r, 0, R_, s.r_mm), (bank_n, 4 * D, N_, s.n_mm), (bank_z, 0, Z_, s.z_mm)):
                    add_state(to[c][:, chain_cols(c, off, u)], gw[:, 6 * kind + 3 + g, :], h).then_inc(done, 1)

            def chain_seed(s, c, kind, t1, x):
                pe.wait_ge(s.r_ok, t1)
                pe.wait_ge(s.z_ok, t1)
                seed_rz(c, kind, 0, x)
                pe.wait_ge(s.n_ok, t1)
                seed_n(c, kind, 0, x)

            def phase2(i, first):
                base = pe.snap(i * UN)
                top = pe.snap(limited(n_slots * UN - base, UN, 2 * T))
                for u in range(UN):
                    chain_step(aug_a, 0, AUG, u, base + (u + 1), state[:, u % 2, 0:D])
                    if u % 2 == 0 and not (first and u == 0):
                        chain_seed(gru_b, 1, GRU, base + u, pair_of_inputs(1, top, u))
                    if u % 2:
                        att_layer2(1, u // 2, i * 4 + (u // 2 + 1), i + 1)
                    chain_step(gru_b, 1, GRU, u, base + (u + 1), state[:, u % 2, D:2 * D])
                    if u == 0:
                        pe.wait_ge(s_stored, base + 2)
                        att_layer3(1, i)
                    if u % 2:
                        chain_seed(aug_a, 0, AUG, base + (u + 1), pair_of_states(0, base, u + 1))
                    else:
                        att_layer1(1, top + UN, u // 2, i * 4 + (u // 2 + 1))

            pe.wait_ge(s_zero_b, 1)
            phase2(0, True)
            with pe.Fori(1, n_b) as i:
                phase2(pe.snap(limited(i, 1, BODIES - 1)), False)
            top = pe.snap(limited(n_slots * UN - n_b * UN, 0, 2 * T))
            pe.wait_ge(s_stored, n_b * UN + 2)
            for u in range(UN):
                att_extras(1, top + UN, n_b, u)
            att_layer3(1, n_b + 1)

            done = pe.snap(limited(n_b * UN, UN, T))
            first = pe.snap(sp_min(pe, "first_pair", done, T - UN))
            seed_all(0, AUG, 0, pair_of_states(0, first, 0))
            seed_all(0, AUG, P, pair_of_inputs(1, first_top, 0))
            att_turn(1)
            n_rest = pe.snap(sp_max(pe, BODIES - n_b, n_b))
            with pe.Fori(0, n_rest) as i:
                base = pe.snap(sp_min(pe, "pair", (n_b + i) * UN, T - UN))
                begun = pe.snap(i * UN)
                top = pe.snap(limited(n_slots * UN - begun, UN, 2 * T))
                for u in range(UN):
                    q, t1 = u // 2 % 2, begun + (u + 1)
                    pe.wait_ge(both.keep_ok, t1)
                    add_state(cols(bank_r[q], True, 0, u), minus_r[:, :], keep_t[:, :])
                    pe.wait_ge(both.v_ok, t1)
                    add_state(cols(bank_r[q], True, 0, u), gw[:, 9 + R_, :], v_t[:, :]).then_inc(both.r_mm, 1)
                    pe.wait_ge(both.state_ok, t1)
                    h = state[:, u % 2, :]
                    add_state(cols(bank_n[q], True, 4 * D, u), gw[:, 9 + N_, :], h).then_inc(both.n_mm, 1)
                    add_state(cols(bank_z[q], True, 0, u), gw[:, 9 + Z_, :], h).then_inc(both.z_mm, 1)
                    if u % 2 == 0:
                        seed_all(1 - q, AUG, 0, pair_of_states(0, base, u + 2))
                    else:
                        seed_all(1 - q, AUG, P, pair_of_inputs(1, top, u + 1))

            pe.wait_ge(s_sparse, 16 * 2 * NSP)
            pe.wait_ge(s_ptc[1], 1)
            for c in range(2):
                for k in range(2):
                    last = nc.tensor.transpose(bank_1[:, (2 * c + k) * P:(2 * c + k + 1) * P],
                                               sparse[:, c, k * P:(k + 1) * P], ident[:, :])
            last.then_inc(s_spt, 1)
            pe.wait_ge(s_norm, 1)
            for m in range(2):
                for k, rows_ in enumerate((P, P, D + ND)):
                    last = mm(bank_r[m][:, 0:B], w1_sb[0:rows_, k, m * P:(m + 1) * P], fnorm[k][0:rows_, :],
                              start=k == 0, stop=k == 2)
            last.then_inc(s_h1, 1)
            pe.wait_ge(s_h1c, 2)
            for m in range(2):
                last = mm(bank_z[0][:, 0:B], w2_sb[:, m, :], h1[:, m, :], start=m == 0, stop=m == 1)
            last.then_inc(s_h2, 1)
            pe.wait_ge(s_h2c, 1)
            for c in range(2):
                last = mm(bank_z[1][:, c:c + 1], h2[:, c * P:(c + 1) * P], ow_sb[:, :], start=True, stop=True)
            last.then_inc(s_y, 1)
            pe.wait_ge(s_yc, 1)
            for c in range(2):
                last = mm(bank_2[0:1, 0:B], ycol[:, c:c + 1], perm_t[:, c, :], start=c == 0, stop=c == 1)
            last.then_inc(s_yo, 1)

        @block.scalar
        def _(act):
            A = nc.scalar.activation

            def file_piece(m, k, n):
                e, s = n // 2, n % 2
                if n == 0:
                    act.wait_ge(s_turned, m * 4 + (2 * k + 2))
                src = turn_bank[k][e * D:(e + 1) * D, 0:2 * P].rearrange("p (q c) -> p q c", q=2)[:, :, s * D:(s + 1) * D]
                dst = slot_x[s * D:(s + 1) * D, bass.ds(m * UN + (4 * k + e), 2, step=2), :]
                A(dst, src, ACT.Copy).then_inc(s_filed, 1)

            def sig_r(s, bank_, u, pair, t1):
                act.wait_ge(s.r_mm, t1)
                A(own(r_t, pair), cols(bank_, pair, 0, u), ACT.Sigmoid).then_inc(s.r_ok, 1)

            def sig_z(s, bank_, u, pair, t1):
                act.wait_ge(s.z_mm, t1)
                A(own(z_t, pair), cols(bank_, pair, 0, u), ACT.Sigmoid).then_inc(s.z_ok, 1)

            def tanh(s, bank_, u, pair, t1):
                act.wait_ge(s.pre_ok, t1)
                A(own(n_t, pair), cols(bank_, pair, 0, u), ACT.Tanh).then_inc(s.n_ok, 1)

            def att_relu1(c, i, p):
                n1 = i * 4 + (p + 1)
                act.wait_ge(s_l1q[c], n1)
                act.wait_ge(s_l2[c], n1)
                A(att1[:, :], bank_1[:, 0:P], ACT.Relu).then_inc(s_a1[c], 1)

            def att_relu2(c, i):
                act.wait_ge(s_l2[c], i * 4 + 5)
                A(att2[:, :], bank_2[:, 0:P], ACT.Relu, bias=ab2[:, :]).then_inc(s_a2[c], 1)

            def load_gate_functions():
                A(table_call[:, :], iota_p[:, :], ACT.Sigmoid)

            act.wait_ge(s_consts, 7)
            load_gate_functions()
            act.wait_ge(s_permt, 1)
            for c in range(2):
                last = A(perm_t[:, c, :], bank_n[c][:, 0:B], ACT.Copy)
            last.then_inc(s_permc, 1)
            act.wait_ge(s_dt, 1)
            A(feat[2][D:D + ND, :], bank_2[0:ND, 256:512], ACT.Copy).then_inc(s_feat, 1)
            act.wait_ge(s_setup, 1)
            for n in range(4):
                file_piece(0, 0, n)
            act.wait_ge(s_query, 1)
            for c in range(2):
                for s in range(2):
                    A(query[c][s * D:(s + 1) * D, :], bank_1[c * D:(c + 1) * D, s * D:(s + 1) * D],
                      ACT.Copy).then_inc(s_qcopy, 1)
            n_slots, n_b = bounds(act)

            def phase1(i, turning):
                base = act.snap(i * UN) if not isinstance(i, int) else i * UN
                for u in range(UN):
                    q, t1 = u // 2 % 2, base + (u + 1)
                    sig_r(alone, bank_r[0], u, False, t1)
                    if u % 2:
                        att_relu1(0, i, u // 2)
                    sig_z(alone, bank_z[0], u, False, t1)
                    tanh(alone, bank_n[q], u, False, t1)
                    if u == UN - 1:
                        att_relu2(0, i)
                    if u in (0, 1):
                        file_piece(i, 1, 2 * u)
                        file_piece(i, 1, 2 * u + 1)
                    if turning and u in (4, 5):
                        file_piece(i + 1, 0, 2 * (u - 4))
                        file_piece(i + 1, 0, 2 * (u - 4) + 1)

            with act.Fori(0, BODIES - 1) as i:
                phase1(i, True)
            phase1(BODIES - 1, False)
            with act.Fori(BODIES, n_slots) as m:
                m = act.snap(limited(m, BODIES, 2 * BODIES - 1))
                for k in range(2):
                    for n in range(4):
                        file_piece(m, k, n)
            for p in range(4):
                att_relu1(0, BODIES, p)
            att_relu2(0, BODIES)

            def exps(c):
                act.wait_ge(s_max[c], 1)
                for s in range(2):
                    last = A(prob[:, s, :], score[c][:, s, 2 * UN:], ACT.Exp, bias=smx[:, s:s + 1],
                             accum_out=ssum[:, s:s + 1])
                last.then_inc(s_exp[c], 1)
                load_gate_functions()

            exps(0)
            with act.Fori(0, n_b) as i:
                base = act.snap(i * UN)
                for u in range(UN):
                    for c, s in ((0, aug_a), (1, gru_b)):
                        mine, t1 = slice(c * D, (c + 1) * D), base + (u + 1)
                        at = chain_cols(c, 0, u)
                        act.wait_ge(s.r_mm, t1)
                        A(r_t[:, mine], bank_r[c][:, at], ACT.Sigmoid).then_inc(s.r_ok, 1)
                        act.wait_ge(s.z_mm, t1)
                        A(z_t[:, mine], bank_z[c][:, at], ACT.Sigmoid).then_inc(s.z_ok, 1)
                        act.wait_ge(s.pre_ok, t1)
                        A(n_t[:, mine], bank_n[c][:, at], ACT.Tanh).then_inc(s.n_ok, 1)
                    if u % 2 == 0:
                        att_relu1(1, i, u // 2)
                    if u == UN - 1:
                        att_relu2(1, i)
            for p in range(4):
                att_relu1(1, n_b, p)
            att_relu2(1, n_b)
            exps(1)
            n_rest = act.snap(sp_max(act, BODIES - n_b, n_b))
            with act.Fori(0, n_rest) as i:
                begun = act.snap(i * UN)
                for u in range(UN):
                    q, t1 = u // 2 % 2, begun + (u + 1)
                    sig_r(both, bank_r[q], u, True, t1)
                    sig_z(both, bank_z[q], u, True, t1)
                    tanh(both, bank_n[q], u, True, t1)
            act.wait_ge(s_var, 1)
            A(std[:, :], mv[:, :, 1], ACT.Sqrt).then_inc(s_std, 1)
            act.wait_ge(s_h1, 1)
            for m in range(2):
                A(h1[:, m, :], bank_r[m][:, 0:B], ACT.Relu, bias=b1_sb[:, m:m + 1]).then_inc(s_h1c, 1)
            act.wait_ge(s_h2, 1)
            A(h2[:, :], bank_z[0][:, 0:B], ACT.Relu, bias=b2_sb[:, :]).then_inc(s_h2c, 1)

        @block.vector
        def _(dve):
            v = nc.vector
            count = [0]

            def link(ins):
                count[0] += 1
                ins.then_inc(s_dve, 1)
                dve.wait_ge(s_dve, count[0])

            dve.wait_ge(s_ints, 48)
            dve.wait_ge(s_consts, 7)
            link(v.tensor_scalar(lrow_i, lrow_i, 0.0, float(T), ALU.max, ALU.min))
            link(v.tensor_scalar(lcol_i[:, :], lcol_i[:, :], 0.0, float(T), ALU.max, ALU.min))
            link(v.scalar_tensor_tensor(key_row, lrow_i, float(B), iota_b, ALU.mult, ALU.add))
            link(v.tensor_scalar(key_col[:, 0:1], iota_p[:, :], 0.0, None, ALU.add))
            link(v.tensor_scalar(key_col[:, 1:2], iota_p[:, :], float(P), None, ALU.add))
            link(v.scalar_tensor_tensor(key_col[:, :], lcol_i[:, :], float(B), key_col[:, :], ALU.mult, ALU.add))
            for k in range(2):
                link(v.tensor_scalar(above, key_row, key_col[:, k:k + 1], None, ALU.is_gt))
                link(v.reduce_sum(rank[:, k:k + 1], above, AX.X))
                link(v.tensor_scalar(perm[:, k, :], pos_rank, rank[:, k:k + 1], None, ALU.is_equal))
            link(v.tensor_scalar(wrapped[:, :, :], raw[:, :, :], 0.0, float(V), ALU.is_lt, ALU.mult))
            link(v.tensor_tensor(rows[:, :, :], wrapped[:, :, :], raw[:, :, :], ALU.add))
            link(v.tensor_scalar(wrapped[:, :, :], rows[:, :, :], 0.0, float(V - 1), ALU.max, ALU.min))
            at = IDX + MISC - 1
            link(v.tensor_copy(wrapped[:, 0, at:at + 1], lcol_i[:, 0:1]))
            link(v.tensor_copy(wrapped[:, 1, at:at + 1], lcol_i[:, 1:2]))
            v.memset(from_b[:, :, :], 0.0)
            v.memset(score[0][:, :, :], 0.0)
            v.memset(score[1][:, :, :], 0.0).then_inc(s_perm, 1)
            for c in range(2):
                dve.wait_ge(s_sorted, c + 1)
                link(v.tensor_copy(srt[:, c, :], bank_r[c][:, 0:IDX + MISC]))
            len_a = srt[:, 0, IDX + MISC - 1:IDX + MISC]
            len_b = srt[:, 1, MISC - 1:MISC]
            link(v.tensor_tensor(ends[:, 0:1], len_a, len_b, ALU.add))
            v.tensor_copy(ends[:, 1:2], len_b).then_inc(s_ends, 1)
            v.tensor_copy(misc_idx[:, 0, :], srt[:, 0, IDX:IDX + 2 + NSP])
            v.tensor_copy(misc_idx[:, 1, :], srt[:, 1, 0:2 + NSP])
            for s in range(2):
                v.tensor_copy(len_f[:, 0, s:s + 1], len_a[s * D:(s + 1) * D, :])
                v.tensor_copy(len_f[:, 1, s:s + 1], len_b[s * D:(s + 1) * D, :])
            dve.wait_ge(s_sorted, 3)
            link(v.reduce_max(ends_f[:, :], bank_z[0][0:1, 0:B].rearrange("p (k n) -> p k n", k=2), AX.X))
            link(v.tensor_scalar(ends_f[:, 0:1], ends_f[:, 0:1], float(T + UN), None, ALU.max))
            link(v.tensor_scalar(ends_f[:, 1:2], ends_f[:, 1:2], 1.0, None, ALU.max))
            v.tensor_copy(ends_i[:, :], ends_f[:, :]).then_inc(s_bounds, 1)
            n_slots, n_b = bounds(dve)
            off = dve.snap(limited(n_slots * UN - T, UN, T))
            link(v.tensor_copy(from_b[:, bass.ds(off, T), :].rearrange("p k f -> p (k f)"), srt[:, 1, MISC:]))
            link(v.tensor_scalar(keep_a, slot_no[:, :], len_a, None, ALU.is_lt))
            for f in range(2):
                link(v.tensor_tensor(rows[:, f, 0:T], srt[:, 0, 0:IDX].rearrange("p (k f) -> p f k", f=2)[:, f, :],
                                     from_b[:, 0:T, f], ALU.subtract))
                link(v.tensor_tensor(rows[:, f, 0:T], rows[:, f, 0:T], keep_a, ALU.mult))
                link(v.tensor_tensor(slot_idx[:, 0:T, f], rows[:, f, 0:T], from_b[:, 0:T, f], ALU.add))
            v.memset(slot_idx[:, 2 * T:, :], 0)
            v.tensor_copy(slot_idx[:, T:2 * T, :].rearrange("p k f -> p (k f)"),
                          from_b[:, T:, :].rearrange("p k f -> p (k f)")).then_inc(s_table, 1)

            dve.wait_ge(s_weights, 128)
            v.memset(bias_w[:, :, :].rearrange("p g c -> p (g c)").bitcast(F32), 0.0)
            v.memset(ones_b[:, :], 1.0)
            for k in range(2):
                link(v.tensor_tensor(gbs[:, 4 * k:4 * k + 2, :], gb[:, 6 * k:6 * k + 2, :],
                                     gb[:, 6 * k + 3:6 * k + 5, :], ALU.add))
                link(v.tensor_copy(gbs[:, 4 * k + 2:4 * k + 3, :], gb[:, 6 * k + 2:6 * k + 3, :]))
                link(v.tensor_copy(gbs[:, 4 * k + 3:4 * k + 4, :], gb[:, 6 * k + 5:6 * k + 6, :]))
            link(v.tensor_scalar(gbs[:, Z_, :], gbs[:, Z_, :], -1.0, None, ALU.mult))
            link(v.tensor_scalar(gw[:, Z_, :], gw[:, Z_, :], -1.0, None, ALU.mult))
            link(v.tensor_scalar(gw[:, 3 + Z_, :], gw[:, 3 + Z_, :], -1.0, None, ALU.mult))
            link(v.tensor_scalar(minus_r[:, :], gw[:, 9 + R_, :], -1.0, None, ALU.mult))
            link(v.tensor_copy(gb1[:, :, :], gbs[:, :, :]))
            link(v.tensor_scalar(bias_w[0:3, :, :], gb1[:, :, :], ident[0:3, 0:1], None, ALU.mult))
            link(v.tensor_tensor(gbr[:, :, :], gbs[:, :, :], gb1[:, :, :], ALU.subtract))
            link(v.tensor_copy(gb1[:, :, :], gbr[:, :, :]))
            flat_b = bias_w[0:3, :, :].rearrange("p g c -> p (g c)")
            flat_1 = gb1[:, :, :].rearrange("p g c -> p (g c)")
            link(v.scalar_tensor_tensor(flat_b, flat_1, ident[0:3, 1:2], flat_b, ALU.mult, ALU.add))
            link(v.tensor_tensor(gbs[:, :, :], gbr[:, :, :], gb1[:, :, :], ALU.subtract))
            link(v.tensor_copy(gb1[:, :, :], gbs[:, :, :]))
            link(v.scalar_tensor_tensor(flat_b, flat_1, ident[0:3, 2:3], flat_b, ALU.mult, ALU.add))
            v.tensor_tensor(aw1[:, 1, :], aw1[:, 1, :], aw1[:, 2, :], ALU.subtract)
            v.tensor_tensor(aw1[:, 0, :], aw1[:, 0, :], aw1[:, 2, :], ALU.add)
            v.memset(hist_a[:, 0:UN + 1, :], 0.0)
            v.memset(hist_a[:, UN + 1 + T:, :], 0.0)
            v.memset(qh[:, :, :, :], 0.0)
            v.memset(att1[:, :], 0.0)
            v.memset(att2[:, :], 0.0)
            v.memset(feat[2][0:D, :], 0.0)
            v.memset(mv[:, :, :], 0.0)
            v.memset(state[:, 0, :], 0.0)
            first_counts = [s_filed, s_hist, s_stored, s_stored, alone.state_ok]
            for c in range(2):
                first_counts += [s_qh[c], s_a1[c], s_l2[c], s_a2[c]]
            for k, free in enumerate(first_counts):
                v.memset(v_t[:, k:k + 1], 0.0).then_inc(free, 1)
            v.memset(z_t[:, :], 0.0).then_inc(s_setup, 1)
            dve.wait_ge(s_hq, 1)
            for c in range(2):
                v.tensor_scalar(hq[c][:, :], bank_2[:, c * D:(c + 1) * D], ab1[:, :], None,
                                ALU.add).then_inc(s_hqs, 1)

            def sums(s, bank_, u, pair, t1):
                dve.wait_ge(s.r_ok, t1)
                dve.wait_ge(s.n_mm, t1)
                v.tensor_tensor(own(m_t, pair), cols(bank_, pair, 4 * D, u), own(r_t, pair),
                                ALU.mult).then_inc(s.mul_ok, 1)
                dve.wait_ge(s.mul_ok, t1)
                v.tensor_tensor(cols(bank_, pair, 0, u), own(m_t, pair), cols(bank_, pair, 0, u),
                                ALU.add).then_inc(s.pre_ok, 1)

            def kept(s, n, w, before, t1):
                return v.scalar_tensor_tensor(keep_t[:, 0:n], w[:, 0:n], -1.0, before, ALU.add,
                                              ALU.mult).then_inc(s.keep_ok, 1)

            def new_state(s, n, w, after, t1, lead):
                dve.wait_ge(s.n_ok, t1)
                v.tensor_tensor(v_t[:, 0:n], w[:, 0:n], n_t[:, 0:n], ALU.mult).then_inc(s.v_ok, 1)
                dve.wait_ge(s.v_ok, t1 + lead)
                dve.wait_ge(s.keep_ok, t1 + lead)
                v.tensor_tensor(after, v_t[:, 0:n], keep_t[:, 0:n], ALU.subtract).then_inc(s.state_ok, 1)

            def both_step(u, flip, t1):
                sums(both, bank_n[u // 2 % 2], u, True, t1)
                dve.wait_ge(both.z_ok, t1)
                a = blocks(att_bc, flip * (UN * 2) + 2 * u, 2)
                v.tensor_tensor(az_t[:, :], z_t[:, :], a, ALU.mult).then_inc(both.az_ok, 1)
                dve.wait_ge(both.az_ok, t1)
                kept(both, 2 * D, az_t, state[:, u % 2, :], t1)
                new_state(both, 2 * D, az_t, state[:, (u + 1) % 2, :], t1, 1)

            def chain_step(s, c, w, before, after, u, t1, flip, between=None):
                mine = slice(c * D, (c + 1) * D)
                dve.wait_ge(s.r_ok, t1)
                dve.wait_ge(s.n_mm, t1)
                v.tensor_tensor(m_t[:, mine], bank_n[c][:, chain_cols(c, 4 * D, u)], r_t[:, mine],
                                ALU.mult).then_inc(s.mul_ok, 1)
                dve.wait_ge(s.mul_ok, t1)
                to = bank_n[c][:, chain_cols(c, 0, u)]
                v.tensor_tensor(to, m_t[:, mine], to, ALU.add).then_inc(s.pre_ok, 1)
                dve.wait_ge(s.z_ok, t1)
                if c == 0:
                    v.tensor_tensor(az_t[:, mine], z_t[:, mine], blocks(att_bc, flip * (UN * 2) + 2 * u, 1),
                                    ALU.mult).then_inc(s.az_ok, 1)
                    dve.wait_ge(s.az_ok, t1)
                v.scalar_tensor_tensor(keep_t[:, mine], w[:, mine], -1.0, before, ALU.add,
                                       ALU.mult).then_inc(s.keep_ok, 1)
                if between:
                    between()
                dve.wait_ge(s.n_ok, t1)
                v.tensor_tensor(v_t[:, mine], w[:, mine], n_t[:, mine], ALU.mult).then_inc(s.v_ok, 1)
                dve.wait_ge(s.v_ok, t1)
                dve.wait_ge(s.keep_ok, t1)
                v.tensor_tensor(after, v_t[:, mine], keep_t[:, mine], ALU.subtract).then_inc(s.state_ok, 1)

            def att_query(c, base, p):
                twice = query[c][:, :].rearrange("p (o d) -> p o d", o=1).to_broadcast([P, 2, D])
                v.tensor_tensor(qh[:, p % 2, :, :], twice,
                                pair_of_states(c, base, 2 * p).rearrange("p (o d) -> p o d", o=2),
                                ALU.mult).then_inc(s_qh[c], 1)

            def file_scores(c, i):
                dve.wait_ge(s_l3[c], i + 1)
                src = bank_2[:, P:P + 8].rearrange("p (g s) -> p s g", s=2)
                for e in range(2):
                    at = e if c == 0 else 1 - e
                    to = limited(i * UN + at, 0, UN + T + at)
                    last = v.tensor_copy(score[c][:, :, bass.ds(to, 4, step=2)], src[e * D:(e + 1) * D])
                last.then_inc(s_sc[c], 1)

            def att_add_query(c, i, p):
                twice = hq[c][:, :].rearrange("p (o d) -> p o d", o=1).to_broadcast([P, 2, D])
                to = bank_1[:, 0:P].rearrange("p (o d) -> p o d", o=2)
                dve.wait_ge(s_l1[c], i * 4 + (p + 1))
                v.tensor_tensor(to, to, twice, ALU.add).then_inc(s_l1q[c], 1)

            def att_extras(c, base, i, u):
                back, here = base
                if u == 0:
                    file_scores(c, i)
                if u % 2 == 0:
                    att_add_query(c, i, u // 2)
                if u % 2 and u < UN - 1:
                    att_query(c, back, (u + 1) // 2)
                if u == UN - 1 and here is not None:
                    att_query(c, here, 0)

            def phase1(i):
                base = dve.snap(i * UN) if not isinstance(i, int) else i * UN
                for u in range(UN):
                    t1 = base + (u + 1)
                    sums(alone, bank_n[u // 2 % 2], u, False, t1)
                    dve.wait_ge(alone.z_ok, t1)
                    kept(alone, D, z_t, state[:, u % 2, 0:D], t1)
                    after = state[:, (u + 1) % 2, 0:D]
                    new_state(alone, D, z_t, after, t1, 0)
                    dve.wait_ge(alone.state_ok, t1 + 1)
                    v.tensor_copy(blocks(hist_a, base + (UN + 1 + u), 1), after).then_inc(s_hist, 1)
                    if u == UN - 1:
                        dve.wait_ge(s_hist, base + 3)
                    att_extras(0, (base - UN, base), i, u)

            dve.wait_ge(s_qcopy, 4)
            with dve.Fori(0, BODIES - 1) as i:
                phase1(i)
            phase1(BODIES - 1)
            dve.wait_ge(s_hist, T + 1)
            for u in range(UN):
                att_extras(0, (T - UN, None), BODIES, u)
            file_scores(0, BODIES + 1)

            def softmax(c):
                x = score[c][:, :, 2 * UN:]
                for s in range(2):
                    link(v.tensor_scalar(mask[:, s, :], slot_no[0:D, 0:T], len_f[:, c, s:s + 1], None, ALU.is_lt))
                    link(v.scalar_tensor_tensor(x[:, s, :], x[:, s, :], ab3[:, :], mask[:, s, :], ALU.add, ALU.mult))
                link(v.tensor_scalar(prob[:, :, :], mask[:, :, :], 1.0, MASKED, ALU.subtract, ALU.mult))
                link(v.tensor_tensor(x, x, prob[:, :, :], ALU.add))
                link(v.reduce_max(smx[:, :], x, AX.X))
                v.tensor_scalar(smx[:, :], smx[:, :], -1.0, None, ALU.mult).then_inc(s_max[c], 1)
                dve.wait_ge(s_exp[c], 1)
                link(v.reciprocal(ssum[:, :], ssum[:, :]))
                for s in range(2):
                    last = v.scalar_tensor_tensor(prob[:, s, :], prob[:, s, :], ssum[:, s:s + 1], mask[:, s, :],
                                                  ALU.mult, ALU.mult)
                last.then_inc(s_prob[c], 1)
                dve.wait_ge(s_pt[c], 1)
                v.tensor_copy(prob_t[:, 0:3, :], bank_2[:, 0:3 * D].rearrange("p (k d) -> p k d", k=3))
                left = 2 * T - 3 * P
                v.tensor_copy(prob_t[0:left, 3, :], bank_2[0:left, 3 * D:4 * D]).then_inc(s_ptc[c], 1)

            softmax(0)
            v.memset(state[:, 0, 0:D], 0.0).then_inc(aug_a.state_ok, 1)
            v.memset(state[:, 0, D:2 * D], 0.0).then_inc(gru_b.state_ok, 1)
            end = dve.snap(limited(n_slots * UN, T + UN, 2 * T))
            v.tensor_copy(blocks(slot_x, end, UN), blocks(hist_a, 0, UN)).then_inc(s_zero_b, 1)

            with dve.Fori(0, n_b) as i:
                base = dve.snap(i * UN)
                top = dve.snap(limited(n_slots * UN - base, UN, 2 * T))
                flip = dve.snap(i & 1)
                dve.wait_ge(s_bc, i * 32 + 32)
                for u in range(UN):
                    chain_step(aug_a, 0, az_t, state[:, u % 2, 0:D], state[:, (u + 1) % 2, 0:D], u, base + (u + 1), flip)
                    dve.wait_ge(s_stored, base + (u + 1))
                    def attention(u=u):
                        if u == UN - 1:
                            dve.wait_ge(s_stored, base + 4)
                        att_extras(1, (top + UN, top), i, u)

                    chain_step(gru_b, 1, z_t, state[:, u % 2, D:2 * D], state[:, (u + 1) % 2, D:2 * D], u,
                               base + (u + 1), None, attention)
            top = dve.snap(limited(n_slots * UN - n_b * UN, 0, 2 * T))
            for u in range(UN):
                att_extras(1, (top + UN, None), n_b, u)
            file_scores(1, n_b + 1)
            dve.wait_ge(s_stored, n_b * UN + 2)
            dve.wait_ge(aug_a.state_ok, n_b * UN + 1)
            link(v.memset(state[:, 0, D:2 * D], 0.0))
            v.tensor_copy(v_t[:, :], state[:, 0, :]).then_inc(both.v_ok, 1)
            v.memset(keep_t[:, :], 0.0).then_inc(both.keep_ok, 1)
            v.memset(m_t[:, :], 0.0).then_inc(both.state_ok, 1)
            softmax(1)

            n_rest = dve.snap(sp_max(dve, BODIES - n_b, n_b))
            with dve.Fori(0, n_rest) as i:
                begun = dve.snap(i * UN)
                flip = dve.snap(i & 1)
                dve.wait_ge(s_bc_both, i * 64 + 64)
                for u in range(UN):
                    both_step(u, flip, begun + (u + 1))

            dve.wait_ge(s_spt, 1)
            dve.wait_ge(both.state_ok, n_rest * UN + 1)
            for c in range(2):
                for k in range(2):
                    v.tensor_copy(feat[k][:, c * P:(c + 1) * P], bank_1[:, (2 * c + k) * P:(2 * c + k + 1) * P])
                for s in range(2):
                    at = c * P + s * D
                    last = v.tensor_copy(feat[2][0:D, at:at + D], state[s * D:(s + 1) * D, 0, c * D:(c + 1) * D])
            link(last)
            dve.wait_ge(s_feat, 1)
            for k, n in enumerate((P, P, D + ND)):
                link(v.bn_stats(stats[0:n, k, :], feat[k][0:n, :]))
                link(v.bn_aggr(mv[0:n, k, :], stats[0:n, k, :]))
            v.tensor_scalar(mv[:, :, 1], mv[:, :, 1], BN_EPS, None, ALU.add).then_inc(s_var, 1)
            dve.wait_ge(s_std, 1)
            link(v.reciprocal(std[:, :], std[:, :]))
            link(v.tensor_tensor(sc[:, :], std[:, :], par[:, :, 0], ALU.mult))
            for k, n in enumerate((P, P, D + ND)):
                link(v.tensor_scalar(feat[k][0:n, :], feat[k][0:n, :], mv[0:n, k, 0:1], None, ALU.subtract))
                last = v.tensor_scalar(fnorm[k][0:n, :], feat[k][0:n, :], sc[0:n, k:k + 1], par[0:n, k, 1:2],
                                       ALU.mult, ALU.add)
            last.then_inc(s_norm, 1)
            dve.wait_ge(s_y, 1)
            v.tensor_copy(ycol[:, :], bank_z[1][:, 0:2]).then_inc(s_yc, 1)
            dve.wait_ge(s_yo, 1)
            v.tensor_scalar(yrow, bank_2[0:1, 0:B], ob_sb[:, :], None, ALU.add).then_inc(s_yr, 1)


def held(eng, name, value, low, high):
    out = eng.alloc_register(name)
    eng.reg_mov(out, eng.to_reg(value))
    return bass.RuntimeValue.of_register_unchecked(out, min_val=low, max_val=high)


def sp_max(eng, a, b):
    out = eng.alloc_register("larger")
    eng.reg_alu(out, eng.to_reg(a), eng.to_reg(b), ALU.max)
    return bass.RuntimeValue.of_register_unchecked(out, min_val=BODIES // 2, max_val=BODIES)


def sp_min(eng, name, a, b):
    out = eng.alloc_register(name)
    eng.reg_alu(out, eng.to_reg(a), b, ALU.min)
    return bass.RuntimeValue.of_register_unchecked(out, min_val=0, max_val=b)


def _twice(w):
    import numpy as np
    n, m = w.shape
    o = np.zeros((2 * n, 2 * m), w.dtype)
    o[:n, :m] = w
    o[n:, m:] = w
    return o


def kernel(**inputs):
    import numpy as np
    import concourse.bacc as bacc
    from concourse.bass_utils import run_bass_kernel_spmd

    x = {k: np.asarray(v) for k, v in inputs.items()}
    lens = x["r_hist_valid_lens"]
    hist = x["r_hist_item"]
    two = lambda a: np.ascontiguousarray(a.reshape(2, P, -1).transpose(1, 0, 2))
    ints = np.concatenate([hist.reshape(B, -1), x["r_target_item"], x["r_sparse_feature"], lens[:, None],
                           hist[:, ::-1].reshape(B, -1)], axis=1)
    gate_w, gate_b = [], []
    for n in ("gru", "augru"):
        for m in ("ih", "hh"):
            w, b = x[f"L0_rec_{n}_w{m}"], x[f"L0_rec_{n}_b{m}"]
            for g in range(3):
                gate_w.append(_twice(w[g * D:(g + 1) * D].T))
                gate_b.append(np.concatenate([b[g * D:(g + 1) * D]] * 2))
    w1 = x["L0_rec_att_w1"]
    w2 = _twice(x["L0_rec_att_w2"])
    aw2 = np.zeros((P, 4, P), w2.dtype)
    aw3 = np.zeros((P, 8), w2.dtype)
    for g in range(4):
        aw2[:, g, g * 32:(g + 1) * 32] = w2
        for s in range(2):
            aw3[g * 32 + s * ATT2:g * 32 + (s + 1) * ATT2, 2 * g + s] = x["L0_rec_att_w3"][:, 0]
    order = np.r_[0:NSP * E, NSP * E + ND:NSP * E + ND + D, NSP * E:NSP * E + ND]
    pad = lambda a: np.concatenate([a, np.zeros((3 * P - len(a),) + a.shape[1:], a.dtype)])
    three = lambda a: np.ascontiguousarray(pad(a[order]).reshape(3, P, -1).transpose(1, 0, 2))
    arrays = {
        "lens_row": np.broadcast_to(lens[None, :], (P, B)),
        "lens_col": lens.reshape(2, P).T,
        "ints": two(ints),
        "dense": two(x["L0_rec_dense_feature"]),
        "emb": x["L0_rec_emb"],
        "gate_w": np.stack(gate_w, axis=1),
        "gate_b": np.stack([np.stack(gate_b)] * 3),
        "att_w1": np.stack([_twice(w1[k * D:(k + 1) * D]) for k in range(4)], axis=1),
        "att_b1": np.concatenate([x["L0_rec_att_b1"]] * 2)[:, None],
        "att_w2": aw2,
        "att_b2": np.concatenate([x["L0_rec_att_b2"]] * 8)[:, None],
        "att_w3": aw3,
        "att_b3": np.broadcast_to(x["L0_rec_att_b3"][None, :], (D, 1)),
        "bn_par": three(np.stack([x["L0_rec_bn_gamma"], x["L0_rec_bn_beta"]], axis=1)),
        "w1": three(x["L0_rec_dnn_w1"]),
        "b1": x["L0_rec_dnn_b1"].reshape(2, P).T,
        "w2": x["L0_rec_dnn_w2"].reshape(2, P, HID2).transpose(1, 0, 2),
        "b2": x["L0_rec_dnn_b2"][:, None],
        "out_w": x["L0_rec_out_w"],
        "out_b": x["L0_rec_out_b"][None, :],
    }
    arrays = {k: np.ascontiguousarray(a) for k, a in arrays.items()}
    nc = bacc.Bacc("TRN2", target_bir_lowering=False, num_devices=1)
    aps = [nc.dram_tensor(k, a.shape, mybir.dt.from_np(a.dtype), kind="ExternalInput").ap()
           for k, a in arrays.items()]
    out = nc.dram_tensor("out", (1, B), F32, kind="ExternalOutput").ap()
    build_dien(nc, *aps, out)
    got = run_bass_kernel_spmd(nc, [arrays], core_ids=[0])
    return got.results[0]["out"].reshape(B, 1)
```

```python
from contextlib import ExitStack

import concourse.bass as bass
from concourse import mybir

F32 = mybir.dt.float32
BF16 = mybir.dt.bfloat16
I32 = mybir.dt.int32
U32 = mybir.dt.uint32
ALU = mybir.AluOpType
ACT = mybir.ActivationFunctionType
AX = mybir.AxisListType

B, T, E, V = 256, 200, 32, 12500
D = 2 * E
HALF = D
P = 128
NSP = 8
ND = 16
HID1, HID2 = 256, 128
ATT1, ATT2 = 64, 16
BN_EPS = 1e-5
MASKED = 1e9
UN = 8
BODIES = T // UN
SLOTS = 2 * T
MISC = 2 + NSP + 1
IDX = 2 * T
WARM = 1
R_, Z_, N_ = 0, 1, 2
GRU, AUG = 0, 1


def build_dien(nc, lens_row, lens_col, ints, dense, emb, gate_w, gate_b, att_w1, att_b1, att_w2, att_b2,
               att_w3, att_b3, bn_par, w1, b1, w2, b2, out_w, out_b, out):
    ctx = ExitStack()
    with ctx:
        def sb(name, shape, dt=F32):
            return ctx.enter_context(nc.sbuf_tensor(name, shape, dt))

        def bank(name):
            return ctx.enter_context(nc.psum_tensor(name, [P, 512], F32))

        def sem(name):
            return ctx.enter_context(nc.semaphore(name))

        slot_x = sb("slot_x", [P, SLOTS, D])
        hist_a = sb("hist_a", [P, UN + 1 + T + 2, D])
        fetched = sb("fetched", [P, UN, D])
        slot_idx = sb("slot_idx", [P, 2 * T + 2, 2], U32)
        stage_idx = sb("stage_idx", [P, UN, 2], U32)
        misc_idx = sb("misc_idx", [P, 2, 2 + NSP], U32)
        spare = [(UN + 1 + 3) * D]

        def early(shape, dt=F32, rows_=P):
            n = 1
            for k in shape:
                n *= k
            words = n if dt != BF16 else n // 2
            flat = hist_a[:, :, :].rearrange("p k d -> p (k d)")[0:rows_, spare[0]:spare[0] + words]
            spare[0] += words
            assert spare[0] <= (UN + 1 + T) * D
            flat = flat if dt == F32 else flat.bitcast(dt)
            return flat if len(shape) == 1 else flat.rearrange("p (a b) -> p a b", a=shape[0])

        raw = early([2, IDX + MISC + IDX], I32)
        rows = early([2, IDX + MISC + IDX])
        wrapped = early([2, IDX + MISC + IDX])
        srt = early([2, IDX + MISC])
        from_b = early([2 * T, 2])
        keep_a = early([T])
        perm = early([2, B])
        slot_no = sb("slot_no", [P, T])
        lrow_i = early([B], I32)
        lcol_i = sb("lcol_i", [P, 2], I32)
        key_row = early([B])
        key_col = sb("key_col", [P, 2])
        iota_b = early([B])
        iota_p = sb("iota_p", [P, 1])
        pos_rank = early([B])
        above = early([B])
        rank = sb("rank", [P, 2])
        perm_t = sb("perm_t", [P, 2, B])
        ends = sb("ends", [P, 2])
        ends_i = sb("ends_i", [1, 2], I32)
        ends_f = sb("ends_f", [1, 2])
        table_call = sb("table_call", [P, 1])
        past_stage = sb("past_stage", [P, 1])
        ident = sb("ident", [P, P])
        gw = sb("gw", [P, 12, P])
        minus_r = sb("minus_r", [P, 2, P])
        gb_col = sb("gb_col", [P, 12])
        bias_col = sb("bias_col", [P, 8])
        parts = early([3, 8])
        part_b = early([8], BF16)
        bias_t = sb("bias_t", [P, P], BF16)
        pick = sb("pick", [P, 8, P], BF16)
        aw1 = sb("aw1", [P, 4, P])
        ab1 = sb("ab1", [P, 1])
        aw2 = sb("aw2", [P, 4, P])
        ab2 = sb("ab2", [P, 1])
        aw3 = sb("aw3", [P, 8])
        ab3 = sb("ab3", [D, 1])
        target = sb("target", [P, 2, D])
        query = [sb(f"query{c}", [P, D]) for c in range(2)]
        hq = [sb(f"hq{c}", [P, D]) for c in range(2)]
        qh = sb("qh", [P, 2, 2, D])
        att1 = sb("att1", [P, P])
        att2 = sb("att2", [P, P])
        score = [sb(f"score{c}", [D, 2, UN + T]) for c in range(2)]
        len_f = sb("len_f", [D, 2, 2])
        mask = sb("mask", [D, 2, T])
        smx = sb("smx", [D, 2])
        ssum = sb("ssum", [D, 2])
        prob = sb("prob", [D, 2, T])
        prob_t = sb("prob_t", [P, 4, D])
        att_bc = sb("att_bc", [P, 2 * UN, 2 * D])
        r_t = sb("r_t", [P, 2 * D])
        z_t = sb("z_t", [P, 2 * D])
        az_t = sb("az_t", [P, 2 * D])
        m_t = sb("m_t", [P, 2 * D])
        n_t = sb("n_t", [P, 2 * D])
        v_t = sb("v_t", [P, 2 * D])
        keep_t = sb("keep_t", [P, 2 * D])
        state = sb("state", [P, 2, 2 * D])
        sparse = slot_idx[:, :, :].rearrange("p k f -> p (k f)")[:, 0:2 * NSP * E].bitcast(F32)
        sparse = sparse.rearrange("p (c n) -> p c n", c=2)
        dense_sb = sb("dense_sb", [P, 2, ND])
        late = hist_a[:, 0:8 * B // D, :].rearrange("p k d -> p (k d)").rearrange("p (k n) -> p k n", n=B)
        feat = [late[:, 0, :], late[:, 1, :], sb("feat2", [P, B])[:, :]]
        fnorm = [late[:, 2 + k, :] for k in range(3)]
        par = sb("par", [P, 3, 2])
        stats = sb("stats", [P, 3, 6])
        mv = sb("mv", [P, 3, 2])
        std = sb("std", [P, 3])
        sc = sb("sc", [P, 3])
        w1_sb = sb("w1_sb", [P, 3, HID1])
        b1_sb = sb("b1_sb", [P, 2])
        w2_sb = sb("w2_sb", [P, 2, HID2])
        b2_sb = sb("b2_sb", [P, 1])
        ow_sb = sb("ow_sb", [P, 1])
        ob_sb = sb("ob_sb", [1, 1])
        h1 = late[:, 5:7, :]
        h2 = late[:, 7, :]
        ycol = sb("ycol", [P, 2])
        yrow = late[0:1, 0, :]

        bank_r = [bank(f"bank_r{q}") for q in range(2)]
        bank_z = [bank(f"bank_z{q}") for q in range(2)]
        bank_n = [bank(f"bank_n{q}") for q in range(2)]
        turn_bank = [bank_r[1], bank_z[1]]
        bank_1 = bank("bank_1")
        bank_2 = bank("bank_2")

        att_dram = nc.dram_tensor("att_dram", [2, 2, 2 * T + UN, D], F32, kind="Internal").ap()

        s_ints = sem("s_ints")
        s_weights = sem("s_weights")
        s_dnn = sem("s_dnn")
        s_consts = sem("s_consts")
        s_pick = sem("s_pick")
        s_dve = sem("s_dve")
        s_perm = sem("s_perm")
        s_sorted = sem("s_sorted")
        s_ends = sem("s_ends")
        s_bounds = sem("s_bounds")
        s_table = sem("s_table")
        s_stage = sem("s_stage")
        s_pair = [sem(f"s_pair{p}") for p in range(4)]
        s_target = sem("s_target")
        s_sparse = sem("s_sparse")
        s_turned = sem("s_turned")
        s_filed = sem("s_filed")
        s_permt = sem("s_permt")
        s_permc = sem("s_permc")
        s_query = sem("s_query")
        s_qcopy = sem("s_qcopy")
        s_hq = sem("s_hq")
        s_hqs = sem("s_hqs")
        s_parts = sem("s_parts")
        s_bt = sem("s_bt")
        s_setup = sem("s_setup")
        s_ztail = sem("s_ztail")
        s_qh = [sem(f"s_qh{c}") for c in range(2)]
        s_l1 = [sem(f"s_l1_{c}") for c in range(2)]
        s_l1q = [sem(f"s_l1q_{c}") for c in range(2)]
        s_a1 = [sem(f"s_a1_{c}") for c in range(2)]
        s_l2 = [sem(f"s_l2_{c}") for c in range(2)]
        s_a2 = [sem(f"s_a2_{c}") for c in range(2)]
        s_l3 = [sem(f"s_l3_{c}") for c in range(2)]
        s_sc = [sem(f"s_sc{c}") for c in range(2)]
        s_max = [sem(f"s_max{c}") for c in range(2)]
        s_exp = [sem(f"s_exp{c}") for c in range(2)]
        s_prob = [sem(f"s_prob{c}") for c in range(2)]
        s_pt = [sem(f"s_pt{c}") for c in range(2)]
        s_ptc = [sem(f"s_ptc{c}") for c in range(2)]
        s_pd = [sem(f"s_pd{c}") for c in range(2)]
        s_hist = sem("s_hist")
        s_stored = sem("s_stored")
        s_bc = sem("s_bc")
        s_bc_both = sem("s_bc_both")
        s_spt = sem("s_spt")
        s_feat = sem("s_feat")
        s_dt = sem("s_dt")
        s_norm = sem("s_norm")
        s_var = sem("s_var")
        s_std = sem("s_std")
        s_h1 = sem("s_h1")
        s_h1c = sem("s_h1c")
        s_h2 = sem("s_h2")
        s_h2c = sem("s_h2c")
        s_y = sem("s_y")
        s_yc = sem("s_yc")
        s_yo = sem("s_yo")
        s_yr = sem("s_yr")
        s_out = sem("s_out")

        class Steps:

            def __init__(self, name):
                self.state_ok = sem(f"{name}_state_ok")
                self.r_mm = sem(f"{name}_r_mm")
                self.z_mm = sem(f"{name}_z_mm")
                self.n_mm = sem(f"{name}_n_mm")
                self.r_ok = sem(f"{name}_r_ok")
                self.z_ok = sem(f"{name}_z_ok")
                self.pre_ok = sem(f"{name}_pre_ok")
                self.n_ok = sem(f"{name}_n_ok")
                self.mul_ok = sem(f"{name}_mul_ok")
                self.az_ok = sem(f"{name}_az_ok")
                self.keep_ok = sem(f"{name}_keep_ok")
                self.v_ok = sem(f"{name}_v_ok")

        alone = Steps("alone")
        aug_a = Steps("aug_a")
        gru_b = Steps("gru_b")
        both = Steps("both")

        def cols(tile, pair, off=0, u=0):
            if not pair:
                return tile[:, off + u % 2 * D:off + (u % 2 + 1) * D]
            four = tile[:, off:off + 4 * D].rearrange("p (k d) -> p k d", d=D)
            return four[:, 0:4:3, :] if u % 2 == 0 else four[:, 1:3, :]

        def chain_cols(c, off, u):
            at = off + (u % 2 if c == 0 else 1 - u % 2) * D
            return slice(at, at + D)

        def own(tile, pair):
            return tile[:, :].rearrange("p (c d) -> p c d", d=D) if pair else tile[:, 0:D]

        def blocks(tile, first, n):
            flat = tile[:, :, :].rearrange("p k d -> p (k d)")
            return flat[:, bass.ds(limited(first * D, 0, flat.shape[1] - n * D), n * D)]

        def b_slot(top, u):
            return top - 1 - u

        def pair_of_states(c, base, u):
            return blocks(hist_a, base + (UN + 1 + u), 2) if c == 0 else blocks(slot_x, b_slot(base, u + 1), 2)

        def pair_of_inputs(c, base, u):
            return blocks(slot_x, base + u, 2) if c == 0 else blocks(slot_x, b_slot(base, u + 1), 2)

        def pair_behind(c, base, back, u):
            return pair_of_states(c, base, u - 2) if u else pair_of_states(c, back, UN - 2)

        def bounds(eng):
            eng.wait_ge(s_bounds, 1)
            slots = eng.value_load(ends_i[0:1, 0:1], min_val=T + UN, max_val=2 * T)
            steps = eng.value_load(ends_i[0:1, 1:2], min_val=UN, max_val=T - 1)
            n_slots = eng.snap((slots + (UN - 1)) >> 3)
            n_more = eng.snap(steps >> 3)
            return n_slots, n_more

        def limited(value, low, high):
            return value if isinstance(value, int) else value.with_bounds(min_val=low, max_val=high)

        block = ctx.enter_context(nc.Block())

        @block.sync
        def _(sp):
            sp.dma_start(lrow_i, lens_row).then_inc(s_ints, 16)
            sp.dma_start(lcol_i[:, :], lens_col).then_inc(s_ints, 16)
            sp.dma_start(raw[:, :, :], ints).then_inc(s_ints, 16)
            sp.dma_start(gw[:, :, :], gate_w).then_inc(s_weights, 16)
            sp.dma_start(gb_col[:, :], gate_b).then_inc(s_weights, 16)
            sp.dma_start(aw1[:, :, :], att_w1).then_inc(s_weights, 16)
            sp.dma_start(ab1[:, :], att_b1).then_inc(s_weights, 16)
            sp.dma_start(aw2[:, :, :], att_w2).then_inc(s_weights, 16)
            sp.dma_start(ab2[:, :], att_b2).then_inc(s_weights, 16)
            sp.dma_start(aw3[:, :], att_w3).then_inc(s_weights, 16)
            sp.dma_start(ab3[:, :], att_b3).then_inc(s_weights, 16)
            sp.dma_start(dense_sb[:, :, :], dense).then_inc(s_dnn, 16)
            sp.dma_start(par[:, :, :], bn_par).then_inc(s_dnn, 16)
            sp.dma_start(w1_sb[:, :, :], w1).then_inc(s_dnn, 16)
            sp.dma_start(b1_sb[:, :], b1).then_inc(s_dnn, 16)
            sp.dma_start(w2_sb[:, :, :], w2).then_inc(s_dnn, 16)
            sp.dma_start(b2_sb[:, :], b2).then_inc(s_dnn, 16)
            sp.dma_start(ow_sb[:, :], out_w).then_inc(s_dnn, 16)
            sp.dma_start(ob_sb[:, :], out_b).then_inc(s_dnn, 16)
            sp.wait_ge(s_setup, 1)
            tail = T + UN
            for c in range(2):
                for s in range(2):
                    sp.dma_start(att_dram[c, s, T:, :].rearrange("(a b) d -> a (b d)", a=tail // UN),
                                 hist_a[0:tail // UN, 0:UN, :].rearrange("p k d -> p (k d)")).then_inc(s_ztail, 16)
            sp.wait_ge(s_ztail, 64)

            def save_att(c):
                flat = att_dram[c, :, 0:T, :]
                sp.wait_ge(s_ptc[c], 1)
                n = 0
                for k in range(4):
                    row, left = k * P, min(P, 2 * T - k * P)
                    while left:
                        s, t0 = row // T, row % T
                        m = min(left, T - t0)
                        at = row - k * P
                        sp.dma_start(flat[s, t0:t0 + m, :], prob_t[at:at + m, k, :]).then_inc(s_pd[c], 16)
                        row, left, n = row + m, left - m, n + 1
                sp.wait_ge(s_pd[c], 16 * n)

            def load_att(c, first, at, landed):
                for s in range(2):
                    src = att_dram[c, s, bass.ds(first, UN), :].rearrange("(a t) d -> a t d", a=1)
                    sp.dma_start(att_bc[s * D:(s + 1) * D, bass.ds(at, UN), c * D:(c + 1) * D],
                                 src.to_broadcast([D, UN, D])).then_inc(landed, 16)

            n_slots, n_more = bounds(sp)
            n_b = sp.snap(n_more + 1)
            n_rest = sp.snap(larger(sp, BODIES - n_b, n_b))
            save_att(0)
            load_att(0, 0, 0, s_bc)
            with sp.Fori(0, n_b) as i:
                first = held(sp, "first", (i + 1) * UN, UN, T + UN)
                at = held(sp, "at", ((i + 1) & 1) * UN, 0, UN)
                sp.wait_ge(aug_a.az_ok, i * UN + 1)
                sp.wait_ge(s_bc, i * 32 + 32)
                load_att(0, first, at, s_bc)
            save_att(1)
            at = held(sp, "first_at", (n_b & 1) * UN, 0, UN)
            load_att(1, 0, at, s_bc_both)
            with sp.Fori(0, n_rest) as i:
                first_a = held(sp, "next_a", (n_b + i + 1) * UN, UN, 2 * T)
                first_b = held(sp, "next_b", (i + 1) * UN, UN, T)
                at = held(sp, "next_at", ((n_b + i + 1) & 1) * UN, 0, UN)
                sp.wait_ge(both.az_ok, i * UN + 1)
                sp.wait_ge(s_bc, n_b * 32 + 32)
                sp.wait_ge(s_bc_both, i * 64 + 32)
                load_att(0, first_a, at, s_bc_both)
                load_att(1, first_b, at, s_bc_both)
            sp.wait_ge(s_bc_both, n_rest * 64 + 32)
            sp.wait_ge(s_yr, 1)
            sp.dma_start(out, yrow).then_inc(s_out, 16)
            sp.wait_ge(s_out, 16)

        @block.gpsimd
        def _(pool):
            nc.gpsimd.memset(ident[:, :], 0.0).then_inc(s_consts, 1)
            pool.wait_ge(s_consts, 1)
            nc.gpsimd.affine_select(out=ident[:, :], in_=ident[:, :], compare_op=ALU.not_equal, fill=1.0, base=0,
                                    pattern=[[-1, P]], channel_multiplier=1).then_inc(s_consts, 1)
            nc.gpsimd.iota(iota_b, pattern=[[1, B]], base=0, channel_multiplier=0,
                           allow_small_or_imprecise_dtypes=True).then_inc(s_consts, 1)
            nc.gpsimd.iota(iota_p[:, :], pattern=[[1, 1]], base=0, channel_multiplier=1,
                           allow_small_or_imprecise_dtypes=True).then_inc(s_consts, 1)
            nc.gpsimd.iota(pos_rank[:, 0:P], pattern=[[1, P]], base=0, channel_multiplier=0,
                           allow_small_or_imprecise_dtypes=True).then_inc(s_consts, 1)
            nc.gpsimd.iota(pos_rank[:, P:B], pattern=[[-1, P]], base=B - 1, channel_multiplier=0,
                           allow_small_or_imprecise_dtypes=True).then_inc(s_consts, 1)
            nc.gpsimd.iota(slot_no[:, :], pattern=[[1, T]], base=0, channel_multiplier=0,
                           allow_small_or_imprecise_dtypes=True).then_inc(s_consts, 1)

            nc.gpsimd.memset(pick[:, :, :], 0.0).then_inc(s_pick, 1)
            for k in range(3):
                pool.wait_ge(s_pick, 1 + k)
                nc.gpsimd.affine_select(out=pick[:, :, :], in_=pick[:, :, :], compare_op=ALU.not_equal, fill=1.0,
                                        base=-8 * k, pattern=[[-1, 8], [0, P]],
                                        channel_multiplier=1).then_inc(s_pick, 1)

            def gather(dst, idx):
                return nc.gpsimd.indirect_dma_start(
                    out=dst, out_offset=None, in_=emb[:, :],
                    in_offset=bass.IndirectOffsetOnAxis(ap=idx, axis=0))

            flat_idx = slot_idx[:, :, :].rearrange("p k f -> p (k f)")

            staged = stage_idx[:, :, :].rearrange("p k f -> p (k f)")

            def stage(i, p):
                nc.gpsimd.tensor_copy(staged[:, 4 * p:4 * p + 4],
                                      flat_idx[:, bass.ds(i * (2 * UN) + 4 * p, 4)]).then_inc(s_stage, 1)

            def fetch_pair(i, p, first):
                nxt, j = (p + 1) % 4, i + (p + 1) // 4
                if not first:
                    pool.wait_ge(s_turned, i * 4 + (p - 3))
                if not first or p == 3:
                    pool.wait_ge(s_pair[nxt], j * 64)
                pool.wait_ge(s_stage, i * 4 + (p + 1))
                stage(j, nxt)
                for slot in (2 * p, 2 * p + 1):
                    for f in range(2):
                        gather(fetched[:, slot, f * E:(f + 1) * E],
                               stage_idx[:, slot, f:f + 1]).then_inc(s_pair[p], 16)

            pool.wait_ge(s_table, 1)
            stage(0, 0)
            for p in range(4):
                fetch_pair(0, p, True)
            for c in range(2):
                for f in range(2):
                    gather(target[:, c, f * E:(f + 1) * E], misc_idx[:, c, f:f + 1]).then_inc(s_target, 16)
            n_slots, n_more = bounds(pool)
            n_b = pool.snap(n_more + 1)
            with pool.Fori(1, n_slots) as i:
                i = pool.snap(limited(i, 1, 2 * BODIES - 1))
                for p in range(4):
                    fetch_pair(i, p, False)
            with pool.Fori(0, n_b) as i:
                base = pool.snap(i * UN)
                top = pool.snap(limited(n_slots * UN - base, UN, 2 * T))
                for u in range(UN):
                    pool.wait_ge(gru_b.state_ok, base + (u + 2))
                    nc.gpsimd.tensor_copy(blocks(slot_x, b_slot(top, u), 1),
                                          state[:, (u + 1) % 2, D:2 * D]).then_inc(s_stored, 1)
            pool.wait_ge(s_stage, n_slots * 4 + 1)
            nc.gpsimd.tensor_tensor(past_stage[:, :], iota_p[:, :], iota_p[:, :], ALU.add)
            for c in range(2):
                for f in range(NSP):
                    gather(sparse[:, c, f * E:(f + 1) * E], misc_idx[:, c, 2 + f:3 + f]).then_inc(s_sparse, 16)

        @block.tensor
        def _(pe):
            mm = nc.tensor.matmul

            pe.wait_ge(s_perm, 1)
            for c in range(2):
                for k in range(2):
                    last = mm(bank_r[c][:, 0:IDX + MISC], perm[:, k, c * P:(c + 1) * P],
                              wrapped[:, k, c * IDX:c * IDX + IDX + MISC], start=k == 0, stop=k == 1)
                last.then_inc(s_sorted, 1)
            pe.wait_ge(s_ends, 1)
            for k in range(2):
                last = mm(bank_z[0][0:1, k * P:(k + 1) * P], ends[:, k:k + 1], ident[:, :], start=True, stop=True)
            last.then_inc(s_sorted, 1)
            for c in range(2):
                for k in range(2):
                    last = nc.tensor.transpose(bank_n[c][:, k * P:(k + 1) * P], perm[:, k, c * P:(c + 1) * P],
                                               ident[:, :])
            last.then_inc(s_permt, 1)
            pe.wait_ge(s_dnn, 128)
            for k in range(2):
                last = mm(bank_2[0:ND, 256:512], dense_sb[:, k, :], perm[:, k, :], start=k == 0, stop=k == 1)
            last.then_inc(s_dt, 1)

            def turn(m, k, q):
                pe.wait_ge(s_pair[2 * k + q], m * 64 + 64)
                if q == 0 and not (isinstance(m, int) and m == 0):
                    pe.wait_ge(s_filed, m * 8 + (4 * k - 3))
                pair = fetched[:, 4 * k + 2 * q:4 * k + 2 * q + 2, :].rearrange("p k d -> p (k d)")
                done = nc.tensor.transpose(turn_bank[k][:, P * q:P * (q + 1)], pair, ident[:, :])
                done.then_inc(s_turned, 1)

            def add_bias(dst, at, first, n):
                mm(dst, bias_t[0:24, :], pick[0:24, first:first + n, :], start=at == 0, stop=True,
                   skip_group_check=True)

            def seed(to, at, bias, w, x):
                add_bias(to[:, at:at + P], at, bias, 1)
                mm(to[:, at:at + P], gw[:, w, :], x, start=False, stop=True, skip_group_check=True)

            def seed_rz(q, kind, at, x):
                seed(bank_r[q], at, 4 * kind + R_, 6 * kind + R_, x)
                seed(bank_z[q], at, 4 * kind + Z_, 6 * kind + Z_, x)

            def seed_n(q, kind, at, x):
                two = bank_n[q][:, :].rearrange("p (o n) -> p o n", o=2)[:, :, at:at + P]
                add_bias(two, at, 4 * kind + 2, 2)
                mm(bank_n[q][:, at:at + P], gw[:, 6 * kind + N_, :], x, start=False, stop=True,
                   skip_group_check=True)

            def seed_all(q, kind, at, x):
                seed_rz(q, kind, at, x)
                seed_n(q, kind, at, x)

            def add_state(dst, w, h):
                return mm(dst, w, h, start=False, stop=True, skip_group_check=True)

            def att_layer1(c, states, p, m):
                pe.wait_ge(s_qh[c], m)
                pe.wait_ge(s_a1[c], m)
                to = bank_1[:, 0:P]
                mm(to, aw1[:, 1, :], states, start=True, stop=False)
                mm(to, aw1[:, 3, :], qh[:, p % 2, :, :], start=False, stop=True).then_inc(s_l1[c], 1)

            def att_layer2(c, p, m):
                pe.wait_ge(s_a1[c], m + 1)
                mm(bank_2[:, 0:P], aw2[:, p, :], att1[:, :], start=p == 0, stop=p == 3,
                   skip_group_check=True).then_inc(s_l2[c], 1)

            def att_layer3(c, body1):
                pe.wait_ge(s_a2[c], body1)
                mm(bank_2[:, P:P + 8], att2[:, :], aw3[:, :], start=True, stop=True,
                   skip_group_check=True).then_inc(s_l3[c], 1)

            def keep_clock(bank_, n):
                for _ in range(n):
                    mm(bank_[:, 0:2 * P], ident[:, :], gw[:, 0:2, :], start=True, stop=True, skip_group_check=True)

            pe.wait_ge(s_consts, 7)
            pe.wait_ge(s_parts, 1)
            pe.wait_ge(s_feat, 1)
            nc.tensor.transpose(bank_2[0:24, 0:P], parts.rearrange("p k g -> p (k g)"), ident[:, :]).then_inc(s_bt, 1)
            keep_clock(bank_1, 8)
            pe.wait_ge(s_setup, 1)
            pe.wait_ge(s_permc, 1)
            for k in range(2):
                for q in range(2):
                    turn(0, k, q)
            pe.wait_ge(s_pick, 4)
            pe.wait_ge(s_filed, 5)
            seed_rz(0, GRU, 0, pair_of_inputs(0, 0, 0))
            seed_n(0, GRU, 0, pair_of_inputs(0, 0, 0))
            pe.wait_ge(s_target, 64)
            nc.tensor.transpose(bank_1[:, 0:P], target[:, :, :].rearrange("p c d -> p (c d)"),
                                ident[:, :]).then_inc(s_query, 1)
            pe.wait_ge(s_qcopy, 4)
            for c in range(2):
                last = mm(bank_2[:, c * D:(c + 1) * D], aw1[:, 0, :], query[c][:, :], start=True, stop=True)
            last.then_inc(s_hq, 1)
            pe.wait_ge(s_hqs, 2)
            n_slots, n_more = bounds(pe)
            n_b = pe.snap(n_more + 1)

            def phase1(i, turning):
                base = pe.snap(i * UN) if not isinstance(i, int) else i * UN
                for u in range(UN):
                    q, t1 = u // 2 % 2, base + (u + 1)
                    pe.wait_ge(alone.keep_ok, t1)
                    add_state(cols(bank_r[0], False, 0, u), minus_r[:, GRU, :], keep_t[:, 0:D])
                    pe.wait_ge(alone.v_ok, t1)
                    add_state(cols(bank_r[0], False, 0, u), gw[:, 3 + R_, :], v_t[:, 0:D]).then_inc(alone.r_mm, 1)
                    pe.wait_ge(alone.state_ok, t1)
                    h = state[:, u % 2, 0:D]
                    add_state(cols(bank_n[q], False, 4 * D, u), gw[:, 3 + N_, :], h).then_inc(alone.n_mm, 1)
                    add_state(cols(bank_z[0], False, 0, u), gw[:, 3 + Z_, :], h).then_inc(alone.z_mm, 1)
                    if turning and u % 2:
                        turn(i + 1, u // 4, u // 2 % 2)
                    if u == 2:
                        att_layer3(0, i + 1)
                    m = i * 4 + (u // 2 + 1)
                    if u % 2 == 0:
                        pe.wait_ge(s_a1[0], m)
                        keep_clock(bank_1[:, 2 * P:4 * P], 1)
                        att_layer1(0, pair_behind(0, base, base - UN, u), (u // 2 - 1) % 4, m)
                    else:
                        if u == 3:
                            pe.wait_ge(s_sc[0], i + 1)
                        att_layer2(0, (u // 2 - 1) % 4, m)
                    if u >= UN - 2 and not turning:
                        continue
                    if u % 2 == 0:
                        if u == 2:
                            pe.wait_ge(s_filed, i * 8 + 9)
                        if u == UN - 2:
                            pe.wait_ge(s_filed, i * 8 + 13)
                        seed_n(1 - q, GRU, 0, pair_of_inputs(0, base, u + 2))
                    else:
                        pe.wait_ge(alone.r_ok, t1)
                        pe.wait_ge(alone.z_ok, t1)
                        seed_rz(0, GRU, 0, pair_of_inputs(0, base, u + 1))

            with pe.Fori(0, BODIES - 1) as i:
                phase1(i, True)
            phase1(BODIES - 1, False)
            with pe.Fori(BODIES, n_slots) as m:
                m = pe.snap(limited(m, BODIES, 2 * BODIES - 1))
                for k in range(2):
                    for q in range(2):
                        turn(m, k, q)

            def att_turn(c, bank_):
                pe.wait_ge(s_prob[c], 1)
                flat = prob[:, :, :].rearrange("p s t -> p (s t)")
                for k in range(4):
                    n = min(P, 2 * T - k * P)
                    last = nc.tensor.transpose(bank_[0:n, k * D:(k + 1) * D], flat[:, k * P:k * P + n],
                                               ident[0:D, 0:D])
                last.then_inc(s_pt[c], 1)

            def chain_step(s, c, kind, u, t1):
                pe.wait_ge(s.state_ok, t1)
                h = state[:, u % 2, c * D:(c + 1) * D]
                for to, off, g, done in ((bank_r, 0, R_, s.r_mm), (bank_n, 4 * D, N_, s.n_mm), (bank_z, 0, Z_, s.z_mm)):
                    add_state(to[c][:, chain_cols(c, off, u)], gw[:, 6 * kind + 3 + g, :], h).then_inc(done, 1)

            def chain_seed(s, c, kind, t1, x):
                pe.wait_ge(s.r_ok, t1)
                pe.wait_ge(s.z_ok, t1)
                seed_rz(c, kind, 0, x)
                pe.wait_ge(s.n_ok, t1)
                seed_n(c, kind, 0, x)

            keep_clock(bank_n[0], WARM)
            pe.wait_ge(s_filed, n_slots * 8 + 1)
            first_top = limited(n_slots * UN, T + UN, 2 * T)
            seed_all(1, GRU, 0, pair_of_inputs(1, first_top, 0))
            for u in range(UN):
                chain_step(gru_b, 1, GRU, u, u + 1)
                if u == 0:
                    att_layer1(0, pair_of_states(0, T - UN, UN - 2), 3, BODIES * 4 + 1)
                if u == 1:
                    att_layer2(0, 3, BODIES * 4 + 1)
                if u == 2:
                    att_layer3(0, BODIES + 1)
                if u == 4:
                    att_turn(0, bank_r[0])
                if u == 6:
                    pe.wait_ge(s_ptc[0], 1)
                    seed_all(0, AUG, 0, pair_of_states(0, 0, 0))
                if u < 6:
                    keep_clock(bank_n[0], WARM)
                if u % 2 and u > 1:
                    att_layer1(1, pair_behind(1, first_top, None, u - 1), u // 2 - 1, u // 2)
                if u == 4:
                    pe.wait_ge(s_sc[0], BODIES + 1)
                if u % 2 == 0 and u > 2:
                    att_layer2(1, u // 2 - 2, u // 2 - 1)
                if u % 2 and u < UN - 1:
                    chain_seed(gru_b, 1, GRU, u + 1, pair_of_inputs(1, first_top, u + 1))

            with pe.Fori(0, n_more) as j:
                i = pe.snap(limited(j + 1, 1, BODIES - 1))
                base, ba = pe.snap(j * UN + UN), pe.snap(j * UN)
                top = pe.snap(limited(n_slots * UN - base, UN, 2 * T))
                for u in range(UN):
                    chain_step(aug_a, 0, AUG, u, ba + (u + 1))
                    if u % 2 == 0:
                        chain_seed(gru_b, 1, GRU, base + u, pair_of_inputs(1, top, u))
                    else:
                        if u == 3:
                            att_layer3(1, i)
                        att_layer1(1, pair_behind(1, top, top + UN, u - 1), (u // 2 - 1) % 4, i * 4 + u // 2)
                    chain_step(gru_b, 1, GRU, u, base + (u + 1))
                    if u % 2 == 0:
                        if u == 4:
                            pe.wait_ge(s_sc[1], i)
                        att_layer2(1, (u // 2 - 2) % 4, j * 4 + (u // 2 + 3))
                    else:
                        chain_seed(aug_a, 0, AUG, ba + (u + 1), pair_of_states(0, ba, u + 1))

            ba = pe.snap(limited(n_more * UN, UN, T - UN))
            done = pe.snap(limited(n_b * UN, UN, T))
            last_top = pe.snap(limited(n_slots * UN - ba, UN, 2 * T))
            first = pe.snap(smaller(pe, "first_pair", done, T - UN))
            for u in range(UN):
                chain_step(aug_a, 0, AUG, u, ba + (u + 1))
                if u == 0:
                    att_layer2(1, 2, n_more * 4 + 3)
                if u == 1:
                    att_layer1(1, pair_of_states(1, last_top, UN - 2), 3, n_b * 4)
                if u == 2:
                    att_layer2(1, 3, n_b * 4)
                if u == 3:
                    att_layer3(1, n_b)
                if u == 0:
                    pe.wait_ge(gru_b.state_ok, n_b * UN + 1)
                if u == 6:
                    pe.wait_ge(s_sc[1], n_b)
                if u not in (4, 5):
                    keep_clock(bank_n[1] if u < 4 else bank_2, WARM)
                if u == 4:
                    seed_all(1, AUG, 0, pair_of_states(0, first, 0))
                if u == 5:
                    seed_all(1, AUG, P, pair_of_inputs(1, first_top, 0))
                if u == 5:
                    att_turn(1, bank_1)
                if u % 2 and u < UN - 1:
                    chain_seed(aug_a, 0, AUG, ba + (u + 1), pair_of_states(0, ba, u + 1))

            pe.wait_ge(s_sparse, 16 * 2 * NSP)
            pe.wait_ge(s_ptc[1], 1)
            for c in range(2):
                for k in range(2):
                    last = nc.tensor.transpose(bank_1[:, (2 * c + k) * P:(2 * c + k + 1) * P],
                                               sparse[:, c, k * P:(k + 1) * P], ident[:, :])
            last.then_inc(s_spt, 1)

            n_rest = pe.snap(larger(pe, BODIES - n_b, n_b))
            with pe.Fori(0, n_rest) as i:
                base = pe.snap(smaller(pe, "pair", (n_b + i) * UN, T - UN))
                begun = pe.snap(i * UN)
                top = pe.snap(limited(n_slots * UN - begun, UN, 2 * T))
                for u in range(UN):
                    q, t1 = 1 - u // 2 % 2, begun + (u + 1)
                    pe.wait_ge(both.keep_ok, t1)
                    add_state(cols(bank_r[q], True, 0, u), minus_r[:, AUG, :], keep_t[:, :])
                    pe.wait_ge(both.v_ok, t1)
                    add_state(cols(bank_r[q], True, 0, u), gw[:, 9 + R_, :], v_t[:, :]).then_inc(both.r_mm, 1)
                    pe.wait_ge(both.state_ok, t1)
                    h = state[:, u % 2, :]
                    add_state(cols(bank_n[q], True, 4 * D, u), gw[:, 9 + N_, :], h).then_inc(both.n_mm, 1)
                    add_state(cols(bank_z[q], True, 0, u), gw[:, 9 + Z_, :], h).then_inc(both.z_mm, 1)
                    if u % 2 == 0:
                        seed_all(1 - q, AUG, 0, pair_of_states(0, base, u + 2))
                    else:
                        seed_all(1 - q, AUG, P, pair_of_inputs(1, top, u + 1))

            for k, rows_ in enumerate((P, P, D + ND)):
                pe.wait_ge(s_norm, k + 1)
                for m in range(2):
                    last = mm(bank_r[m][:, 0:B], w1_sb[0:rows_, k, m * P:(m + 1) * P], fnorm[k][0:rows_, :],
                              start=k == 0, stop=k == 2)
                    if k == 2:
                        last.then_inc(s_h1, 1)
            for m in range(2):
                pe.wait_ge(s_h1c, m + 1)
                last = mm(bank_z[0][:, 0:B], w2_sb[:, m, :], h1[:, m, :], start=m == 0, stop=m == 1)
            last.then_inc(s_h2, 1)
            pe.wait_ge(s_h2c, 1)
            for c in range(2):
                last = mm(bank_z[1][:, c:c + 1], h2[:, c * P:(c + 1) * P], ow_sb[:, :], start=True, stop=True)
            last.then_inc(s_y, 1)
            pe.wait_ge(s_yc, 1)
            for c in range(2):
                last = mm(bank_2[0:1, 0:B], ycol[:, c:c + 1], perm_t[:, c, :], start=c == 0, stop=c == 1)
            last.then_inc(s_yo, 1)

        @block.scalar
        def _(act):
            A = nc.scalar.activation

            def file_piece(m, k, n):
                e, s = n // 2, n % 2
                if n == 0:
                    act.wait_ge(s_turned, m * 4 + (2 * k + 2))
                src = turn_bank[k][e * D:(e + 1) * D, 0:2 * P].rearrange("p (q c) -> p q c", q=2)[:, :, s * D:(s + 1) * D]
                dst = slot_x[s * D:(s + 1) * D, bass.ds(m * UN + (4 * k + e), 2, step=2), :]
                A(dst, src, ACT.Copy).then_inc(s_filed, 1)

            def sig_r(s, bank_, u, pair, t1):
                act.wait_ge(s.r_mm, t1)
                A(own(r_t, pair), cols(bank_, pair, 0, u), ACT.Sigmoid).then_inc(s.r_ok, 1)

            def sig_z(s, bank_, u, pair, t1):
                act.wait_ge(s.z_mm, t1)
                A(own(z_t, pair), cols(bank_, pair, 0, u), ACT.Sigmoid).then_inc(s.z_ok, 1)

            def tanh(s, bank_, u, pair, t1):
                act.wait_ge(s.pre_ok, t1)
                A(own(n_t, pair), cols(bank_, pair, 0, u), ACT.Tanh).then_inc(s.n_ok, 1)

            def att_relu1(c, m):
                act.wait_ge(s_l1q[c], m)
                act.wait_ge(s_l2[c], m)
                A(att1[:, :], bank_1[:, 0:P], ACT.Relu).then_inc(s_a1[c], 1)

            def att_relu2(c, seen):
                act.wait_ge(s_l2[c], seen)
                A(att2[:, :], bank_2[:, 0:P], ACT.Relu, bias=ab2[:, :]).then_inc(s_a2[c], 1)

            def load_gate_functions():
                A(table_call[:, :], iota_p[:, :], ACT.Sigmoid)

            act.wait_ge(s_consts, 7)
            load_gate_functions()
            act.wait_ge(s_permt, 1)
            for c in range(2):
                last = A(perm_t[:, c, :], bank_n[c][:, 0:B], ACT.Copy)
            last.then_inc(s_permc, 1)
            act.wait_ge(s_dt, 1)
            A(feat[2][D:D + ND, :], bank_2[0:ND, 256:512], ACT.Copy).then_inc(s_feat, 1)
            act.wait_ge(s_setup, 1)
            for n in range(4):
                file_piece(0, 0, n)
            act.wait_ge(s_query, 1)
            for c in range(2):
                for s in range(2):
                    A(query[c][s * D:(s + 1) * D, :], bank_1[c * D:(c + 1) * D, s * D:(s + 1) * D],
                      ACT.Copy).then_inc(s_qcopy, 1)
            n_slots, n_more = bounds(act)
            n_b = act.snap(n_more + 1)

            def phase1(i, turning):
                base = act.snap(i * UN) if not isinstance(i, int) else i * UN
                for u in range(UN):
                    q, t1 = u // 2 % 2, base + (u + 1)
                    sig_r(alone, bank_r[0], u, False, t1)
                    if u % 2:
                        att_relu1(0, i * 4 + (u // 2 + 1))
                    sig_z(alone, bank_z[0], u, False, t1)
                    tanh(alone, bank_n[q], u, False, t1)
                    if u == 1:
                        att_relu2(0, i * 4 + 2)
                    if u in (0, 1):
                        file_piece(i, 1, 2 * u)
                        file_piece(i, 1, 2 * u + 1)
                    if turning and u in (4, 5):
                        file_piece(i + 1, 0, 2 * (u - 4))
                        file_piece(i + 1, 0, 2 * (u - 4) + 1)

            with act.Fori(0, BODIES - 1) as i:
                phase1(i, True)
            phase1(BODIES - 1, False)
            with act.Fori(BODIES, n_slots) as m:
                m = act.snap(limited(m, BODIES, 2 * BODIES - 1))
                for k in range(2):
                    for n in range(4):
                        file_piece(m, k, n)

            def exps(c):
                act.wait_ge(s_max[c], 1)
                for s in range(2):
                    last = A(prob[:, s, :], score[c][:, s, UN:], ACT.Exp, bias=smx[:, s:s + 1],
                             accum_out=ssum[:, s:s + 1])
                last.then_inc(s_exp[c], 1)
                load_gate_functions()

            def chain_step(s, c, u, t1, between=None):
                mine, at = slice(c * D, (c + 1) * D), chain_cols(c, 0, u)
                act.wait_ge(s.r_mm, t1)
                A(r_t[:, mine], bank_r[c][:, at], ACT.Sigmoid).then_inc(s.r_ok, 1)
                if between:
                    between()
                act.wait_ge(s.z_mm, t1)
                A(z_t[:, mine], bank_z[c][:, at], ACT.Sigmoid).then_inc(s.z_ok, 1)
                act.wait_ge(s.pre_ok, t1)
                A(n_t[:, mine], bank_n[c][:, at], ACT.Tanh).then_inc(s.n_ok, 1)

            for u in range(UN):
                chain_step(gru_b, 1, u, u + 1, (lambda: att_relu1(0, BODIES * 4 + 1)) if u == 1 else None)
                if u == 1:
                    att_relu2(0, BODIES * 4 + 2)
                if u == 3:
                    exps(0)
                if u % 2 and u > 1:
                    att_relu1(1, u // 2)
            with act.Fori(0, n_more) as j:
                i = act.snap(limited(j + 1, 1, BODIES - 1))
                base, ba = act.snap(j * UN + UN), act.snap(j * UN)
                for u in range(UN):
                    chain_step(aug_a, 0, u, ba + (u + 1))
                    chain_step(gru_b, 1, u, base + (u + 1))
                    if u % 2:
                        att_relu1(1, i * 4 + u // 2)
                    if u == 2:
                        att_relu2(1, i * 4 + 1)
            ba = act.snap(limited(n_more * UN, UN, T - UN))
            for u in range(UN):
                chain_step(aug_a, 0, u, ba + (u + 1), (lambda: att_relu1(1, n_b * 4)) if u == 2 else None)
                if u == 2:
                    att_relu2(1, n_b * 4 + 1)
                if u == 4:
                    exps(1)
            n_rest = act.snap(larger(act, BODIES - n_b, n_b))
            with act.Fori(0, n_rest) as i:
                begun = act.snap(i * UN)
                for u in range(UN):
                    q, t1 = 1 - u // 2 % 2, begun + (u + 1)
                    sig_r(both, bank_r[q], u, True, t1)
                    sig_z(both, bank_z[q], u, True, t1)
                    tanh(both, bank_n[q], u, True, t1)
            A(table_call[:, :], iota_p[:, :], ACT.Sqrt)
            act.wait_ge(s_var, 1)
            A(std[:, :], mv[:, :, 1], ACT.Sqrt).then_inc(s_std, 1)
            for m in range(2):
                act.wait_ge(s_h1, m + 1)
                A(h1[:, m, :], bank_r[m][:, 0:B], ACT.Relu, bias=b1_sb[:, m:m + 1]).then_inc(s_h1c, 1)
            act.wait_ge(s_h2, 1)
            A(h2[:, :], bank_z[0][:, 0:B], ACT.Relu, bias=b2_sb[:, :]).then_inc(s_h2c, 1)

        @block.vector
        def _(dve):
            v = nc.vector
            count = [0]

            def link(ins):
                count[0] += 1
                ins.then_inc(s_dve, 1)
                dve.wait_ge(s_dve, count[0])

            dve.wait_ge(s_ints, 48)
            dve.wait_ge(s_consts, 7)
            link(v.tensor_scalar(lrow_i, lrow_i, 0.0, float(T), ALU.max, ALU.min))
            link(v.tensor_scalar(lcol_i[:, :], lcol_i[:, :], 0.0, float(T), ALU.max, ALU.min))
            link(v.scalar_tensor_tensor(key_row, lrow_i, float(B), iota_b, ALU.mult, ALU.add))
            link(v.tensor_scalar(key_col[:, 0:1], iota_p[:, :], 0.0, None, ALU.add))
            link(v.tensor_scalar(key_col[:, 1:2], iota_p[:, :], float(P), None, ALU.add))
            link(v.scalar_tensor_tensor(key_col[:, :], lcol_i[:, :], float(B), key_col[:, :], ALU.mult, ALU.add))
            for k in range(2):
                link(v.tensor_scalar(above, key_row, key_col[:, k:k + 1], None, ALU.is_gt))
                link(v.reduce_sum(rank[:, k:k + 1], above, AX.X))
                link(v.tensor_scalar(perm[:, k, :], pos_rank, rank[:, k:k + 1], None, ALU.is_equal))
            link(v.tensor_scalar(wrapped[:, :, :], raw[:, :, :], 0.0, float(V), ALU.is_lt, ALU.mult))
            link(v.tensor_tensor(rows[:, :, :], wrapped[:, :, :], raw[:, :, :], ALU.add))
            link(v.tensor_scalar(wrapped[:, :, :], rows[:, :, :], 0.0, float(V - 1), ALU.max, ALU.min))
            at = IDX + MISC - 1
            link(v.tensor_copy(wrapped[:, 0, at:at + 1], lcol_i[:, 0:1]))
            link(v.tensor_copy(wrapped[:, 1, at:at + 1], lcol_i[:, 1:2]))
            v.memset(from_b[:, :, :], 0.0)
            v.memset(score[0][:, :, :], 0.0)
            v.memset(score[1][:, :, :], 0.0).then_inc(s_perm, 1)
            for c in range(2):
                dve.wait_ge(s_sorted, c + 1)
                link(v.tensor_copy(srt[:, c, :], bank_r[c][:, 0:IDX + MISC]))
            len_a = srt[:, 0, IDX + MISC - 1:IDX + MISC]
            len_b = srt[:, 1, MISC - 1:MISC]
            link(v.tensor_tensor(ends[:, 0:1], len_a, len_b, ALU.add))
            v.tensor_copy(ends[:, 1:2], len_b).then_inc(s_ends, 1)
            v.tensor_copy(misc_idx[:, 0, :], srt[:, 0, IDX:IDX + 2 + NSP])
            v.tensor_copy(misc_idx[:, 1, :], srt[:, 1, 0:2 + NSP])
            for s in range(2):
                v.tensor_copy(len_f[:, 0, s:s + 1], len_a[s * D:(s + 1) * D, :])
                v.tensor_copy(len_f[:, 1, s:s + 1], len_b[s * D:(s + 1) * D, :])
            dve.wait_ge(s_sorted, 3)
            link(v.reduce_max(ends_f[:, :], bank_z[0][0:1, 0:B].rearrange("p (k n) -> p k n", k=2), AX.X))
            link(v.tensor_scalar(ends_f[:, 0:1], ends_f[:, 0:1], float(T + UN), None, ALU.max))
            link(v.tensor_scalar(ends_f[:, 1:2], ends_f[:, 1:2], -1.0, float(UN), ALU.add, ALU.max))
            v.tensor_copy(ends_i[:, :], ends_f[:, :]).then_inc(s_bounds, 1)
            n_slots, n_more = bounds(dve)
            n_b = dve.snap(n_more + 1)
            off = dve.snap(limited(n_slots * UN - T, UN, T))
            link(v.tensor_copy(from_b[:, bass.ds(off, T), :].rearrange("p k f -> p (k f)"), srt[:, 1, MISC:]))
            link(v.tensor_scalar(keep_a, slot_no[:, :], len_a, None, ALU.is_lt))
            for f in range(2):
                link(v.tensor_tensor(rows[:, f, 0:T], srt[:, 0, 0:IDX].rearrange("p (k f) -> p f k", f=2)[:, f, :],
                                     from_b[:, 0:T, f], ALU.subtract))
                link(v.tensor_tensor(rows[:, f, 0:T], rows[:, f, 0:T], keep_a, ALU.mult))
                link(v.tensor_tensor(slot_idx[:, 0:T, f], rows[:, f, 0:T], from_b[:, 0:T, f], ALU.add))
            v.memset(slot_idx[:, 2 * T:, :], 0)
            v.tensor_copy(slot_idx[:, T:2 * T, :].rearrange("p k f -> p (k f)"),
                          from_b[:, T:, :].rearrange("p k f -> p (k f)")).then_inc(s_table, 1)

            dve.wait_ge(s_weights, 128)
            v.tensor_scalar(gw[:, Z_, :], gw[:, Z_, :], -1.0, None, ALU.mult)
            v.tensor_scalar(gw[:, 3 + Z_, :], gw[:, 3 + Z_, :], -1.0, None, ALU.mult)
            for k in range(2):
                v.tensor_scalar(minus_r[:, k, :], gw[:, 6 * k + 3 + R_, :], -1.0, None, ALU.mult)
                v.tensor_tensor(bias_col[:, 4 * k:4 * k + 2], gb_col[:, 6 * k:6 * k + 2],
                                gb_col[:, 6 * k + 3:6 * k + 5], ALU.add)
                v.tensor_copy(bias_col[:, 4 * k + 2:4 * k + 3], gb_col[:, 6 * k + 2:6 * k + 3])
                last = v.tensor_copy(bias_col[:, 4 * k + 3:4 * k + 4], gb_col[:, 6 * k + 5:6 * k + 6])
            link(last)
            link(v.tensor_scalar(bias_col[:, Z_:Z_ + 1], bias_col[:, Z_:Z_ + 1], -1.0, None, ALU.mult))
            link(v.tensor_copy(part_b, bias_col[:, :]))
            link(v.tensor_copy(parts[:, 0, :], part_b))
            link(v.tensor_tensor(parts[:, 2, :], bias_col[:, :], parts[:, 0, :], ALU.subtract))
            link(v.tensor_copy(part_b, parts[:, 2, :]))
            link(v.tensor_copy(parts[:, 1, :], part_b))
            link(v.tensor_tensor(parts[:, 2, :], parts[:, 2, :], parts[:, 1, :], ALU.subtract))
            link(v.tensor_copy(part_b, parts[:, 2, :]))
            v.tensor_copy(parts[:, 2, :], part_b).then_inc(s_parts, 1)
            dve.wait_ge(s_bt, 1)
            v.tensor_copy(bias_t[0:24, :], bank_2[0:24, 0:P])
            v.tensor_tensor(aw1[:, 1, :], aw1[:, 1, :], aw1[:, 2, :], ALU.subtract)
            v.tensor_tensor(aw1[:, 0, :], aw1[:, 0, :], aw1[:, 2, :], ALU.add)
            v.memset(hist_a[:, 0:UN + 1, :], 0.0)
            v.memset(hist_a[:, UN + 1 + T:, :], 0.0)
            v.memset(qh[:, :, :, :], 0.0)
            v.memset(att1[:, :], 0.0)
            v.memset(att2[:, :], 0.0)
            v.memset(feat[2][0:D, :], 0.0)
            v.memset(mv[:, :, :], 0.0)
            v.memset(state[:, 0, :], 0.0)
            v.memset(keep_t[:, :], 0.0)
            link(v.memset(v_t[:, :], 0.0))
            first_counts = [s_filed, s_hist, s_stored, s_stored, alone.state_ok, alone.v_ok, alone.keep_ok, s_qh[0]]
            for c in range(2):
                first_counts += [s_a1[c], s_l2[c]]
            for k, free in enumerate(first_counts):
                v.memset(v_t[:, k:k + 1], 0.0).then_inc(free, 1)
            v.memset(z_t[:, :], 0.0).then_inc(s_setup, 1)
            dve.wait_ge(s_hq, 1)
            for c in range(2):
                v.tensor_scalar(hq[c][:, :], bank_2[:, c * D:(c + 1) * D], ab1[:, :], None,
                                ALU.add).then_inc(s_hqs, 1)

            def sums(s, bank_, u, pair, t1):
                dve.wait_ge(s.r_ok, t1)
                dve.wait_ge(s.n_mm, t1)
                v.tensor_tensor(own(m_t, pair), cols(bank_, pair, 4 * D, u), own(r_t, pair),
                                ALU.mult).then_inc(s.mul_ok, 1)
                dve.wait_ge(s.mul_ok, t1)
                v.tensor_tensor(cols(bank_, pair, 0, u), own(m_t, pair), cols(bank_, pair, 0, u),
                                ALU.add).then_inc(s.pre_ok, 1)

            def kept(s, n, w, before, t1):
                return v.scalar_tensor_tensor(keep_t[:, 0:n], w[:, 0:n], -1.0, before, ALU.add,
                                              ALU.mult).then_inc(s.keep_ok, 1)

            def new_state(s, n, w, after, t1):
                dve.wait_ge(s.n_ok, t1)
                v.tensor_tensor(v_t[:, 0:n], w[:, 0:n], n_t[:, 0:n], ALU.mult).then_inc(s.v_ok, 1)
                dve.wait_ge(s.v_ok, t1 + 1)
                dve.wait_ge(s.keep_ok, t1 + 1)
                v.tensor_tensor(after, v_t[:, 0:n], keep_t[:, 0:n], ALU.subtract).then_inc(s.state_ok, 1)

            def both_step(u, flip, t1):
                sums(both, bank_n[1 - u // 2 % 2], u, True, t1)
                dve.wait_ge(both.z_ok, t1)
                a = blocks(att_bc, flip * (UN * 2) + 2 * u, 2)
                v.tensor_tensor(az_t[:, :], z_t[:, :], a, ALU.mult).then_inc(both.az_ok, 1)
                dve.wait_ge(both.az_ok, t1)
                kept(both, 2 * D, az_t, state[:, u % 2, :], t1)
                new_state(both, 2 * D, az_t, state[:, (u + 1) % 2, :], t1)

            def chain_step(s, c, u, t1, flip=None, between=None):
                mine, w = slice(c * D, (c + 1) * D), (az_t, z_t)[c]
                before, after = state[:, u % 2, mine], state[:, (u + 1) % 2, mine]
                if c == 1:
                    dve.wait_ge(s_stored, t1)
                dve.wait_ge(s.r_ok, t1)
                dve.wait_ge(s.n_mm, t1)
                v.tensor_tensor(m_t[:, mine], bank_n[c][:, chain_cols(c, 4 * D, u)], r_t[:, mine],
                                ALU.mult).then_inc(s.mul_ok, 1)
                dve.wait_ge(s.mul_ok, t1)
                to = bank_n[c][:, chain_cols(c, 0, u)]
                v.tensor_tensor(to, m_t[:, mine], to, ALU.add).then_inc(s.pre_ok, 1)
                dve.wait_ge(s.z_ok, t1)
                if c == 0:
                    v.tensor_tensor(az_t[:, mine], z_t[:, mine], blocks(att_bc, flip * (UN * 2) + 2 * u, 1),
                                    ALU.mult).then_inc(s.az_ok, 1)
                    dve.wait_ge(s.az_ok, t1)
                v.scalar_tensor_tensor(keep_t[:, mine], w[:, mine], -1.0, before, ALU.add,
                                       ALU.mult).then_inc(s.keep_ok, 1)
                if between:
                    between()
                dve.wait_ge(s.n_ok, t1)
                v.tensor_tensor(v_t[:, mine], w[:, mine], n_t[:, mine], ALU.mult).then_inc(s.v_ok, 1)
                dve.wait_ge(s.v_ok, t1)
                dve.wait_ge(s.keep_ok, t1)
                v.tensor_tensor(after, v_t[:, mine], keep_t[:, mine], ALU.subtract).then_inc(s.state_ok, 1)

            def att_query(c, states, p):
                twice = query[c][:, :].rearrange("p (o d) -> p o d", o=1).to_broadcast([P, 2, D])
                v.tensor_tensor(qh[:, p % 2, :, :], twice, states.rearrange("p (o d) -> p o d", o=2),
                                ALU.mult).then_inc(s_qh[c], 1)

            def att_add_query(c, m):
                twice = hq[c][:, :].rearrange("p (o d) -> p o d", o=1).to_broadcast([P, 2, D])
                to = bank_1[:, 0:P].rearrange("p (o d) -> p o d", o=2)
                dve.wait_ge(s_l1[c], m)
                v.tensor_tensor(to, to, twice, ALU.add).then_inc(s_l1q[c], 1)

            def file_scores(c, i, body1):
                dve.wait_ge(s_l3[c], body1)
                src = bank_2[:, P:P + 8].rearrange("p (g s) -> p s g", s=2)
                for e in range(2):
                    at = e if c == 0 else 1 - e
                    to = limited(i * UN + at, 0, T + at)
                    last = v.tensor_copy(score[c][:, :, bass.ds(to, 4, step=2)], src[e * D:(e + 1) * D])
                last.then_inc(s_sc[c], 1)

            def masks(c):
                for s in range(2):
                    last = v.tensor_scalar(mask[:, s, :], slot_no[0:D, 0:T], len_f[:, c, s:s + 1], None, ALU.is_lt)
                link(last)
                link(v.tensor_scalar(prob[:, :, :], mask[:, :, :], 1.0, MASKED, ALU.subtract, ALU.mult))

            def score_max(c):
                x = score[c][:, :, UN:]
                dve.wait_ge(s_sc[c], (BODIES + 1, n_b)[c])
                link(v.scalar_tensor_tensor(x, x, ab3[:, :], prob[:, :, :], ALU.add, ALU.add))
                link(v.reduce_max(smx[:, :], x, AX.X))
                v.tensor_scalar(smx[:, :], smx[:, :], -1.0, None, ALU.mult).then_inc(s_max[c], 1)

            def normalise(c):
                dve.wait_ge(s_exp[c], 1)
                link(v.reciprocal(ssum[:, :], ssum[:, :]))
                for s in range(2):
                    last = v.scalar_tensor_tensor(prob[:, s, :], prob[:, s, :], ssum[:, s:s + 1], mask[:, s, :],
                                                  ALU.mult, ALU.mult)
                last.then_inc(s_prob[c], 1)

            def copy_turned(c, bank_):
                dve.wait_ge(s_pt[c], 1)
                v.tensor_copy(prob_t[:, 0:3, :], bank_[:, 0:3 * D].rearrange("p (k d) -> p k d", k=3))
                left = 2 * T - 3 * P
                v.tensor_copy(prob_t[0:left, 3, :], bank_[0:left, 3 * D:4 * D]).then_inc(s_ptc[c], 1)

            masks(0)

            def phase1(i):
                base = dve.snap(i * UN) if not isinstance(i, int) else i * UN
                for u in range(UN):
                    t1 = base + (u + 1)
                    sums(alone, bank_n[u // 2 % 2], u, False, t1)
                    dve.wait_ge(alone.z_ok, t1)
                    kept(alone, D, z_t, state[:, u % 2, 0:D], t1)
                    after = state[:, (u + 1) % 2, 0:D]
                    new_state(alone, D, z_t, after, t1)
                    dve.wait_ge(alone.state_ok, t1 + 1)
                    v.tensor_copy(blocks(hist_a, base + (UN + 1 + u), 1), after).then_inc(s_hist, 1)
                    if u % 2:
                        dve.wait_ge(s_hist, base + (u + 2))
                        att_query(0, pair_behind(0, base, None, u + 1), u // 2)
                    else:
                        att_add_query(0, i * 4 + (u // 2 + 1))
                    if u == 2:
                        file_scores(0, i, i + 1)

            dve.wait_ge(s_qcopy, 4)
            with dve.Fori(0, BODIES - 1) as i:
                phase1(i)
            phase1(BODIES - 1)
            v.memset(state[:, 0, D:2 * D], 0.0).then_inc(gru_b.state_ok, 1)
            v.memset(state[:, 0, 0:D], 0.0).then_inc(aug_a.state_ok, 1)

            first_top = limited(n_slots * UN, T + UN, 2 * T)
            for u in range(UN):
                def between():
                    if u % 2 == 0:
                        dve.wait_ge(s_stored, u + 2)
                        att_query(1, pair_behind(1, first_top, None, u), u // 2 - 1)
                    else:
                        att_add_query(1, u // 2)

                chain_step(gru_b, 1, u, u + 1, None, between if u > 1 else None)
                if u == 0:
                    att_add_query(0, BODIES * 4 + 1)
                if u == 2:
                    file_scores(0, BODIES, BODIES + 1)
                    score_max(0)
                if u == 3:
                    normalise(0)
                if u == 4:
                    copy_turned(0, bank_r[0])
                if u == 6:
                    masks(1)
            with dve.Fori(0, n_more) as j:
                i = dve.snap(limited(j + 1, 1, BODIES - 1))
                base, ba = dve.snap(j * UN + UN), dve.snap(j * UN)
                top = dve.snap(limited(n_slots * UN - base, UN, 2 * T))
                flip = dve.snap(j & 1)
                dve.wait_ge(s_bc, i * 32)
                for u in range(UN):
                    def between():
                        if u % 2 == 0:
                            dve.wait_ge(s_stored, base + (u + 2))
                            att_query(1, pair_behind(1, top, top + UN, u), (u // 2 - 1) % 4)
                        else:
                            if u == 3:
                                file_scores(1, i, i)
                            att_add_query(1, i * 4 + u // 2)

                    chain_step(aug_a, 0, u, ba + (u + 1), flip)
                    chain_step(gru_b, 1, u, base + (u + 1), None, between)
            ba = dve.snap(limited(n_more * UN, UN, T - UN))
            last_top = dve.snap(limited(n_slots * UN - ba, UN, 2 * T))
            flip = dve.snap(n_more & 1)
            dve.wait_ge(s_bc, n_b * 32)
            for u in range(UN):
                chain_step(aug_a, 0, u, ba + (u + 1), flip)
                if u == 0:
                    dve.wait_ge(s_stored, n_b * UN + 2)
                    att_query(1, pair_of_states(1, last_top, UN - 2), 3)
                if u == 1:
                    att_add_query(1, n_b * 4)
                if u == 3:
                    file_scores(1, n_b, n_b)
                    score_max(1)
                if u == 4:
                    normalise(1)
                if u == 5:
                    copy_turned(1, bank_1)
            dve.wait_ge(aug_a.state_ok, n_b * UN + 1)
            dve.wait_ge(s_bc, n_b * 32 + 32)
            link(v.memset(state[:, 0, D:2 * D], 0.0))
            v.tensor_copy(v_t[:, :], state[:, 0, :]).then_inc(both.v_ok, 1)
            v.memset(keep_t[:, :], 0.0).then_inc(both.keep_ok, 1)
            v.memset(m_t[:, :], 0.0).then_inc(both.state_ok, 1)

            n_rest = dve.snap(larger(dve, BODIES - n_b, n_b))
            with dve.Fori(0, n_rest) as i:
                begun = dve.snap(i * UN)
                flip = dve.snap((n_b + i) & 1)
                dve.wait_ge(s_bc_both, i * 64 + 32)
                for u in range(UN):
                    both_step(u, flip, begun + (u + 1))

            dve.wait_ge(s_spt, 1)
            dve.wait_ge(both.state_ok, n_rest * UN + 1)
            for k in range(2):
                v.tensor_copy(feat[k].rearrange("p (c n) -> p c n", c=2),
                              bank_1[:, :].rearrange("p (c k n) -> p k c n", c=2, k=2)[:, k])
            for c in range(2):
                for s in range(2):
                    at = c * P + s * D
                    last = v.tensor_copy(feat[2][0:D, at:at + D], state[s * D:(s + 1) * D, 0, c * D:(c + 1) * D])
            link(last)
            dve.wait_ge(s_feat, 1)
            for k, n in enumerate((P, P, D + ND)):
                last = v.bn_stats(stats[0:n, k, :], feat[k][0:n, :])
            link(last)
            for k, n in enumerate((P, P, D + ND)):
                last = v.bn_aggr(mv[0:n, k, :], stats[0:n, k, :])
            link(last)
            v.tensor_scalar(mv[:, :, 1], mv[:, :, 1], BN_EPS, None, ALU.add).then_inc(s_var, 1)
            dve.wait_ge(s_std, 1)
            link(v.reciprocal(std[:, :], std[:, :]))
            link(v.tensor_tensor(sc[:, :], std[:, :], par[:, :, 0], ALU.mult))
            for k, n in enumerate((P, P, D + ND)):
                link(v.tensor_scalar(feat[k][0:n, :], feat[k][0:n, :], mv[0:n, k, 0:1], None, ALU.subtract))
                v.tensor_scalar(fnorm[k][0:n, :], feat[k][0:n, :], sc[0:n, k:k + 1], par[0:n, k, 1:2],
                                ALU.mult, ALU.add).then_inc(s_norm, 1)
            dve.wait_ge(s_y, 1)
            v.tensor_copy(ycol[:, :], bank_z[1][:, 0:2]).then_inc(s_yc, 1)
            dve.wait_ge(s_yo, 1)
            v.tensor_scalar(yrow, bank_2[0:1, 0:B], ob_sb[:, :], None, ALU.add).then_inc(s_yr, 1)


def held(eng, name, value, low, high):
    out = eng.alloc_register(name)
    eng.reg_mov(out, eng.to_reg(value))
    return bass.RuntimeValue.of_register_unchecked(out, min_val=low, max_val=high)


def larger(eng, a, b):
    out = eng.alloc_register("larger")
    eng.reg_alu(out, eng.to_reg(a), eng.to_reg(b), ALU.max)
    return bass.RuntimeValue.of_register_unchecked(out, min_val=BODIES // 2, max_val=BODIES)


def smaller(eng, name, a, b):
    out = eng.alloc_register(name)
    eng.reg_alu(out, eng.to_reg(a), b, ALU.min)
    return bass.RuntimeValue.of_register_unchecked(out, min_val=0, max_val=b)


def _twice(w):
    import numpy as np
    n, m = w.shape
    o = np.zeros((2 * n, 2 * m), w.dtype)
    o[:n, :m] = w
    o[n:, m:] = w
    return o


def kernel(**inputs):
    import numpy as np
    import concourse.bacc as bacc
    from concourse.bass_utils import run_bass_kernel_spmd

    x = {k: np.asarray(v) for k, v in inputs.items()}
    lens = x["r_hist_valid_lens"]
    hist = x["r_hist_item"]
    two = lambda a: np.ascontiguousarray(a.reshape(2, P, -1).transpose(1, 0, 2))
    ints = np.concatenate([hist.reshape(B, -1), x["r_target_item"], x["r_sparse_feature"], lens[:, None],
                           hist[:, ::-1].reshape(B, -1)], axis=1)
    gate_w, gate_b = [], []
    for n in ("gru", "augru"):
        for m in ("ih", "hh"):
            w, b = x[f"L0_rec_{n}_w{m}"], x[f"L0_rec_{n}_b{m}"]
            for g in range(3):
                gate_w.append(_twice(w[g * D:(g + 1) * D].T))
                gate_b.append(np.concatenate([b[g * D:(g + 1) * D]] * 2))
    w1 = x["L0_rec_att_w1"]
    w2 = _twice(x["L0_rec_att_w2"])
    aw2 = np.zeros((P, 4, P), w2.dtype)
    aw3 = np.zeros((P, 8), w2.dtype)
    for g in range(4):
        aw2[:, g, g * 32:(g + 1) * 32] = w2
        for s in range(2):
            aw3[g * 32 + s * ATT2:g * 32 + (s + 1) * ATT2, 2 * g + s] = x["L0_rec_att_w3"][:, 0]
    order = np.r_[0:NSP * E, NSP * E + ND:NSP * E + ND + D, NSP * E:NSP * E + ND]
    pad = lambda a: np.concatenate([a, np.zeros((3 * P - len(a),) + a.shape[1:], a.dtype)])
    three = lambda a: np.ascontiguousarray(pad(a[order]).reshape(3, P, -1).transpose(1, 0, 2))
    arrays = {
        "lens_row": np.broadcast_to(lens[None, :], (P, B)),
        "lens_col": lens.reshape(2, P).T,
        "ints": two(ints),
        "dense": two(x["L0_rec_dense_feature"]),
        "emb": x["L0_rec_emb"],
        "gate_w": np.stack(gate_w, axis=1),
        "gate_b": np.stack(gate_b, axis=1),
        "att_w1": np.stack([_twice(w1[k * D:(k + 1) * D]) for k in range(4)], axis=1),
        "att_b1": np.concatenate([x["L0_rec_att_b1"]] * 2)[:, None],
        "att_w2": aw2,
        "att_b2": np.concatenate([x["L0_rec_att_b2"]] * 8)[:, None],
        "att_w3": aw3,
        "att_b3": np.broadcast_to(x["L0_rec_att_b3"][None, :], (D, 1)),
        "bn_par": three(np.stack([x["L0_rec_bn_gamma"], x["L0_rec_bn_beta"]], axis=1)),
        "w1": three(x["L0_rec_dnn_w1"]),
        "b1": x["L0_rec_dnn_b1"].reshape(2, P).T,
        "w2": x["L0_rec_dnn_w2"].reshape(2, P, HID2).transpose(1, 0, 2),
        "b2": x["L0_rec_dnn_b2"][:, None],
        "out_w": x["L0_rec_out_w"],
        "out_b": x["L0_rec_out_b"][None, :],
    }
    arrays = {k: np.ascontiguousarray(a) for k, a in arrays.items()}
    nc = bacc.Bacc("TRN2", target_bir_lowering=False, num_devices=1)
    aps = [nc.dram_tensor(k, a.shape, mybir.dt.from_np(a.dtype), kind="ExternalInput").ap()
           for k, a in arrays.items()]
    out = nc.dram_tensor("out", (1, B), F32, kind="ExternalOutput").ap()
    build_dien(nc, *aps, out)
    got = run_bass_kernel_spmd(nc, [arrays], core_ids=[0])
    return got.results[0]["out"].reshape(B, 1)
```
